# Optimizing a Trainium2 kernel written in Bass

```python
import numpy as np
import jax
import jax.numpy as jnp

def _softmax(x, axis=-1):
    return jax.nn.softmax(x, axis=axis)

def _gelu(x):
    return jax.nn.gelu(x, approximate=True)

def _silu(x):
    return jax.nn.silu(x)

def _sigmoid(x):
    return jax.nn.sigmoid(x)

def _layernorm(x, axis=-1, eps=1e-05):
    m = jnp.mean(x, axis=axis, keepdims=True)
    v = jnp.var(x, axis=axis, keepdims=True)
    return (x - m) / jnp.sqrt(v + eps)

def _scatter_add(tgt, idx, src, axis=0):
    return tgt.at[idx].add(src)

def _segment_sum(src, seg, n):
    return jax.ops.segment_sum(src, seg, n)
kernel_name = 'mk_hybrid_d1_jaxref_r8_ad1b65'

def setup_inputs(seed: int=0):
    np.random.seed(seed)
    _w = jnp.asarray

    def _L0_attn_a_setup():
        import jax, jax.numpy as jnp
        import numpy as np
        B, N, D, H = (2, 256, 128, 8)
        DH = D // H
        key = jax.random.key(seed)
        k0, k1, k2 = jax.random.split(key, 3)
        s = 1.0 / np.sqrt(D).astype(np.float32)
        return {'x': jax.random.normal(k0, (B, N, D), dtype=jnp.float32), 'w_qkv': jax.random.normal(k1, (3 * D, D), dtype=jnp.float32) * s, 'b_qkv': jnp.zeros((3 * D,), dtype=jnp.float32), 'w_o': jax.random.normal(k2, (D, D), dtype=jnp.float32) * s, 'b_o': jnp.zeros((D,), dtype=jnp.float32)}
    _L0_attn_a_in = _L0_attn_a_setup()

    def _L0_attn_b_setup():
        import jax, jax.numpy as jnp
        import numpy as np
        N_HEAD = 16
        key = jax.random.key(seed)
        ks = jax.random.split(key, 9)
        B, T, C = (4, 256, 128)
        s = 0.02
        return {'x': jax.random.normal(ks[0], (B, T, C), dtype=jnp.float32), 'Wq': jax.random.normal(ks[1], (C, C), dtype=jnp.float32) * s, 'bq': jnp.zeros((C,), dtype=jnp.float32), 'Wk': jax.random.normal(ks[2], (C, C), dtype=jnp.float32) * s, 'bk': jnp.zeros((C,), dtype=jnp.float32), 'Wv': jax.random.normal(ks[3], (C, C), dtype=jnp.float32) * s, 'bv': jnp.zeros((C,), dtype=jnp.float32), 'Wo': jax.random.normal(ks[4], (C, C), dtype=jnp.float32) * s, 'bo': jnp.zeros((C,), dtype=jnp.float32)}
    _L0_attn_b_in = _L0_attn_b_setup()

    def _L0_ffn_setup():
        import jax, jax.numpy as jnp
        import numpy as np
        TOP_K = 2
        key = jax.random.key(seed)
        ks = jax.random.split(key, 5)
        B, S, D, H, E = (2, 256, 128, 352, 8)
        x = jax.random.normal(ks[0], (B, S, D), dtype=jnp.float32)
        Wg = jax.random.normal(ks[1], (E, D), dtype=jnp.float32) * 0.02
        W1 = jax.random.normal(ks[2], (E, H, D), dtype=jnp.float32) * 0.02
        W2 = jax.random.normal(ks[3], (E, H, D), dtype=jnp.float32) * 0.02
        W3 = jax.random.normal(ks[4], (E, D, H), dtype=jnp.float32) * 0.02
        return {'x': x, 'Wg': Wg, 'W1': W1, 'W2': W2, 'W3': W3}
    _L0_ffn_in = _L0_ffn_setup()
    _d = {'L0_attn_a_x': _L0_attn_a_in['x'], 'L0_attn_a_w_qkv': _L0_attn_a_in['w_qkv'], 'L0_attn_a_b_qkv': _L0_attn_a_in['b_qkv'], 'L0_attn_a_w_o': _L0_attn_a_in['w_o'], 'L0_attn_a_b_o': _L0_attn_a_in['b_o'], 'L0_attn_b_Wq': _L0_attn_b_in['Wq'], 'L0_attn_b_bq': _L0_attn_b_in['bq'], 'L0_attn_b_Wk': _L0_attn_b_in['Wk'], 'L0_attn_b_bk': _L0_attn_b_in['bk'], 'L0_attn_b_Wv': _L0_attn_b_in['Wv'], 'L0_attn_b_bv': _L0_attn_b_in['bv'], 'L0_attn_b_Wo': _L0_attn_b_in['Wo'], 'L0_attn_b_bo': _L0_attn_b_in['bo'], 'L0_ffn_Wg': _L0_ffn_in['Wg'], 'L0_ffn_W1': _L0_ffn_in['W1'], 'L0_ffn_W2': _L0_ffn_in['W2'], 'L0_ffn_W3': _L0_ffn_in['W3']}
    _x0 = _d['L0_attn_a_x']
    _d['L0_attn_a_x'] = jax.random.normal(jax.random.fold_in(jax.random.key(seed), 1), (4, 1024, 128), dtype=_x0.dtype)
    del _x0
    return _d

def reference(L0_attn_a_x, L0_attn_a_w_qkv, L0_attn_a_b_qkv, L0_attn_a_w_o, L0_attn_a_b_o, L0_attn_b_Wq, L0_attn_b_bq, L0_attn_b_Wk, L0_attn_b_bk, L0_attn_b_Wv, L0_attn_b_bv, L0_attn_b_Wo, L0_attn_b_bo, L0_ffn_Wg, L0_ffn_W1, L0_ffn_W2, L0_ffn_W3):

    def _L0_attn_a_ref(x, w_qkv, b_qkv, w_o, b_o):
        import jax, jax.numpy as jnp
        import numpy as np
        B, N, D, H = (2, 256, 128, 8)
        DH = D // H
        b, n, d = x.shape
        h = H
        dh = d // h
        qkv = x @ w_qkv.T + b_qkv
        qkv = qkv.reshape(b, n, 3, dh, h)
        qkv = jnp.transpose(qkv, (2, 0, 4, 1, 3))
        q, k, v = (qkv[0], qkv[1], qkv[2])
        attn = jnp.einsum('bhik,bhjk->bhij', q, k)
        out = jnp.einsum('bhik,bhkj->bhij', attn, v)
        out = jnp.transpose(out, (0, 2, 1, 3)).reshape(b, n, d)
        return out @ w_o.T + b_o

    def _L0_attn_b_ref(x, Wq, bq, Wk, bk, Wv, bv, Wo, bo):
        import jax, jax.numpy as jnp
        import numpy as np
        N_HEAD = 16
        B, T, C = x.shape
        H = N_HEAD
        d = C // H

        def proj(W, b):
            return (x @ W + b).reshape(B, T, H, d).transpose(0, 2, 1, 3)
        q = proj(Wq, bq)
        k = proj(Wk, bk)
        v = proj(Wv, bv)
        scale = jnp.float32(d) ** (-0.5)
        scores = jnp.einsum('bhtd,bhsd->bhts', q, k) * scale
        attn = jax.nn.softmax(scores, axis=-1)
        out = jnp.einsum('bhts,bhsd->bhtd', attn, v)
        out = out.transpose(0, 2, 1, 3).reshape(B, T, C)
        return out @ Wo + bo

    def _L0_ffn_ref(x, Wg, W1, W2, W3):
        import jax, jax.numpy as jnp
        import numpy as np
        TOP_K = 2
        B, S, D = x.shape
        E = Wg.shape[0]
        xt = x.reshape(B * S, D)
        scores = xt @ Wg.T
        topk_scores, topk_idx = jax.lax.top_k(scores, TOP_K)
        gate = jax.nn.silu(jnp.einsum('td,ehd->teh', xt, W1))
        up = jnp.einsum('td,ehd->teh', xt, W2)
        y = jnp.einsum('teh,edh->ted', gate * up, W3)
        onehot = jax.nn.one_hot(topk_idx, E, dtype=x.dtype)
        w = jnp.einsum('tke,tk->te', onehot, topk_scores)
        out = jnp.einsum('te,ted->td', w, y)
        return out.reshape(B, S, D)
    x = L0_attn_a_x
    x = x + _L0_attn_a_ref(_layernorm(x, axis=-1), L0_attn_a_w_qkv, L0_attn_a_b_qkv, L0_attn_a_w_o, L0_attn_a_b_o)
    x = x + _L0_ffn_ref(_layernorm(x, axis=-1), L0_ffn_Wg, L0_ffn_W1, L0_ffn_W2, L0_ffn_W3)
    x = x + _L0_attn_b_ref(_layernorm(x, axis=-1), L0_attn_b_Wq, L0_attn_b_bq, L0_attn_b_Wk, L0_attn_b_bk, L0_attn_b_Wv, L0_attn_b_bv, L0_attn_b_Wo, L0_attn_b_bo)
    x = x + _L0_ffn_ref(_layernorm(x, axis=-1), L0_ffn_Wg, L0_ffn_W1, L0_ffn_W2, L0_ffn_W3)
    return x

_drawn_inputs = setup_inputs


def setup_inputs(seed=0):
    import zlib

    import numpy as np

    out = dict(_drawn_inputs(seed))
    spreads = {'L0_attn_a_b_qkv': (0.0, 0.1),
     'L0_attn_a_b_o': (0.0, 2.0),
     'L0_attn_b_bq': (0.0, 2.0),
     'L0_attn_b_bk': (0.0, 0.8),
     'L0_attn_b_bv': (0.0, 2.0),
     'L0_attn_b_bo': (0.0, 2.0)}
    factors = {'L0_attn_b_Wq': 64.0,
     'L0_attn_b_Wk': 64.0,
     'L0_attn_b_Wv': 64.0,
     'L0_attn_b_Wo': 64.0,
     'L0_ffn_Wg': 8.0,
     'L0_ffn_W1': 8.0,
     'L0_ffn_W2': 8.0,
     'L0_ffn_W3': 8.0}
    for name, (base, spread) in spreads.items():
        noise = np.random.default_rng([zlib.crc32(name.encode()), seed]).standard_normal(out[name].shape)
        drawn = base * np.exp(spread * noise) if base else spread * noise
        out[name] = jnp.asarray(drawn.astype(out[name].dtype))
    for name, factor in factors.items():
        out[name] = (out[name] * factor).astype(out[name].dtype)
    return out
```

```python
from contextlib import ExitStack

import concourse.bass as bass
from concourse import mybir

F32 = mybir.dt.float32
F32R = mybir.dt.float32r
U32 = mybir.dt.uint32
ALU = mybir.AluOpType
ACT = mybir.ActivationFunctionType
AX_X = mybir.AxisListType.X

P = 128
B, N, D = 4, 1024, 128
TPB = N // P
TILES = B * TPB
E, HID, TOP = 8, 352, 2
NA = 8
NB, DB = 16, 8
EPS = 1e-5
CT = 4
CHUNK = CT * P
CHUNKS = TILES // CT
PAD = CT
BLOCKS = [(0, 128), (128, 128), (256, 96)]
NBLK = len(BLOCKS)
KPC = E * NBLK
GH = 4
GPB = NB // GH
GROUPS = B * GPB
SR = P // GH
GC = GH * DB


class Chip:

    def __init__(self, nc, ctx):
        self.nc, self.ctx = nc, ctx

    def sb(self, name, shape, dt=F32):
        return self.ctx.enter_context(self.nc.sbuf_tensor(name, shape, dt))

    def sem(self, name):
        return self.ctx.enter_context(self.nc.semaphore(name))


def residual_tiles(x, first, count):
    return x[:, bass.ds(first + PAD, count), :]


def attention_a(nc, c, io):
    with ExitStack() as ctx:
        def sb(name, shape, dt=F32):
            return ctx.enter_context(nc.sbuf_tensor(name, shape, dt))

        def psum(name, shape):
            return ctx.enter_context(nc.psum_tensor(name, shape, F32))

        wkv = sb("a_wkv", [P, 2 * D])
        wq = sb("a_wq", [P, D])
        wo = sb("a_wo", [P, D])
        bkv = sb("a_bkv", [P, 2 * D])
        bq = sb("a_bq", [P, 1])
        bo = sb("a_bo", [1, D])
        mask = sb("a_mask", [P, P])
        ones = sb("a_ones", [1, P])
        xn = sb("a_xn", [P, TPB, D])
        xnt = sb("a_xnt", [P, N])
        kv = sb("a_kv", [P, 2, 2 * D])
        vk = sb("a_vk", [P, P])
        vk_wo = sb("a_vk_wo", [P, D])
        fold = sb("a_fold", [P, D])
        bias_row = sb("a_bias_row", [1, D])
        stats = sb("a_stats", [P, TPB, 6])
        moments = sb("a_moments", [P, TPB, 2])
        p_t = psum("a_p_t", [P, N])
        p_kv = [psum(f"a_p_kv{i}", [P, 512]) for i in range(2)]
        p_acc = psum("a_p_acc", [P, 512])
        p_fold = psum("a_p_fold", [P, 512])
        p_y = psum("a_p_y", [P, TPB, D])

        x_in = c.sem("a_x_in")
        w_in = c.sem("a_w_in")
        dve_step = c.sem("a_dve_step")
        sqrt_done = c.sem("a_sqrt_done")
        rstd_ready = c.sem("a_rstd_ready")
        xn_ready = c.sem("a_xn_ready")
        xt_ready = c.sem("a_xt_ready")
        xnt_ready = c.sem("a_xnt_ready")
        kv_ready = c.sem("a_kv_ready")
        kv_copied = c.sem("a_kv_copied")
        vk_ready = c.sem("a_vk_ready")
        vk_masked = c.sem("a_vk_masked")
        vkwo_ready = c.sem("a_vkwo_ready")
        vkwo_copied = c.sem("a_vkwo_copied")
        fold_ready = c.sem("a_fold_ready")
        fold_copied = c.sem("a_fold_copied")
        bias_copied = c.sem("a_bias_copied")
        y_ready = c.sem("a_y_ready")
        y_added = c.sem("a_y_added")
        moved = c.sem("a_moved")

        loads = [(wkv, io["wkv_a"]), (wq, io["wq_a"]), (wo, io["wo_a"]), (mask, io["head_mask"]),
                 (c.ident, io["ident"]), (c.iota, io["iota"]), (bq, io["bq_a"]), (bo, io["bo_a"]),
                 (bkv, io["bkv_a"])]
        block = ctx.enter_context(nc.Block())

        @block.sync
        def _(sp):
            for b in range(B):
                sp.dma_start(c.x[:, PAD + b * TPB:PAD + (b + 1) * TPB, :],
                             io["x"][b].rearrange("(p j) d -> p j d", p=P)).then_inc(x_in, 16)

        @block.scalar
        def _(act):
            for dst, src in loads:
                act.dma_start(dst[:], src).then_inc(w_in, 16)
            act.wait_ge(dve_step, TILES * 2 + 1)
            nc.scalar.activation(c.rstd[:, PAD:PAD + TILES], c.rstd[:, PAD:PAD + TILES], ACT.Sqrt).then_inc(sqrt_done, 1)
            with act.Fori(0, B) as b:
                act.wait_ge(xt_ready, b + 1)
                nc.scalar.activation(xnt[:], p_t[:], ACT.Copy).then_inc(xnt_ready, 1)
                act.wait_ge(vkwo_ready, b + 1)
                nc.scalar.activation(vk_wo[:], p_fold[:, 0:D], ACT.Copy).then_inc(vkwo_copied, 1)
                act.wait_ge(fold_ready, b + 1)
                nc.scalar.activation(fold[:], p_fold[:, D:2 * D], ACT.Copy).then_inc(fold_copied, 1)

        @block.vector
        def _(dve):
            nc.vector.memset(ones[:], 1.0)
            nc.vector.memset(c.mv[:], 0.0)
            nc.vector.memset(c.rstd[:], 1.0)
            nc.vector.memset(c.x[:, 0:PAD, :], 0.0)
            nc.vector.memset(c.x[:, PAD + TILES:, :], 0.0)
            for t in range(TILES):
                if t == 0:
                    dve.wait_ge(x_in, 16 * B)
                if t >= TPB:
                    dve.wait_ge(dve_step, 2 * (t - TPB) + 1)
                nc.vector.bn_stats(stats[:, t % TPB, :], c.x[:, PAD + t, :]).then_inc(dve_step, 1)
                dve.wait_ge(dve_step, 2 * t + 1)
                nc.vector.bn_aggr(c.mv[:, PAD + t, :], stats[:, t % TPB, :]).then_inc(dve_step, 1)
            dve.wait_ge(dve_step, 2 * TILES)
            nc.vector.tensor_scalar(c.rstd[:, PAD:PAD + TILES], c.mv[:, PAD:PAD + TILES, 1], EPS, None, ALU.add).then_inc(dve_step, 1)
            dve.wait_ge(sqrt_done, 1)
            nc.vector.reciprocal(c.rstd[:, PAD:PAD + TILES], c.rstd[:, PAD:PAD + TILES]).then_inc(rstd_ready, 1)
            dve.wait_ge(rstd_ready, 1)
            dve.wait_ge(w_in, 16 * len(loads))
            step = 2 * TILES + 1
            with dve.Fori(0, B) as b:
                with_first = b * (2 * TPB) + step
                for t in range(TPB):
                    last = nc.vector.tensor_scalar(xn[:, t, :], residual_tiles(c.x, b * TPB + t, 1)[:, 0, :],
                                                   c.mv[:, bass.ds(b * TPB + (PAD + t), 1), 0],
                                                   c.rstd[:, bass.ds(b * TPB + (PAD + t), 1)],
                                                   ALU.subtract, ALU.mult)
                last.then_inc(xn_ready, 1)
                for t in range(TPB):
                    dve.wait_ge(kv_ready, b * TPB + (t + 1))
                    if t >= 2:
                        dve.wait_ge(vk_ready, b * TPB + (t - 1))
                    nc.vector.tensor_tensor(kv[:, t % 2, :], p_kv[t % 2][:, 0:2 * D], bkv[:],
                                            ALU.add).then_inc(kv_copied, 1)
                dve.wait_ge(vk_ready, (b + 1) * TPB)
                nc.vector.tensor_tensor(vk[:], p_acc[:, 0:P], mask[:], ALU.mult).then_inc(vk_masked, 1)
                dve.wait_ge(fold_ready, b + 1)
                dve.wait_ge(fold_copied, b + 1)
                nc.vector.tensor_tensor(bias_row[:], p_fold[0:1, 2 * D:3 * D], bo[:], ALU.add).then_inc(bias_copied, 1)
                dve.wait_ge(y_ready, b + 1)
                nc.vector.tensor_tensor(residual_tiles(c.x, b * TPB, TPB), residual_tiles(c.x, b * TPB, TPB),
                                        p_y[:], ALU.add).then_inc(y_added, 1)
                nc.vector.drain()
                for t in range(TPB):
                    nc.vector.bn_stats(stats[:, t, :], residual_tiles(c.x, b * TPB + t, 1)[:, 0, :]).then_inc(dve_step, 1)
                nc.vector.drain()
                for t in range(TPB):
                    nc.vector.bn_aggr(moments[:, t, :], stats[:, t, :]).then_inc(dve_step, 1)
                nc.vector.drain()
                nc.vector.tensor_copy(c.mv[:, bass.ds(b * TPB + PAD, TPB), :], moments[:]).then_inc(moved, 1)
                dve.wait_ge(moved, b + 1)

        @block.tensor
        def _(pe):
            pe.wait_ge(w_in, 16 * len(loads))
            with pe.Fori(0, B) as b:
                pe.wait_ge(xn_ready, b + 1)
                for t in range(TPB):
                    last = nc.tensor.transpose(p_t[:, t * P:(t + 1) * P], xn[:, t, :], c.ident[:])
                last.then_inc(xt_ready, 1)
                pe.wait_ge(xnt_ready, b + 1)
                for t in range(TPB):
                    if t >= 2:
                        pe.wait_ge(kv_copied, b * TPB + (t - 1))
                    nc.tensor.matmul(p_kv[t % 2][:, 0:2 * D], xnt[:, t * P:(t + 1) * P], wkv[:],
                                     start=True, stop=True).then_inc(kv_ready, 1)
                    if t >= 1:
                        pe.wait_ge(kv_copied, b * TPB + t)
                        nc.tensor.matmul(p_acc[:, 0:P], kv[:, (t - 1) % 2, D:2 * D], kv[:, (t - 1) % 2, 0:D],
                                         start=t == 1, stop=False).then_inc(vk_ready, 1)
                pe.wait_ge(kv_copied, (b + 1) * TPB)
                nc.tensor.matmul(p_acc[:, 0:P], kv[:, (TPB - 1) % 2, D:2 * D], kv[:, (TPB - 1) % 2, 0:D],
                                 start=False, stop=True).then_inc(vk_ready, 1)
                pe.wait_ge(vk_masked, b + 1)
                nc.tensor.matmul(p_fold[:, 0:D], vk[:], wo[:], start=True, stop=True).then_inc(vkwo_ready, 1)
                pe.wait_ge(vkwo_copied, b + 1)
                nc.tensor.matmul(p_fold[:, D:2 * D], wq[:], vk_wo[:], start=True, stop=True)
                nc.tensor.matmul(p_fold[0:1, 2 * D:3 * D], bq[:], vk_wo[:], start=True, stop=True).then_inc(fold_ready, 1)
                pe.wait_ge(fold_copied, b + 1)
                pe.wait_ge(bias_copied, b + 1)
                for t in range(TPB):
                    nc.tensor.matmul(p_y[:, t, :], xnt[:, t * P:(t + 1) * P], fold[:], start=True, stop=False)
                    last = nc.tensor.matmul(p_y[:, t, :], ones[:], bias_row[:], start=False, stop=True)
                last.then_inc(y_ready, 1)
                pe.wait_ge(y_added, b + 1)


def feed_forward(nc, c, io, tag, out=None):
    WC = 2 * HID + NBLK * D
    UNROLL = 2
    MID = list(range(KPC))
    with ExitStack() as ctx:
        def sb(name, shape, dt=F32):
            return ctx.enter_context(nc.sbuf_tensor(f"{tag}_{name}", shape, dt))

        def psum(name, shape):
            return ctx.enter_context(nc.psum_tensor(f"{tag}_{name}", shape, F32))

        def sem(name):
            return c.sem(f"{tag}_{name}")

        w_hi = sb("w_hi", [P, E, WC], F32R)
        w_lo = sb("w_lo", [P, E, WC], F32R)
        w_raw = sb("w_raw", [P, 2, WC])
        wg_raw = sb("wg_raw", [P, E])
        wg_hi = sb("wg_hi", [P, E], F32R)
        wg_lo = sb("wg_lo", [P, E], F32R)
        xn = [sb(f"xn{u}", [P, CT, D]) for u in range(2)]
        xt_hi = [sb(f"xt_hi{u}", [P, CHUNK], F32R) for u in range(2)]
        xt_lo = [sb(f"xt_lo{u}", [P, CHUNK], F32R) for u in range(2)]
        mix = [sb(f"mix{u}", [P, CT, E]) for u in range(2)]
        xw = sb("xw", [P, CT, D])
        xw_hi = [sb(f"xw_hi{u}", [P, CHUNK], F32R) for u in range(2)]
        xw_lo = [sb(f"xw_lo{u}", [P, CHUNK], F32R) for u in range(2)]
        gate = [sb(f"gate{u}", [P, CHUNK]) for u in range(2)]
        hid = [sb(f"hid{u}", [P, CHUNK]) for u in range(3)]
        hid_hi = [sb(f"hid_hi{u}", [P, CHUNK], F32R) for u in range(3)]
        hid_lo = [sb(f"hid_lo{u}", [P, CHUNK], F32R) for u in range(3)]
        y_t = sb("y_t", [P, CHUNK])
        score = sb("score", [P, CT, E])
        best = sb("best", [P, CT, 8])
        best_at = sb("best_at", [P, CT, 8], U32)
        best_atf = sb("best_atf", [P, CT, 8])
        onehot = sb("onehot", [P, CT, TOP, E])
        stats = sb("stats", [P, CT, 6])
        moments = sb("moments", [P, CT, 2])

        p_gate = [psum(f"p_gate{u}", [P, CHUNK]) for u in range(2)]
        p_up = [psum(f"p_up{u}", [P, CHUNK]) for u in range(2)]
        p_y = psum("p_y", [P, CHUNK])
        p_xw = psum("p_xw", [P, CHUNK])
        p_t = psum("p_t", [P, CHUNK])
        p_score = psum("p_score", [P, CT, E])

        raw_in = [sem(f"raw_in{u}") for u in range(2)]
        wg_in = sem("wg_in")
        split_hi = sem("split_hi")
        weights_ready = sem("weights_ready")
        sqrt_ready = sem("sqrt_ready")
        var_ready = sem("var_ready")
        xn_ready = sem("xn_ready")
        xt_ready = sem("xt_ready")
        xt_hi_ready = sem("xt_hi_ready")
        xt_lo_ready = sem("xt_lo_ready")
        scores_ready = sem("scores_ready")
        scores_copied = sem("scores_copied")
        mix_ready = sem("mix_ready")
        xw_ready = sem("xw_ready")
        xwt_ready = sem("xwt_ready")
        xw_hi_ready = sem("xw_hi_ready")
        xw_lo_ready = sem("xw_lo_ready")
        gate_ready = sem("gate_ready")
        up_ready = sem("up_ready")
        silu_done = sem("silu_done")
        hid_ready = sem("hid_ready")
        hid_hi_ready = sem("hid_hi_ready")
        hid_lo_ready = sem("hid_lo_ready")
        down_done = sem("down_done")
        y_copied = sem("y_copied")
        yt_ready = sem("yt_ready")
        x_added = sem("x_added")
        dve_step = sem("dve_step")
        moved = sem("moved")
        stored = sem("stored")

        def three(out_ap, lhs, rhs, start=True, stop=True):
            nc.tensor.matmul(out_ap, lhs[0], rhs[0], start=start, stop=False)
            nc.tensor.matmul(out_ap, lhs[1], rhs[0], start=False, stop=False)
            return nc.tensor.matmul(out_ap, lhs[0], rhs[1], start=False, stop=stop)

        block = ctx.enter_context(nc.Block())

        @block.sync
        def _(sp):
            sp.dma_start(wg_raw[:], io["wg"]).then_inc(wg_in, 16)
            for e in range(E):
                if e >= 2:
                    sp.wait_ge(weights_ready, e)
                sp.dma_start(w_raw[:, e % 2, :], io["w_ffn"][e]).then_inc(raw_in[e % 2], 16)
            if out is not None:
                halves = TPB // CT
                rows = out.rearrange("b (p j) d -> p b j d", p=P)
                with sp.Fori(0, B) as b:
                    for h in range(halves):
                        sp.wait_ge(x_added, b * halves + (h + 2))
                        sp.dma_start(rows[:, bass.ds(b, 1), h * CT:(h + 1) * CT, :][:, 0],
                                     residual_tiles(c.x, b * TPB + h * CT, CT)).then_inc(stored, 16)
                sp.wait_ge(stored, 16 * CHUNKS)

        @block.gpsimd
        def _(pool):
            def scale(mixed, u, e, count):
                pool.wait_ge(mix_ready, mixed)
                pool.wait_ge(xwt_ready, count) if count is not None else None
                nc.gpsimd.tensor_tensor(xw[:], xn[u][:], mix[u][:, :, e:e + 1].broadcast_to([P, CT, D]),
                                        ALU.mult).then_inc(xw_ready, 1)

            scale(1, 0, 0, None)
            with pool.Fori(0, CHUNKS // UNROLL) as i:
                for u in range(UNROLL):
                    for e in range(1, E + 1):
                        done = i * (UNROLL * E) + (u * E + e)
                        if e < E:
                            scale(i * UNROLL + (u + 1), u, e, done)
                        else:
                            scale(i * UNROLL + (u + 2), 1 - u, 0, done)

        @block.scalar
        def _(act):
            act.wait_ge(var_ready, 1)
            nc.scalar.activation(c.rstd[:, PAD:PAD + TILES], c.rstd[:, PAD:PAD + TILES], ACT.Sqrt).then_inc(sqrt_ready, 1)
            act.wait_ge(wg_in, 16)
            nc.scalar.activation(wg_hi[:], wg_raw[:], ACT.Copy).then_inc(split_hi, 1)
            for e in range(E):
                act.wait_ge(raw_in[e % 2], 16 * (e // 2 + 1))
                nc.scalar.activation(w_hi[:, e, :], w_raw[:, e % 2, :], ACT.Copy).then_inc(split_hi, 1)

            def hi_of_xt(u, count):
                act.wait_ge(xt_ready, count)
                nc.scalar.activation(xt_hi[u][:], p_t[:], ACT.Copy).then_inc(xt_hi_ready, 1)

            def hi_of_xw(v, count):
                act.wait_ge(xwt_ready, count)
                nc.scalar.activation(xw_hi[v][:], p_xw[:], ACT.Copy).then_inc(xw_hi_ready, 1)

            def hi_of_hid(k, hid_count, down_count, rows):
                act.wait_ge(hid_ready, hid_count)
                act.wait_ge(down_done, down_count)
                nc.scalar.activation(hid_hi[k % 3][0:rows, :], hid[k % 3][0:rows, :], ACT.Copy).then_inc(hid_hi_ready, 1)

            hi_of_xt(0, 1)
            hi_of_xw(0, 1)
            with act.Fori(0, CHUNKS // UNROLL) as i:
                for u in range(UNROLL):
                    for k in range(KPC):
                        kk = i * (UNROLL * KPC) + (u * KPC + k)
                        e, j = k // NBLK, k % NBLK
                        rows = BLOCKS[j][1]
                        if k == 2:
                            act.wait_ge(down_done, i * (UNROLL * KPC) + (u * KPC + 4))
                            nc.scalar.activation(y_t[:], p_y[:], ACT.Copy).then_inc(y_copied, 1)
                        act.wait_ge(gate_ready, kk + 1)
                        nc.scalar.activation(gate[k % 2][0:rows, :], p_gate[k % 2][0:rows, :], ACT.Silu).then_inc(silu_done, 1)
                        hi_of_hid(k - 1, kk + 2, kk + 1, BLOCKS[(k - 1) % NBLK][1])
                        if k == 11:
                            hi_of_xt(1 - u, i * UNROLL + (u + 2))
                        if j == 1:
                            hi_of_xw((e + 1) % 2, i * (UNROLL * E) + (u * E + e + 2))
            hi_of_hid(KPC - 1, CHUNKS * KPC + 2, CHUNKS * KPC + 1, BLOCKS[-1][1])
            act.wait_ge(down_done, CHUNKS * KPC + 4)
            nc.scalar.activation(y_t[:], p_y[:], ACT.Copy).then_inc(y_copied, 1)

        STEPS = 4 * CT + 3

        @block.vector
        def _(dve):
            def step(ins):
                ins.then_inc(dve_step, 1)

            def norm(first, u):
                for t in range(CT):
                    at = bass.ds(first + (PAD + t), 1)
                    last = nc.vector.tensor_scalar(xn[u][:, t, :], c.x[:, at, :][:, 0, :], c.mv[:, at, 0], c.rstd[:, at],
                                                   ALU.subtract, ALU.mult)
                last.then_inc(xn_ready, 1)

            def lo_of_xt(u, count):
                dve.wait_ge(xt_hi_ready, count)
                nc.vector.tensor_tensor(xt_lo[u][:], p_t[:], xt_hi[u][:].bitcast(F32), ALU.subtract).then_inc(xt_lo_ready, 1)

            def lo_of_xw(v, count):
                dve.wait_ge(xw_hi_ready, count)
                nc.vector.tensor_tensor(xw_lo[v][:], p_xw[:], xw_hi[v][:].bitcast(F32), ALU.subtract).then_inc(xw_lo_ready, 1)

            def lo_of_hid(k, count, rows):
                dve.wait_ge(hid_hi_ready, count)
                nc.vector.tensor_tensor(hid_lo[k % 3][0:rows, :], hid[k % 3][0:rows, :],
                                        hid_hi[k % 3][0:rows, :].bitcast(F32), ALU.subtract).then_inc(hid_lo_ready, 1)

            def copy_scores(count):
                dve.wait_ge(scores_ready, count)
                nc.vector.tensor_copy(score[:], p_score[:]).then_inc(scores_copied, 1)

            def find_best():
                for t in range(CT):
                    step(nc.vector.max(best[:, t, :], score[:, t, :]))

            def find_where():
                for t in range(CT):
                    step(nc.vector.max_index(best_at[:, t, :], best[:, t, :], score[:, t, :]))

            def mix_of(u, s):
                dve.wait_ge(dve_step, s + 2 * CT)
                step(nc.vector.tensor_copy(best_atf[:], best_at[:]))
                dve.wait_ge(dve_step, s + (2 * CT + 1))
                step(nc.vector.tensor_tensor(
                    onehot[:], c.iota[:].unsqueeze(1).unsqueeze(1).broadcast_to([P, CT, TOP, E]),
                    best_atf[:, :, 0:TOP].unsqueeze(3).broadcast_to([P, CT, TOP, E]), ALU.is_equal))
                dve.wait_ge(dve_step, s + (2 * CT + 2))
                step(nc.vector.tensor_tensor(
                    onehot[:], onehot[:], best[:, :, 0:TOP].unsqueeze(3).broadcast_to([P, CT, TOP, E]), ALU.mult))
                dve.wait_ge(dve_step, s + (2 * CT + 3))
                nc.vector.tensor_tensor(mix[u][:], onehot[:, :, 0, :], onehot[:, :, 1, :], ALU.add).then_inc(mix_ready, 1)

            PRE = 2 * CT + 3
            OWN = {13: CT, 14: 2 * CT, 17: 3 * CT}
            nc.vector.tensor_scalar(c.rstd[:, PAD:PAD + TILES], c.mv[:, PAD:PAD + TILES, 1], EPS, None, ALU.add).then_inc(var_ready, 1)
            for v in range(1, 3):
                nc.vector.memset(hid[v][:], 0.0).then_inc(hid_ready, 1)
            for v in range(3):
                nc.vector.memset(hid_hi[v][:].bitcast(F32), 0.0)
                last = nc.vector.memset(hid_lo[v][:].bitcast(F32), 0.0)
            last.then_inc(hid_lo_ready, 1)
            nc.vector.memset(y_t[:], 0.0)
            dve.wait_ge(sqrt_ready, 1)
            nc.vector.reciprocal(c.rstd[:, PAD:PAD + TILES], c.rstd[:, PAD:PAD + TILES]).then_inc(var_ready, 1)
            dve.wait_ge(var_ready, 2)
            norm(0, 0)
            dve.wait_ge(split_hi, 1)
            nc.vector.tensor_tensor(wg_lo[:], wg_raw[:], wg_hi[:].bitcast(F32), ALU.subtract).then_inc(weights_ready, 1)
            for e in range(E):
                dve.wait_ge(split_hi, e + 2)
                nc.vector.tensor_tensor(w_lo[:, e, :], w_raw[:, e % 2, :], w_hi[:, e, :].bitcast(F32),
                                        ALU.subtract).then_inc(weights_ready, 1)
            lo_of_xt(0, 1)
            copy_scores(1)
            dve.wait_ge(scores_copied, 1)
            find_best()
            dve.wait_ge(dve_step, CT)
            find_where()
            mix_of(0, 0)
            lo_of_xw(0, 1)
            with dve.Fori(0, CHUNKS // UNROLL) as i:
                for u in range(UNROLL):
                    s = i * (UNROLL * STEPS) + (u * STEPS + PRE)
                    for k in range(KPC):
                        kk = i * (UNROLL * KPC) + (u * KPC + k)
                        e, j = k // NBLK, k % NBLK
                        rows = BLOCKS[j][1]
                        if k == 12:
                            dve.wait_ge(x_added, i * UNROLL + (u + 1))
                        if k in OWN:
                            dve.wait_ge(dve_step, s + OWN[k])
                        if k == 16:
                            dve.wait_ge(scores_copied, i * UNROLL + (u + 2))
                        dve.wait_ge(silu_done, kk + 1)
                        dve.wait_ge(up_ready, kk + 1)
                        nc.vector.tensor_tensor(hid[k % 3][0:rows, :], gate[k % 2][0:rows, :], p_up[k % 2][0:rows, :],
                                                ALU.mult).then_inc(hid_ready, 1)
                        lo_of_hid(k - 1, kk + 1, BLOCKS[(k - 1) % NBLK][1])
                        first = i * (UNROLL * CT) + (u - 1) * CT
                        if k == 6:
                            dve.wait_ge(yt_ready, i * UNROLL + (u + 1))
                            at = bass.ds(i * (UNROLL * CT) + u * CT, CT)
                            nc.vector.tensor_tensor(c.x[:, at, :], c.x[:, at, :], p_t[:].rearrange("p (t d) -> p t d", t=CT),
                                                    ALU.add).then_inc(x_added, 1)
                        if k == 7:
                            norm(i * (UNROLL * CT) + (u + 1) * CT, 1 - u)
                        if k == 11:
                            lo_of_xt(1 - u, i * UNROLL + (u + 2))
                        if k == 12:
                            for t in range(CT):
                                step(nc.vector.bn_stats(stats[:, t, :], c.x[:, bass.ds(i * (UNROLL * CT) + (u * CT + t), 1), :][:, 0, :]))
                        if k == 13:
                            for t in range(CT):
                                step(nc.vector.bn_aggr(moments[:, t, :], stats[:, t, :]))
                        if k == 14:
                            nc.vector.tensor_copy(c.mv[:, bass.ds(i * (UNROLL * CT) + u * CT, CT), :], moments[:]).then_inc(moved, 1)
                        if k == 15:
                            copy_scores(i * UNROLL + (u + 2))
                        if k == 16:
                            find_best()
                        if k == 17:
                            find_where()
                        if k == 18:
                            mix_of(1 - u, s + 2 * CT)
                        if j == 1:
                            lo_of_xw((e + 1) % 2, i * (UNROLL * E) + (u * E + e + 2))
            lo_of_hid(KPC - 1, CHUNKS * KPC + 1, BLOCKS[-1][1])
            dve.wait_ge(yt_ready, CHUNKS + 1)
            tail = c.x[:, TILES:TILES + CT, :]
            nc.vector.tensor_tensor(tail, tail, p_t[:].rearrange("p (t d) -> p t d", t=CT), ALU.add).then_inc(x_added, 1)
            dve.wait_ge(x_added, CHUNKS + 1)
            end = CHUNKS * STEPS + PRE
            for t in range(CT):
                step(nc.vector.bn_stats(stats[:, t, :], c.x[:, TILES + t, :]))
            for t in range(CT):
                dve.wait_ge(dve_step, end + t + 1)
                step(nc.vector.bn_aggr(c.mv[:, TILES + t, :], stats[:, t, :]))

        @block.tensor
        def _(pe):
            def transposes(dst, src, ready):
                for t in range(CT):
                    last = nc.tensor.transpose(dst[:, t * P:(t + 1) * P], src(t), c.ident[:])
                last.then_inc(ready, 1)

            def scores(u, count):
                pe.wait_ge(xt_lo_ready, count)
                for t in range(CT):
                    at = slice(t * P, (t + 1) * P)
                    last = three(p_score[:, t, :], (xt_hi[u][:, at], xt_lo[u][:, at]), (wg_hi[:], wg_lo[:]))
                last.then_inc(scores_ready, 1)

            def down(k, lo_count):
                e, j = k // NBLK, k % NBLK
                rows = BLOCKS[j][1]
                pe.wait_ge(hid_lo_ready, lo_count)
                cols = slice(2 * HID + j * D, 2 * HID + (j + 1) * D)
                three(p_y[:], (w_hi[0:rows, e, cols], w_lo[0:rows, e, cols]),
                      (hid_hi[k % 3][0:rows, :], hid_lo[k % 3][0:rows, :]), k == 0, k == KPC - 1).then_inc(down_done, 1)

            pe.wait_ge(xn_ready, 1)
            transposes(p_t, lambda t: xn[0][:, t, :], xt_ready)
            pe.wait_ge(weights_ready, 1)
            scores(0, 1)
            pe.wait_ge(hid_lo_ready, 1)
            pe.wait_ge(weights_ready, 2)
            for n in range(2):
                three(p_y[:], (w_hi[:, 0, 0:D], w_lo[:, 0, 0:D]), (hid_hi[0][:], hid_lo[0][:]),
                      start=n == 0, stop=False).then_inc(down_done, 1)
            pe.wait_ge(xw_ready, 1)
            transposes(p_xw, lambda t: xw[:, t, :], xwt_ready)
            with pe.Fori(0, CHUNKS // UNROLL) as i:
                for u in range(UNROLL):
                    for k in range(KPC):
                        kk = i * (UNROLL * KPC) + (u * KPC + k)
                        e, j = k // NBLK, k % NBLK
                        first, rows = BLOCKS[j]
                        pe.wait_ge(hid_ready, kk + 1)
                        if j == 0:
                            pe.wait_ge(weights_ready, e + 2)
                        three(p_gate[k % 2][0:rows, :],
                              (w_hi[:, e, first:first + rows], w_lo[:, e, first:first + rows]),
                              (xt_hi[u][:], xt_lo[u][:])).then_inc(gate_ready, 1)
                        if j == 0:
                            pe.wait_ge(xw_lo_ready, i * (UNROLL * E) + (u * E + e + 1))
                        three(p_up[k % 2][0:rows, :],
                              (w_hi[:, e, HID + first:HID + first + rows], w_lo[:, e, HID + first:HID + first + rows]),
                              (xw_hi[e % 2][:], xw_lo[e % 2][:])).then_inc(up_ready, 1)
                        if k == 2:
                            pe.wait_ge(y_copied, i * UNROLL + (u + 1))
                        down((k - 2) % KPC, kk + 1)
                        if k == 4:
                            transposes(p_t, lambda t: y_t[:, t * P:(t + 1) * P], yt_ready)
                        if k == 9:
                            pe.wait_ge(xn_ready, i * UNROLL + (u + 2))
                            pe.wait_ge(x_added, i * UNROLL + (u + 1))
                            transposes(p_t, lambda t: xn[1 - u][:, t, :], xt_ready)
                        if k == 13:
                            pe.wait_ge(scores_copied, i * UNROLL + (u + 1))
                            scores(1 - u, i * UNROLL + (u + 2))
                        if j == 0:
                            pe.wait_ge(xw_ready, i * (UNROLL * E) + (u * E + e + 2))
                            transposes(p_xw, lambda t: xw[:, t, :], xwt_ready)
            down(KPC - 2, CHUNKS * KPC + 1)
            down(KPC - 1, CHUNKS * KPC + 2)
            pe.wait_ge(y_copied, CHUNKS + 1)
            transposes(p_t, lambda t: y_t[:, t * P:(t + 1) * P], yt_ready)


def project_qkv(nc, c, io, tag):
    with ExitStack() as ctx:
        def sb(name, shape, dt=F32):
            return ctx.enter_context(nc.sbuf_tensor(f"{tag}_{name}", shape, dt))

        def psum(name, shape):
            return ctx.enter_context(nc.psum_tensor(f"{tag}_{name}", shape, F32))

        def sem(name):
            return c.sem(f"{tag}_{name}")

        w = sb("w", [P, 3 * D])
        bias = sb("bias", [P, 3 * D])
        xn = [sb(f"xn{u}", [P, TPB, D]) for u in range(2)]
        xnt = [sb(f"xnt{u}", [P, N]) for u in range(2)]
        p_t = psum("p_t", [P, N])
        p_qkv = [psum(f"p_qkv{u}", [P, 512]) for u in range(4)]
        w_in = sem("w_in")
        var_ready = sem("var_ready")
        sqrt_done = sem("sqrt_done")
        xn_ready = sem("xn_ready")
        xt_ready = sem("xt_ready")
        xnt_ready = sem("xnt_ready")
        qkv_ready = sem("qkv_ready")
        qkv_stored = sem("qkv_stored")
        block = ctx.enter_context(nc.Block())

        @block.sync
        def _(sp):
            sp.dma_start(w[:], io["w_b"]).then_inc(w_in, 16)
            sp.dma_start(bias[:], io["b_b"]).then_inc(w_in, 16)

        @block.scalar
        def _(act):
            act.wait_ge(var_ready, 1)
            nc.scalar.activation(c.rstd[:, PAD:PAD + TILES], c.rstd[:, PAD:PAD + TILES], ACT.Sqrt).then_inc(sqrt_done, 1)
            with act.Fori(0, B // 2) as i:
                for u in range(2):
                    act.wait_ge(xt_ready, i * 2 + (u + 1))
                    nc.scalar.activation(xnt[u][:], p_t[:], ACT.Copy).then_inc(xnt_ready, 1)

        @block.vector
        def _(dve):
            nc.vector.tensor_scalar(c.rstd[:, PAD:PAD + TILES], c.mv[:, PAD:PAD + TILES, 1], EPS, None, ALU.add).then_inc(var_ready, 1)
            dve.wait_ge(sqrt_done, 1)
            nc.vector.reciprocal(c.rstd[:, PAD:PAD + TILES], c.rstd[:, PAD:PAD + TILES]).then_inc(var_ready, 1)
            dve.wait_ge(var_ready, 2)
            dve.wait_ge(w_in, 32)
            with dve.Fori(0, B // 2) as i:
                for u in range(2):
                    b = i * 2 + u
                    for t in range(TPB):
                        at = bass.ds(b * TPB + (PAD + t), 1)
                        last = nc.vector.tensor_scalar(xn[u][:, t, :], c.x[:, at, :][:, 0, :], c.mv[:, at, 0], c.rstd[:, at],
                                                       ALU.subtract, ALU.mult)
                    last.then_inc(xn_ready, 1)
                    for t in range(TPB):
                        dve.wait_ge(qkv_ready, b * TPB + (t + 1))
                        nc.vector.tensor_tensor(c.qkv[:, :, bass.ds(b * GPB + 1, GPB), t, :],
                                                p_qkv[t % 4][:, 0:3 * D].rearrange("p (a g d) -> p a g d", a=3, g=GPB),
                                                bias[:].rearrange("p (a g d) -> p a g d", a=3, g=GPB),
                                                ALU.add).then_inc(qkv_stored, 1)

        @block.tensor
        def _(pe):
            pe.wait_ge(w_in, 32)
            with pe.Fori(0, B // 2) as i:
                for u in range(2):
                    b = i * 2 + u
                    pe.wait_ge(xn_ready, b + 1)
                    for t in range(TPB):
                        last = nc.tensor.transpose(p_t[:, t * P:(t + 1) * P], xn[u][:, t, :], c.ident[:])
                    last.then_inc(xt_ready, 1)
                    pe.wait_ge(xnt_ready, b + 1)
                    for t in range(TPB):
                        if t >= 4:
                            pe.wait_ge(qkv_stored, b * TPB + (t - 3))
                        nc.tensor.matmul(p_qkv[t % 4][:, 0:3 * D], xnt[u][:, t * P:(t + 1) * P], w[:],
                                         start=True, stop=True).then_inc(qkv_ready, 1)
                    pe.wait_ge(qkv_stored, b * TPB + TPB)


def softmax_attention(nc, c, io, tag):
    SCALE = float(DB) ** -0.5
    HALF = N // 2
    QUADS = 2 * TPB
    S_TILES = TPB * GH
    LEAD = 4
    TURNS = [("scores_t", 0, 0), ("scores", 0, 0), ("scores", 0, 1), ("scores_t", 1, 0), ("output", 0, 0),
             ("scores_t", 2, 0), ("scores", 1, 0), ("scores", 1, 1), ("scores_t", 3, 0), ("output", 0, 1)]
    PARTS = sum(kind == "output" for kind, _, _ in TURNS)
    O_AT, Q_AT, K_AT, M_AT = 2, 5, 7, QUADS - 1
    with ExitStack() as ctx:
        def sb(name, shape, dt=F32):
            return ctx.enter_context(nc.sbuf_tensor(f"{tag}_{name}", shape, dt))

        def psum(name, shape):
            return ctx.enter_context(nc.psum_tensor(f"{tag}_{name}", shape, F32))

        def sem(name):
            return c.sem(f"{tag}_{name}")

        q_nat = [sb(f"q_nat{u}", [P, TPB, GH, SR]) for u in range(2)]
        k_nat = sb("k_nat", [P, TPB, GH, SR])
        q_t = sb("q_t", [P, N], F32R)
        k_t = [sb(f"k_t{u}", [P, N], F32R) for u in range(2)]
        qm_t = [sb(f"qm_t{u}", [P, N], F32R) for u in range(2)]
        q_pad = [sb(f"q_pad{u}", [P, GH, N], F32R) for u in range(2)]
        k_pad = [sb(f"k_pad{u}", [P, GH, N], F32R) for u in range(2)]
        v_nat = [sb(f"v_nat{u}", [P, TPB, GH, 32]) for u in range(2)]
        row_max = [sb(f"row_max{u}", [P, TPB, GH]) for u in range(2)]
        prob = [sb(f"prob{n}", [P, HALF]) for n in range(2 * GH)]
        o_t = sb("o_t", [P, N])
        o_den = sb("o_den", [P, TPB, GH])
        p_s = [psum(f"p_s{u}", [P, N]) for u in range(2)]
        p_e = [psum(f"p_e{u}", [P, HALF]) for u in range(2)]
        p_o = psum("p_o", [P, N])

        hi_ready = sem("hi_ready")
        stack_ready = sem("stack_ready")
        v_ready = sem("v_ready")
        zeroed = sem("zeroed")
        q_pad_zeroed = sem("q_pad_zeroed")
        qt_ready = sem("qt_ready")
        kt_ready = sem("kt_ready")
        qt_copied = sem("qt_copied")
        kt_copied = sem("kt_copied")
        q_pad_in = sem("q_pad_in")
        k_pad_in = sem("k_pad_in")
        s_ready = sem("s_ready")
        max_done = sem("max_done")
        neg_hi = sem("neg_hi")
        m_ready = sem("m_ready")
        qm_ready = sem("qm_ready")
        qm_copied = sem("qm_copied")
        st_ready = sem("st_ready")
        exp_done = sem("exp_done")
        pv_done = sem("pv_done")
        o_copied = sem("o_copied")
        ot_ready = sem("ot_ready")
        den_done = sem("den_done")
        o_done = sem("o_done")

        def users(g):
            out = []
            for q in range(QUADS):
                for n in (2 * q, 2 * q + 1):
                    group, tile = (g, n + LEAD) if n + LEAD < S_TILES else (g + 1, n + LEAD - S_TILES)
                    out.append(("s", group, tile) if group < GROUPS else None)
                if q == O_AT:
                    out.append(("o", g - 2, 0) if g >= 1 else None)
                if q == Q_AT:
                    out.append(("q", g + 1, 0) if g + 1 < GROUPS else None)
                if q == K_AT:
                    out.append(("k", g + 1, 0) if g + 1 < GROUPS else None)
                if q == M_AT:
                    out.append(("m", g, 0) if g < GROUPS else None)
            return out

        FIRST = [("q", 0, 0), ("k", 0, 0)] + [("s", 0, n) for n in range(LEAD)]
        ALL = FIRST + [x for g in range(GROUPS + 1) for x in users(g)] + [("o", GROUPS - 1, 0)]
        PLACE = {x: n for n, x in enumerate(ALL) if x is not None}
        FREED = {"s": (max_done, S_TILES, 0), "q": (qt_copied, 1, 0), "k": (kt_copied, 1, 0),
                 "m": (qm_copied, 1, 0), "o": (o_done, 1, 1)}

        def count(group, shift, per, k):
            return group * per + (shift * per + k + 1)

        block = ctx.enter_context(nc.Block())

        def steps(eng, body):
            body(0, 0)
            with eng.Fori(0, (GROUPS - 2) // 2) as i:
                for u in range(2):
                    body(i * 2 + (1 + u), 3 + u)
            body(GROUPS - 1, GROUPS - 1)
            body(GROUPS, GROUPS)


        @block.sync
        def _(sp):
            def pads(dst, src, done):
                for h in range(GH):
                    rows = slice(SR * h, SR * (h + 1))
                    sp.dma_start(dst[rows, h, :].bitcast(F32), src[rows, :].bitcast(F32)).then_inc(done, 16)

            def step(g, r):
                if r < GROUPS:
                    sp.wait_ge(v_ready, count(g, 0, 1, 0))
                    sp.wait_ge(kt_copied, count(g, 0, 1, 0))
                    pads(k_pad[r % 2], k_t[r % 2], k_pad_in)
                if r + 1 < GROUPS:
                    sp.wait_ge(qt_copied, count(g, 1, 1, 0))
                    pads(q_pad[(r + 1) % 2], q_t, q_pad_in)

            sp.wait_ge(zeroed, 4)
            sp.wait_ge(q_pad_zeroed, 1)
            sp.wait_ge(qt_copied, 1)
            pads(q_pad[0], q_t, q_pad_in)
            steps(sp, step)

        @block.gpsimd
        def _(pool):
            def stack(g, r):
                u = r % 2
                q = c.qkv[:, 0, bass.ds(g + 1, 1), :, :][:, 0].rearrange("p t (h d) -> p t h d", h=GH)
                k = c.qkv[:, 1, bass.ds(g + 1, 1), :, :][:, 0].rearrange("p t (h d) -> p t h d", h=GH)
                pool.wait_ge(hi_ready, count(g, 0, 2, 0))
                nc.gpsimd.tensor_tensor(q_nat[u][:, :, :, DB:2 * DB], q, q_nat[u][:, :, :, 0:DB], ALU.subtract)
                nc.gpsimd.tensor_copy(q_nat[u][:, :, :, 2 * DB:3 * DB], q_nat[u][:, :, :, 0:DB])
                nc.gpsimd.memset(q_nat[u][:, :, :, 3 * DB:3 * DB + 2], 0.0).then_inc(stack_ready, 1)
                pool.wait_ge(hi_ready, count(g, 0, 2, 1))
                nc.gpsimd.tensor_tensor(k_nat[:, :, :, 2 * DB:3 * DB], k, k_nat[:, :, :, 0:DB], ALU.subtract)
                nc.gpsimd.tensor_copy(k_nat[:, :, :, DB:2 * DB], k_nat[:, :, :, 0:DB]).then_inc(stack_ready, 1)

            def values(g, r):
                v = c.qkv[:, 2, bass.ds(g + 1, 1), :, :][:, 0].rearrange("p t (h d) -> p t h d", h=GH)
                nc.gpsimd.tensor_copy(v_nat[r % 2][:, :, :, 0:DB], v).then_inc(v_ready, 1)

            def step(g, r):
                if r + 1 < GROUPS:
                    stack(g + 1, r + 1)
                elif r < GROUPS:
                    pool.wait_ge(pv_done, count(g, -2, QUADS, QUADS - 1))
                if r < GROUPS:
                    values(g, r)

            for u in range(2):
                nc.gpsimd.memset(q_nat[u][:, :, :, 3 * DB:], 0.0)
                nc.gpsimd.memset(v_nat[u][:, :, :, DB:], 0.0).then_inc(zeroed, 1)
            nc.gpsimd.memset(k_nat[:, :, :, 3 * DB:], 0.0).then_inc(zeroed, 1)
            pool.wait_ge(zeroed, 3)
            for u in range(2):
                nc.gpsimd.memset(v_nat[u][:, :, :, DB:DB + 1], 1.0)
            nc.gpsimd.memset(k_nat[:, :, :, 3 * DB:3 * DB + 2], 1.0)
            for u in range(2):
                last = nc.gpsimd.memset(k_pad[u][:].bitcast(F32), 0.0)
            last.then_inc(zeroed, 1)
            stack(0, 0)
            steps(pool, step)

        @block.scalar
        def _(act):
            def his(g, r):
                for n, dst in enumerate((q_nat[r % 2], k_nat)):
                    src = c.qkv[:, n, bass.ds(g + 1, 1), :, :][:, 0].rearrange("p t (h d) -> p t h d", h=GH)
                    nc.scalar.activation(dst[:, :, :, 0:DB].bitcast(F32R), src, ACT.Copy).then_inc(hi_ready, 1)

            def place(x):
                return p_s[PLACE[x] % 2]

            def q_copy(g, r):
                act.wait_ge(qt_ready, count(g, 0, 1, 0))
                if r > 0:
                    act.wait_ge(q_pad_in, count(g, -1, 64, 63))
                nc.scalar.activation(q_t[:], place(("q", r, 0))[:], ACT.Copy).then_inc(qt_copied, 1)

            def k_copy(g, r):
                act.wait_ge(kt_ready, count(g, 0, 1, 0))
                nc.scalar.activation(k_t[r % 2][:], place(("k", r, 0))[:], ACT.Copy).then_inc(kt_copied, 1)

            def step(g, r):
                for q in range(QUADS):
                    for h in range(GH):
                        if r > 0:
                            e = 4 * q + h
                            act.wait_ge(st_ready, count(g, -1, 4 * QUADS, e))
                            nc.scalar.activation(prob[(q % 2) * GH + h][:], p_e[e % 2][:], ACT.Exp,
                                                 scale=SCALE).then_inc(exp_done, 1)
                        if h == 0 and r + 1 < GROUPS:
                            if q == 1:
                                if r == 0:
                                    act.wait_ge(kt_ready, 1)
                                his(g + 1, r + 1)
                            if q == Q_AT + 1:
                                q_copy(g + 1, r + 1)
                            if q == K_AT + 1:
                                k_copy(g + 1, r + 1)
                if r < GROUPS:
                    act.wait_ge(qm_ready, count(g, 0, 1, 0))
                    nc.scalar.activation(qm_t[r % 2][:], place(("m", r, 0))[:], ACT.Copy).then_inc(qm_copied, 1)
                if r > 0:
                    act.wait_ge(pv_done, count(g, -1, QUADS, QUADS - 1))
                    nc.scalar.activation(o_t[:], p_o[:], ACT.Copy).then_inc(o_copied, 1)

            act.wait_ge(zeroed, 3)
            nc.scalar.activation(prob[0][:, 0:GH], c.ident[:, 0:GH], ACT.Exp)
            his(0, 0)
            q_copy(0, 0)
            k_copy(0, 0)
            steps(act, step)

        @block.vector
        def _(dve):
            def tile_max(group, shift, r, n):
                dve.wait_ge(s_ready, count(group, shift, S_TILES, n))
                nc.vector.reduce_max(row_max[(r + shift) % 2][:, n // GH, n % GH:n % GH + 1],
                                     p_s[PLACE[("s", r + shift, n)] % 2][:], AX_X).then_inc(max_done, 1)

            def normalize(g, r):
                src = p_s[PLACE[("o", r, 0)] % 2][:].rearrange("p (t h s) -> p t h s", t=TPB, h=GH)
                dve.wait_ge(ot_ready, count(g, 1, 1, 0))
                nc.vector.reciprocal(o_den[:], src[:, :, :, DB]).then_inc(den_done, 1)
                dve.wait_ge(den_done, count(g, 1, 1, 0))
                nc.vector.tensor_tensor(c.qkv[:, 0, bass.ds(g + 1, 1), :, :][:, 0].rearrange("p t (h d) -> p t h d", h=GH),
                                        src[:, :, :, 0:DB], o_den[:].unsqueeze(3).broadcast_to([P, TPB, GH, DB]),
                                        ALU.mult).then_inc(o_done, 1)

            def step(g, r):
                u = r % 2
                for q in range(QUADS):
                    for n in (2 * q, 2 * q + 1):
                        if n + LEAD < S_TILES:
                            if r < GROUPS:
                                tile_max(g, 0, r, n + LEAD)
                        elif r + 1 < GROUPS:
                            tile_max(g, 1, r, n + LEAD - S_TILES)
                        if n + LEAD == S_TILES - 1 and r < GROUPS:
                            dve.wait_ge(max_done, count(g, 0, S_TILES, S_TILES - 1))
                            nc.vector.tensor_scalar(q_nat[u][:, :, :, 3 * DB].bitcast(F32R), row_max[u][:], -1.0, None,
                                                    ALU.mult).then_inc(neg_hi, 1)
                            dve.wait_ge(neg_hi, count(g, 0, 1, 0))
                            nc.vector.scalar_tensor_tensor(
                                out=q_nat[u][:, :, :, 3 * DB + 1].bitcast(F32R), in0=row_max[u][:], scalar=-1.0,
                                in1=q_nat[u][:, :, :, 3 * DB], op0=ALU.mult, op1=ALU.subtract).then_inc(m_ready, 1)
                    if q == O_AT and r > 0:
                        normalize(g - 2, r - 2)

            for u in range(2):
                last = nc.vector.memset(q_pad[u][:].bitcast(F32), 0.0)
            last.then_inc(q_pad_zeroed, 1)
            nc.vector.memset(o_t[:], 1.0).then_inc(o_copied, 1)
            for n in range(LEAD):
                tile_max(0, 0, 0, n)
            steps(dve, step)
            normalize(GROUPS - 1, GROUPS - 1)

        @block.tensor
        def _(pe):
            def place(group, shift, x):
                n = PLACE[x]
                before = [m for m in range(n % 2, n, 2) if ALL[m] is not None]
                if before:
                    kind, at, k = ALL[before[-1]]
                    freed, per, late = FREED[kind]
                    if (kind, at) != ("o", -1) or True:
                        pe.wait_ge(freed, count(group, at - (x[1] - shift) + late, per, k))
                return p_s[n % 2]

            def transposes(dst, src, ready):
                for t in range(TPB):
                    last = nc.tensor.transpose(dst[:, t * P:(t + 1) * P], src(t), c.ident[:])
                last.then_inc(ready, 1)

            def scores(g, r, shift, n, half):
                u, t, h = (r + shift) % 2, n // GH, n % GH
                x = ("s", r + shift, n)
                if n == 0 and half == 0:
                    pe.wait_ge(q_pad_in, count(g, shift, 64, 63))
                    pe.wait_ge(kt_copied, count(g, shift, 1, 0))
                dst = place(g, shift, x) if half == 0 else p_s[PLACE[x] % 2]
                ins = nc.tensor.matmul(dst[:, half * HALF:(half + 1) * HALF], q_pad[u][:, h, t * P:(t + 1) * P],
                                       k_t[u][:, half * HALF:(half + 1) * HALF], start=True, stop=True)
                if half == 1:
                    ins.then_inc(s_ready, 1)

            def scores_t(g, r, q, h):
                u, e, blk, half = (r - 1) % 2, 4 * q + h, q // 2, q % 2
                if e == 0:
                    pe.wait_ge(qm_copied, count(g, -1, 1, 0))
                    pe.wait_ge(k_pad_in, count(g, -1, 64, 63))
                if r > 1 or e >= 2:
                    if e >= 2:
                        pe.wait_ge(exp_done, count(g, -1, 4 * QUADS, e - 2))
                nc.tensor.matmul(p_e[e % 2][:], k_pad[u][:, h, blk * P:(blk + 1) * P],
                                 qm_t[u][:, half * HALF:(half + 1) * HALF], start=True, stop=True).then_inc(st_ready, 1)

            def output(g, r, q, part):
                u, blk, half = (r - 1) % 2, q // 2, q % 2
                if part == 0:
                    if q == 0:
                        pe.wait_ge(v_ready, count(g, -1, 1, 0))
                        pe.wait_ge(o_copied, count(g, -1, 1, 0))
                    pe.wait_ge(exp_done, count(g, -1, 4 * QUADS, 4 * q + 3))
                cols = HALF // PARTS
                for h in range(GH):
                    last = nc.tensor.matmul(p_o[32 * h:32 * (h + 1), half * HALF + part * cols:half * HALF + (part + 1) * cols],
                                            v_nat[u][:, blk, h, :], prob[(q % 2) * GH + h][:, part * cols:(part + 1) * cols],
                                            start=blk == 0 and part == 0, stop=blk == TPB - 1,
                                            skip_group_check=PARTS > 1)
                if part == PARTS - 1:
                    last.then_inc(pv_done, 1)

            def stack_t(g, r, shift, kind, src, stacked, ready):
                pe.wait_ge(stack_ready, count(g, shift, 2, stacked))
                transposes(place(g, shift, (kind, r + shift, 0)), src, ready)

            def step(g, r):
                for q in range(QUADS):
                    for kind, n, half in TURNS:
                        if kind == "scores_t" and r > 0:
                            scores_t(g, r, q, n)
                        if kind == "scores":
                            tile = 2 * q + n + LEAD
                            if tile < S_TILES:
                                if r < GROUPS:
                                    scores(g, r, 0, tile, half)
                            elif r + 1 < GROUPS:
                                scores(g, r, 1, tile - S_TILES, half)
                        if kind == "output" and r > 0 and q >= 1:
                            output(g, r, q - 1, half)
                    if q == O_AT and r > 0:
                        pe.wait_ge(o_copied, count(g, -1, 1, 0))
                        transposes(place(g, -2, ("o", r - 2, 0)), lambda t: o_t[:, t * P:(t + 1) * P], ot_ready)
                    if q == Q_AT and r + 1 < GROUPS:
                        stack_t(g, r, 1, "q", lambda t: q_nat[(r + 1) % 2][:, t], 0, qt_ready)
                    if q == K_AT and r + 1 < GROUPS:
                        stack_t(g, r, 1, "k", lambda t: k_nat[:, t], 1, kt_ready)
                    if q == M_AT and r < GROUPS:
                        pe.wait_ge(m_ready, count(g, 0, 1, 0))
                        transposes(place(g, 0, ("m", r, 0)), lambda t: q_nat[r % 2][:, t], qm_ready)
                if r > 0:
                    for part in range(PARTS):
                        output(g, r, QUADS - 1, part)

            stack_t(0, 0, 0, "q", lambda t: q_nat[0][:, t], 0, qt_ready)
            stack_t(0, 0, 0, "k", lambda t: k_nat[:, t], 1, kt_ready)
            for n in range(LEAD):
                scores(0, 0, 0, n, 0)
                scores(0, 0, 0, n, 1)
            steps(pe, step)
            pe.wait_ge(o_copied, GROUPS + 1)
            transposes(place(GROUPS - 1, 0, ("o", GROUPS - 1, 0)), lambda t: o_t[:, t * P:(t + 1) * P], ot_ready)


def project_out(nc, c, io, tag):
    with ExitStack() as ctx:
        def sb(name, shape, dt=F32):
            return ctx.enter_context(nc.sbuf_tensor(f"{tag}_{name}", shape, dt))

        def psum(name, shape):
            return ctx.enter_context(nc.psum_tensor(f"{tag}_{name}", shape, F32))

        def sem(name):
            return c.sem(f"{tag}_{name}")

        w = sb("w", [P, D])
        bias = sb("bias", [1, D])
        ones = sb("ones", [1, P])
        o = [sb(f"o{u}", [P, TPB, D]) for u in range(2)]
        o_t = [sb(f"o_t{u}", [P, N]) for u in range(2)]
        stats = sb("stats", [P, TPB, 6])
        moments = sb("moments", [P, TPB, 2])
        p_t = [psum(f"p_t{u}", [P, N]) for u in range(2)]
        p_y = [psum(f"p_y{u}", [P, TPB, D]) for u in range(2)]
        w_in = sem("w_in")
        gathered = sem("gathered")
        t_ready = sem("t_ready")
        t_copied = sem("t_copied")
        y_ready = sem("y_ready")
        x_added = sem("x_added")
        counted = sem("counted")
        moved = sem("moved")
        ones_ready = sem("ones_ready")
        block = ctx.enter_context(nc.Block())

        @block.sync
        def _(sp):
            sp.dma_start(w[:], io["wo_b"]).then_inc(w_in, 16)
            sp.dma_start(bias[:], io["bo_b"]).then_inc(w_in, 16)

        @block.scalar
        def _(act):
            with act.Fori(0, B // 2) as i:
                for u in range(2):
                    b = i * 2 + u
                    nc.scalar.activation(o[u][:].rearrange("p t (g d) -> p g t d", g=GPB),
                                         c.qkv[:, 0, bass.ds(b * GPB + 1, GPB), :, :], ACT.Copy).then_inc(gathered, 1)
                for u in range(2):
                    act.wait_ge(t_ready, i * 2 + (u + 1))
                    nc.scalar.activation(o_t[u][:], p_t[u][:], ACT.Copy).then_inc(t_copied, 1)

        @block.vector
        def _(dve):
            nc.vector.memset(ones[:], 1.0).then_inc(ones_ready, 1)
            with dve.Fori(0, B // 2) as i:
                for u in range(2):
                    b = i * 2 + u
                    dve.wait_ge(y_ready, b + 1)
                    nc.vector.tensor_tensor(residual_tiles(c.x, b * TPB, TPB), residual_tiles(c.x, b * TPB, TPB),
                                            p_y[u][:], ALU.add).then_inc(x_added, 1)
                    nc.vector.drain()
                    for t in range(TPB):
                        nc.vector.bn_stats(stats[:, t, :], residual_tiles(c.x, b * TPB + t, 1)[:, 0, :]).then_inc(counted, 1)
                    nc.vector.drain()
                    for t in range(TPB):
                        nc.vector.bn_aggr(moments[:, t, :], stats[:, t, :]).then_inc(counted, 1)
                    nc.vector.drain()
                    nc.vector.tensor_copy(c.mv[:, bass.ds(b * TPB + PAD, TPB), :], moments[:]).then_inc(moved, 1)
                    dve.wait_ge(moved, b + 1)

        @block.tensor
        def _(pe):
            pe.wait_ge(w_in, 32)
            pe.wait_ge(ones_ready, 1)
            with pe.Fori(0, B // 2) as i:
                for u in range(2):
                    pe.wait_ge(gathered, i * 2 + (u + 1))
                    for t in range(TPB):
                        last = nc.tensor.transpose(p_t[u][:, t * P:(t + 1) * P], o[u][:, t, :], c.ident[:])
                    last.then_inc(t_ready, 1)
                for u in range(2):
                    pe.wait_ge(t_copied, i * 2 + (u + 1))
                    for t in range(TPB):
                        nc.tensor.matmul(p_y[u][:, t, :], o_t[u][:, t * P:(t + 1) * P], w[:], start=True, stop=False)
                        last = nc.tensor.matmul(p_y[u][:, t, :], ones[:], bias[:], start=False, stop=True)
                    last.then_inc(y_ready, 1)
                for u in range(2):
                    pe.wait_ge(x_added, i * 2 + (u + 1))


def program(nc, io, out):
    with ExitStack() as ctx:
        c = Chip(nc, ctx)
        c.x = c.sb("x", [P, TILES + 2 * PAD, D])
        c.mv = c.sb("mean_var", [P, TILES + 2 * PAD, 2])
        c.rstd = c.sb("rstd", [P, TILES + 2 * PAD])
        c.ident = c.sb("ident", [P, P])
        c.iota = c.sb("iota", [P, E])
        attention_a(nc, c, io)
        feed_forward(nc, c, io, "f1")
        with nc.sbuf_tensor("qkv", [P, 3, GROUPS + 1, TPB, GC], F32) as c.qkv:
            project_qkv(nc, c, io, "q")
            softmax_attention(nc, c, io, "s")
            project_out(nc, c, io, "o")
        feed_forward(nc, c, io, "f2", out)


def layouts(a):
    import numpy as np

    g = {k: np.asarray(v) for k, v in a.items()}
    w_qkv, b_qkv = g["L0_attn_a_w_qkv"], g["L0_attn_a_b_qkv"]
    wo_a = g["L0_attn_a_w_o"].T.reshape(NA, D // NA, D).transpose(1, 0, 2).reshape(D, D)
    w_ffn = np.zeros((E, D, 2 * HID + NBLK * D), np.float32)
    w_ffn[:, :, 0:HID] = g["L0_ffn_W1"].transpose(0, 2, 1)
    w_ffn[:, :, HID:2 * HID] = g["L0_ffn_W2"].transpose(0, 2, 1)
    for j, (first, rows) in enumerate(BLOCKS):
        w_ffn[:, 0:rows, 2 * HID + j * D:2 * HID + (j + 1) * D] = g["L0_ffn_W3"][:, :, first:first + rows].transpose(0, 2, 1)
    io = {
        "x": g["L0_attn_a_x"],
        "wkv_a": w_qkv[D:].T, "wq_a": w_qkv[:D], "wo_a": wo_a,
        "bkv_a": np.broadcast_to(b_qkv[D:], (P, 2 * D)), "bq_a": b_qkv[:D, None],
        "bo_a": g["L0_attn_a_b_o"][None, :],
        "head_mask": (np.arange(P)[:, None] % NA == np.arange(P)[None, :] % NA).astype(np.float32),
        "ident": np.eye(P, dtype=np.float32),
        "w_b": np.concatenate([g[f"L0_attn_b_W{n}"] for n in "qkv"], 1),
        "b_b": np.broadcast_to(np.concatenate([g[f"L0_attn_b_b{n}"] for n in "qkv"]), (P, 3 * D)),
        "wo_b": g["L0_attn_b_Wo"], "bo_b": g["L0_attn_b_bo"][None, :],
        "wg": g["L0_ffn_Wg"].T,
        "w_ffn": w_ffn,
        "iota": np.broadcast_to(np.arange(E, dtype=np.float32), (P, E)),
    }
    return {k: np.ascontiguousarray(v) for k, v in io.items()}


def kernel(**inputs):
    import concourse.bacc as bacc
    from concourse.bass_utils import run_bass_kernel_spmd

    arrays = layouts(inputs)
    nc = bacc.Bacc("TRN2", target_bir_lowering=False, num_devices=1)
    io = {k: nc.dram_tensor(f"in_{k}", v.shape, F32, kind="ExternalInput").ap() for k, v in arrays.items()}
    out = nc.dram_tensor("out", (B, N, D), F32, kind="ExternalOutput").ap()
    program(nc, io, out)
    r = run_bass_kernel_spmd(nc, [{f"in_{k}": v for k, v in arrays.items()}], core_ids=[0])
    return r.results[0]["out"]
```

```python
from contextlib import ExitStack

import concourse.bass as bass
from concourse import mybir

F32 = mybir.dt.float32
F32R = mybir.dt.float32r
U32 = mybir.dt.uint32
ALU = mybir.AluOpType
ACT = mybir.ActivationFunctionType
AX_X = mybir.AxisListType.X

P = 128
B, N, D = 4, 1024, 128
TPB = N // P
TILES = B * TPB
E, HID, TOP = 8, 352, 2
NA = 8
NB, DB = 16, 8
EPS = 1e-5
CT = 4
CHUNK = CT * P
CHUNKS = TILES // CT
PAD, TAIL = CT, TPB
WHOLE = HID // P
REST = HID - WHOLE * P


def packed(n):
    parts, row = [], 0
    for e in range(E):
        lo, hi = max(e * REST, n * P), min((e + 1) * REST, (n + 1) * P)
        if lo < hi:
            parts.append((e, WHOLE * P + lo - e * REST, hi - lo))
    placed = []
    for e, first, count in sorted(parts, key=lambda part: -part[2]):
        placed.append((row, e, first, count))
        row += count
    return placed


BLOCKS = []
for e in range(E):
    BLOCKS += [[(0, e, j * P, P)] for j in range(WHOLE)]
    BLOCKS += [packed(n) for n in range(E * REST // P) if ((n + 1) * P - 1) // REST == e]
assert E * REST % P == 0
KPC = len(BLOCKS)
PACKED = sum(len(block) > 1 for block in BLOCKS)
GH = 4
GPB = NB // GH
GROUPS = B * GPB
SR = P // GH
GC = GH * DB


class Chip:

    def __init__(self, nc, ctx):
        self.nc, self.ctx = nc, ctx

    def sb(self, name, shape, dt=F32):
        return self.ctx.enter_context(self.nc.sbuf_tensor(name, shape, dt))

    def sem(self, name):
        return self.ctx.enter_context(self.nc.semaphore(name))


def residual_tiles(x, first, count):
    return x[:, bass.ds(first + PAD, count), :]


def attention_a(nc, c, io, weights):
    PAIR = 2 * TPB
    with ExitStack() as ctx:
        def sb(name, shape, dt=F32):
            return ctx.enter_context(nc.sbuf_tensor(name, shape, dt))

        def psum(name, shape):
            return ctx.enter_context(nc.psum_tensor(name, shape, F32))

        wkv = sb("a_wkv", [P, 2 * D])
        wq = sb("a_wq", [P, D])
        wo = sb("a_wo", [P, D])
        bkv = sb("a_bkv", [P, 2 * D])
        bq = sb("a_bq", [P, P])
        bo = sb("a_bo", [P, D])
        mask = sb("a_mask", [P, P])
        xn = [sb(f"a_xn{u}", [P, TPB, D]) for u in range(2)]
        xnt = [sb(f"a_xnt{u}", [P, N]) for u in range(2)]
        kv = [sb(f"a_kv{n}", [P, 2 * D]) for n in range(4)]
        vk = [sb(f"a_vk{u}", [P, P]) for u in range(2)]
        vk_wo = [sb(f"a_vk_wo{u}", [P, D]) for u in range(2)]
        fold = [sb(f"a_fold{u}", [P, D]) for u in range(2)]
        bias = [sb(f"a_bias{u}", [P, D]) for u in range(2)]
        stats = sb("a_stats", [P, PAIR, 6])
        moments = sb("a_moments", [P, PAIR, 2])
        rstd = sb("a_rstd", [P, PAIR])
        p_big = [psum(f"a_p_big{u}", [P, TPB, D]) for u in range(2)]
        p_kv = [psum(f"a_p_kv{n}", [P, 512]) for n in range(2)]
        p_fold = [psum(f"a_p_fold{u}", [P, 4, D]) for u in range(2)]

        x_in = [c.sem(f"a_x_in{n}") for n in range(2)]
        w_in = c.sem("a_w_in")
        dve_step = c.sem("a_dve_step")
        var_ready = c.sem("a_var_ready")
        sqrt_done = c.sem("a_sqrt_done")
        xn_ready = c.sem("a_xn_ready")
        xt_ready = c.sem("a_xt_ready")
        xnt_ready = c.sem("a_xnt_ready")
        kv_ready = c.sem("a_kv_ready")
        kv_copied = c.sem("a_kv_copied")
        vk_ready = c.sem("a_vk_ready")
        vk_masked = c.sem("a_vk_masked")
        vkwo_ready = c.sem("a_vkwo_ready")
        vkwo_copied = c.sem("a_vkwo_copied")
        fold_ready = c.sem("a_fold_ready")
        fold_copied = c.sem("a_fold_copied")
        bias_copied = c.sem("a_bias_copied")
        y_ready = c.sem("a_y_ready")

        loads = [(c.ident, io["ident"]), (wkv, io["wkv_a"]), (bkv, io["bkv_a"]), (mask, io["head_mask"]),
                 (wo, io["wo_a"]), (wq, io["wq_a"]), (bq, io["bq_a"]), (bo, io["bo_a"]), (c.iota, io["iota"])]
        later = [(c.w_qkv, io["w_b"]), (c.b_qkv, io["b_b"]), (c.w_o, io["wo_b"]), (c.b_o, io["bo_b"])]
        later_in = c.sem("a_later_in")
        weights.begin(ctx)
        block = ctx.enter_context(nc.Block())

        @block.sync
        def _(sp):
            for b in range(B):
                sp.dma_start(c.x[:, PAD + b * TPB:PAD + (b + 1) * TPB, :],
                             io["x"][b].rearrange("(p j) d -> p j d", p=P)).then_inc(x_in[b // 2], 16)
            weights.load(sp, io)
            for dst, src in later:
                sp.dma_start(dst[:], src).then_inc(later_in, 16)
            sp.wait_ge(later_in, 16 * len(later))

        @block.gpsimd
        def _(pool):
            weights.split(pool, slice(None))

        @block.scalar
        def _(act):
            for dst, src in loads:
                act.dma_start(dst[:], src).then_inc(w_in, 16)
            with act.Fori(0, B // 2) as i:
                act.wait_ge(var_ready, i + 1)
                nc.scalar.activation(rstd[:], rstd[:], ACT.Sqrt).then_inc(sqrt_done, 1)
                for u in range(2):
                    act.wait_ge(xt_ready, i * 2 + (u + 1))
                    nc.scalar.activation(xnt[u][:], p_big[u][:].rearrange("p t d -> p (t d)"), ACT.Copy).then_inc(xnt_ready, 1)
                for u in range(2):
                    act.wait_ge(vkwo_ready, i * 2 + (u + 1))
                    nc.scalar.activation(vk_wo[u][:], p_fold[u][:, 1], ACT.Copy).then_inc(vkwo_copied, 1)
                    act.wait_ge(fold_ready, i * 2 + (u + 1))
                    nc.scalar.activation(fold[u][:], p_fold[u][:, 2], ACT.Copy).then_inc(fold_copied, 1)

        @block.vector
        def _(dve):
            def mask_vk(i, u):
                dve.wait_ge(vk_ready, i * PAIR + (u + 1) * TPB)
                nc.vector.tensor_tensor(vk[u][:], p_fold[u][:, 0], mask[:], ALU.mult).then_inc(vk_masked, 1)

            def bias_of(i, u):
                dve.wait_ge(fold_ready, i * 2 + (u + 1))
                dve.wait_ge(fold_copied, i * 2 + (u + 1))
                nc.vector.tensor_tensor(bias[u][:], p_fold[u][:, 3], bo[:], ALU.add).then_inc(bias_copied, 1)

            nc.vector.memset(c.mv[:], 0.0)
            nc.vector.memset(c.rstd[:], 1.0)
            nc.vector.memset(c.x[:, 0:PAD, :], 0.0)
            nc.vector.memset(c.x[:, PAD + TILES:, :], 0.0)
            dve.wait_ge(x_in[0], 32)
            with dve.Fori(0, B // 2) as i:
                for t in range(PAIR):
                    nc.vector.bn_stats(stats[:, t, :], residual_tiles(c.x, i * PAIR + t, 1)[:, 0, :]).then_inc(dve_step, 1)
                nc.vector.drain()
                for t in range(PAIR):
                    nc.vector.bn_aggr(moments[:, t, :], stats[:, t, :]).then_inc(dve_step, 1)
                nc.vector.drain()
                nc.vector.tensor_scalar(rstd[:], moments[:, :, 1], EPS, None, ALU.add).then_inc(var_ready, 1)
                dve.wait_ge(sqrt_done, i + 1)
                nc.vector.reciprocal(rstd[:], rstd[:]).then_inc(dve_step, 1)
                nc.vector.drain()
                for u in range(2):
                    for t in range(TPB):
                        at = slice(u * TPB + t, u * TPB + t + 1)
                        last = nc.vector.tensor_scalar(xn[u][:, t, :], residual_tiles(c.x, i * PAIR + (u * TPB + t), 1)[:, 0, :],
                                                       moments[:, at, 0], rstd[:, at], ALU.subtract, ALU.mult)
                    last.then_inc(xn_ready, 1)
                dve.wait_ge(w_in, 16 * len(loads))
                for n in range(PAIR):
                    dve.wait_ge(kv_ready, i * PAIR + (n + 1))
                    if n >= 4:
                        dve.wait_ge(vk_ready, i * PAIR + (n - 3))
                    nc.vector.tensor_tensor(kv[n % 4][:], p_kv[n % 2][:, 0:2 * D], bkv[:], ALU.add).then_inc(kv_copied, 1)
                    if n == TPB + 1:
                        mask_vk(i, 0)
                mask_vk(i, 1)
                for u in range(2):
                    bias_of(i, u)
                    nc.vector.drain()
                    tiles = residual_tiles(c.x, i * PAIR + u * TPB, TPB)
                    nc.vector.tensor_tensor(tiles, tiles, bias[u][:].unsqueeze(1).broadcast_to([P, TPB, D]),
                                            ALU.add).then_inc(dve_step, 1)
                nc.vector.drain()
                for u in range(2):
                    tiles = residual_tiles(c.x, i * PAIR + u * TPB, TPB)
                    dve.wait_ge(y_ready, i * 2 + (u + 1))
                    nc.vector.tensor_tensor(tiles, tiles, p_big[u][:], ALU.add).then_inc(dve_step, 1)
                    nc.vector.drain()
                    for t in range(TPB):
                        nc.vector.bn_stats(stats[:, u * TPB + t, :], residual_tiles(c.x, i * PAIR + (u * TPB + t), 1)[:, 0, :]).then_inc(dve_step, 1)
                nc.vector.drain()
                for t in range(PAIR):
                    nc.vector.bn_aggr(moments[:, t, :], stats[:, t, :]).then_inc(dve_step, 1)
                nc.vector.drain()
                nc.vector.tensor_copy(c.mv[:, bass.ds(i * PAIR + PAD, PAIR), :], moments[:]).then_inc(dve_step, 1)
                nc.vector.drain()
                dve.wait_ge(x_in[1], 32)

        @block.tensor
        def _(pe):
            def vk_wo_of(i, u):
                pe.wait_ge(vk_masked, i * 2 + (u + 1))
                nc.tensor.matmul(p_fold[u][:, 1], vk[u][:], wo[:], start=True, stop=True).then_inc(vkwo_ready, 1)

            def fold_of(i, u):
                pe.wait_ge(vkwo_copied, i * 2 + (u + 1))
                nc.tensor.matmul(p_fold[u][:, 2], wq[:], vk_wo[u][:], start=True, stop=True)
                nc.tensor.matmul(p_fold[u][:, 3], bq[:], vk_wo[u][:], start=True, stop=True).then_inc(fold_ready, 1)

            def vk_of(i, n):
                u, t = n // TPB, n % TPB
                pe.wait_ge(kv_copied, i * PAIR + (n + 1))
                nc.tensor.matmul(p_fold[u][:, 0], kv[n % 4][:, D:2 * D], kv[n % 4][:, 0:D],
                                 start=t == 0, stop=t == TPB - 1).then_inc(vk_ready, 1)

            def output(i, u, tiles):
                for t in tiles:
                    last = nc.tensor.matmul(p_big[u][:, t, :], xnt[u][:, t * P:(t + 1) * P], fold[u][:], start=True, stop=True)
                return last

            pe.wait_ge(w_in, 16 * len(loads))
            with pe.Fori(0, B // 2) as i:
                for u in range(2):
                    pe.wait_ge(xn_ready, i * 2 + (u + 1))
                    for t in range(TPB):
                        last = nc.tensor.transpose(p_big[u][:, t, :], xn[u][:, t, :], c.ident[:])
                    last.then_inc(xt_ready, 1)
                for n in range(PAIR):
                    u, t = n // TPB, n % TPB
                    if t == 0:
                        pe.wait_ge(xnt_ready, i * 2 + (u + 1))
                    if n >= 2:
                        pe.wait_ge(kv_copied, i * PAIR + (n - 1))
                    nc.tensor.matmul(p_kv[n % 2][:, 0:2 * D], xnt[u][:, t * P:(t + 1) * P], wkv[:],
                                     start=True, stop=True).then_inc(kv_ready, 1)
                    if n >= 1:
                        vk_of(i, n - 1)
                    if n == TPB + 3:
                        vk_wo_of(i, 0)
                    if n == TPB + 6:
                        fold_of(i, 0)
                vk_of(i, PAIR - 1)
                pe.wait_ge(fold_copied, i * 2 + 1)
                output(i, 0, range(0, 3))
                vk_wo_of(i, 1)
                output(i, 0, range(3, 6))
                fold_of(i, 1)
                output(i, 0, range(6, TPB)).then_inc(y_ready, 1)
                pe.wait_ge(fold_copied, i * 2 + 2)
                output(i, 1, range(TPB)).then_inc(y_ready, 1)


class ExpertWeights:
    PIECE = 2

    def __init__(self, nc, c, ctx, tag):
        self.nc, self.c, self.tag = nc, c, tag

        def pair(name, shape):
            return [ctx.enter_context(nc.sbuf_tensor(f"{tag}_{name}_{part}", shape, F32R)) for part in ("hi", "lo")]

        self.w = pair("w", [P, KPC, 3, P])
        self.wg = pair("wg", [P, E])
        self.spread = pair("spread", [2 * E, E * P])

    def begin(self, ctx):
        def raw(name, like):
            return ctx.enter_context(self.nc.sbuf_tensor(f"{self.tag}_{name}", like[0].shape, F32))

        w, wg, spread = raw("w_raw", self.w), raw("wg_raw", self.wg), raw("spread_raw", self.spread)
        self.hi_done = self.c.sem(f"{self.tag}_hi_done")
        self.own_hi_done = self.c.sem(f"{self.tag}_own_hi_done")
        self.lo_done = self.c.sem(f"{self.tag}_lo_done")
        self.dve_lo_done = self.c.sem(f"{self.tag}_dve_lo_done")
        self.pieces = [(wg[:], self.wg[0][:], self.wg[1][:], self.c.sem(f"{self.tag}_wg_in")),
                       (spread[:], self.spread[0][:], self.spread[1][:], self.c.sem(f"{self.tag}_spread_in"))]
        for n in range(KPC // self.PIECE):
            at = slice(n * self.PIECE, (n + 1) * self.PIECE)
            self.pieces.append((w[:, at], self.w[0][:, at], self.w[1][:, at], self.c.sem(f"{self.tag}_in{n}")))

    def load(self, eng, io):
        sources = [io["wg"], io["spread"]] + [io["w_ffn"][:, n:n + self.PIECE] for n in range(0, KPC, self.PIECE)]
        for (raw, hi, lo, raw_in), source in zip(self.pieces, sources):
            eng.dma_start(raw, source).then_inc(raw_in, 16)

    def split_hi(self, act, which):
        for raw, hi, lo, raw_in in self.pieces[which]:
            act.wait_ge(raw_in, 16)
            self.nc.scalar.activation(hi, raw, ACT.Copy).then_inc(self.hi_done, 1)

    def split_lo(self, eng, ops, which, before, done):
        for n, (raw, hi, lo, raw_in) in enumerate(self.pieces[which]):
            eng.wait_ge(self.hi_done, before + n + 1)
            ops.tensor_tensor(lo, raw, hi.bitcast(F32), ALU.subtract).then_inc(done, 1)

    def split(self, pool, which):
        for n, (raw, hi, lo, raw_in) in enumerate(self.pieces[which]):
            pool.wait_ge(raw_in, 16)
            self.nc.gpsimd.tensor_scalar(hi, raw, 1.0, None, ALU.mult).then_inc(self.own_hi_done, 1)
            pool.wait_ge(self.own_hi_done, n + 1)
            self.nc.gpsimd.tensor_tensor(lo, raw, hi.bitcast(F32), ALU.subtract).then_inc(self.lo_done, 1)


def feed_forward(nc, c, w, tag, out=None):
    UNROLL = 2
    LAG = 3
    RING = LAG + 1
    ROWS = 4
    with ExitStack() as ctx:
        def sb(name, shape, dt=F32):
            return ctx.enter_context(nc.sbuf_tensor(f"{tag}_{name}", shape, dt))

        def psum(name, shape):
            return ctx.enter_context(nc.psum_tensor(f"{tag}_{name}", shape, F32))

        def sem(name):
            return c.sem(f"{tag}_{name}")

        xn = sb("xn", [P, CT, D])
        xt_hi = [sb(f"xt_hi{u}", [P, CHUNK], F32R) for u in range(2)]
        xt_lo = [sb(f"xt_lo{u}", [P, CHUNK], F32R) for u in range(2)]
        mix = sb("mix", [P, CT, E])
        mix_parts = sb("mix_parts", [P, CT, 2 * E])
        mix_t = [sb(f"mix_t{u}", [2 * E, CHUNK], F32R) for u in range(2)]
        mix_rows = [sb(f"mix_rows{u}", [P, CHUNK]) for u in range(ROWS)]
        gate = [sb(f"gate{u}", [P, CHUNK]) for u in range(2)]
        hid = [sb(f"hid{u}", [P, CHUNK]) for u in range(RING)]
        hid_hi = [sb(f"hid_hi{u}", [P, CHUNK], F32R) for u in range(RING)]
        hid_lo = [sb(f"hid_lo{u}", [P, CHUNK], F32R) for u in range(RING)]
        y_t = sb("y_t", [P, CHUNK])
        score = sb("score", [P, CT, E])
        best = sb("best", [P, CT, 8])
        best_at = sb("best_at", [P, CT, 8], U32)
        best_atf = sb("best_atf", [P, CT, 8])
        onehot = sb("onehot", [P, CT, TOP, E])
        stats = sb("stats", [P, CT, 6])
        moments = sb("moments", [P, CT, 2])

        p_gate = [psum(f"p_gate{u}", [P, CHUNK]) for u in range(2)]
        p_up = [psum(f"p_up{u}", [P, CHUNK]) for u in range(2)]
        p_y = psum("p_y", [P, CHUNK])
        p_mix = psum("p_mix", [P, CHUNK])
        p_t = psum("p_t", [P, CHUNK])
        p_score = psum("p_score", [P, CT, E])

        zeroed = sem("zeroed")
        sqrt_ready = sem("sqrt_ready")
        var_ready = sem("var_ready")
        xn_ready = sem("xn_ready")
        xt_ready = sem("xt_ready")
        xt_hi_ready = sem("xt_hi_ready")
        xt_lo_ready = sem("xt_lo_ready")
        scores_ready = sem("scores_ready")
        scores_copied = sem("scores_copied")
        mix_ready = sem("mix_ready")
        mix_t_ready = sem("mix_t_ready")
        mix_t_copied = sem("mix_t_copied")
        spread_ready = sem("spread_ready")
        spread_copied = sem("spread_copied")
        gate_ready = sem("gate_ready")
        up_ready = sem("up_ready")
        silu_done = sem("silu_done")
        mixed = sem("mixed")
        own_mixed = sem("own_mixed")
        hid_ready = sem("hid_ready")
        hid_hi_ready = sem("hid_hi_ready")
        hid_lo_ready = sem("hid_lo_ready")
        down_done = sem("down_done")
        y_copied = sem("y_copied")
        yt_ready = sem("yt_ready")
        x_added = sem("x_added")
        dve_step = sem("dve_step")
        moved = sem("moved")
        stored = sem("stored")

        def three(out_ap, lhs, rhs, start=True, stop=True):
            nc.tensor.matmul(out_ap, lhs[0], rhs[0], start=start, stop=False)
            nc.tensor.matmul(out_ap, lhs[1], rhs[0], start=False, stop=False)
            return nc.tensor.matmul(out_ap, lhs[0], rhs[1], start=False, stop=stop)

        SPREADS = {BLOCKS.index([(0, e, P, P)]): e + 1 for e in range(E)}
        def mix_part(eng, k, n):
            row, e, _, count = BLOCKS[k][n]
            rows = slice(row, row + count)
            return eng.tensor_tensor(gate[k % 2][rows], gate[k % 2][rows], mix_rows[e % ROWS][rows], ALU.mult)

        def blocks(i, u):
            return [(i * (UNROLL * KPC) + (u * KPC + k), k, u * KPC + k) for k in range(KPC)]

        STEPS = 2 * CT + 5 + 2 * CT
        NORM_AT, NORM_T_AT, XT_AT, SCORES_AT, BEST_AT = 0, 2, 4, 6, 8
        Y_T_AT, Y_AT, STATS_AT, MIX_T_AT, MIX_COPY_AT = 7, 12, 16, 16, 18

        block = ctx.enter_context(nc.Block())

        @block.sync
        def _(sp):
            if out is not None:
                halves = TPB // CT
                rows = out.rearrange("b (p j) d -> p b j d", p=P)
                with sp.Fori(0, B) as b:
                    for h in range(halves):
                        sp.wait_ge(x_added, b * halves + (h + 2))
                        sp.dma_start(rows[:, bass.ds(b, 1), h * CT:(h + 1) * CT, :][:, 0],
                                     residual_tiles(c.x, b * TPB + h * CT, CT)).then_inc(stored, 16)
                sp.wait_ge(stored, 16 * CHUNKS)

        @block.gpsimd
        def _(pool):
            for v in range(LAG):
                nc.gpsimd.memset(hid_hi[v][:].bitcast(F32), 0.0).then_inc(zeroed, 1)
                nc.gpsimd.memset(hid_lo[v][:].bitcast(F32), 0.0).then_inc(zeroed, 1)
            nc.gpsimd.memset(mix_rows[ROWS - 1][:, 0:1], 0.0).then_inc(mixed, 1)
            with pool.Fori(0, CHUNKS // UNROLL) as i:
                for u in range(UNROLL):
                    for kk, k, v in blocks(i, u):
                        pool.wait_ge(spread_copied, i * (UNROLL * E) + (u * E + max(e for _, e, _, _ in BLOCKS[k]) + 1))
                        pool.wait_ge(silu_done, kk + 1)
                        if len(BLOCKS[k]) != len(BLOCKS[k - 1]):
                            pool.wait_ge(mixed, kk + 1)
                        mix_part(nc.gpsimd, k, 0).then_inc(mixed, 1)

        @block.scalar
        def _(act):
            def hi_of_xt(u, count):
                act.wait_ge(xt_ready, count)
                nc.scalar.activation(xt_hi[u][:], p_t[:], ACT.Copy).then_inc(xt_hi_ready, 1)

            def copy_mix(u, count):
                act.wait_ge(mix_t_ready, count)
                nc.scalar.activation(mix_t[u][:], p_t[0:2 * E, :], ACT.Copy).then_inc(mix_t_copied, 1)

            def copy_spread(n, count):
                act.wait_ge(spread_ready, count)
                nc.scalar.activation(mix_rows[n % ROWS][:], p_mix[:], ACT.Copy).then_inc(spread_copied, 1)

            def hi_of_hid(v, hid_count, down_count):
                act.wait_ge(hid_ready, hid_count)
                act.wait_ge(down_done, down_count)
                nc.scalar.activation(hid_hi[v % RING][:], hid[v % RING][:], ACT.Copy).then_inc(hid_hi_ready, 1)

            act.wait_ge(var_ready, 1)
            nc.scalar.activation(c.rstd[:, PAD:PAD + TILES], c.rstd[:, PAD:PAD + TILES], ACT.Sqrt).then_inc(sqrt_ready, 1)
            nc.scalar.activation(gate[0][:, 0:1], c.ident[:, 0:1], ACT.Silu)
            hi_of_xt(0, 1)
            copy_mix(0, 1)
            copy_spread(0, 1)
            with act.Fori(0, CHUNKS // UNROLL) as i:
                for u in range(UNROLL):
                    for kk, k, v in blocks(i, u):
                        if k == LAG:
                            act.wait_ge(down_done, i * (UNROLL * KPC) + (u * KPC + LAG + 2))
                            nc.scalar.activation(y_t[:], p_y[:], ACT.Copy).then_inc(y_copied, 1)
                        act.wait_ge(gate_ready, kk + 1)
                        nc.scalar.activation(gate[k % 2][:], p_gate[k % 2][:], ACT.Silu).then_inc(silu_done, 1)
                        hi_of_hid(v - 1, kk + 2, kk + 1)
                        if k in SPREADS:
                            copy_spread(SPREADS[k], i * (UNROLL * E) + (u * E + SPREADS[k] + 1))
                        if k == XT_AT:
                            hi_of_xt(1 - u, i * UNROLL + (u + 2))
                        if k == MIX_COPY_AT:
                            copy_mix(1 - u, i * UNROLL + (u + 2))
            hi_of_hid(UNROLL * KPC - 1, CHUNKS * KPC + 2, CHUNKS * KPC + 1)
            act.wait_ge(down_done, CHUNKS * KPC + LAG + 2)
            nc.scalar.activation(y_t[:], p_y[:], ACT.Copy).then_inc(y_copied, 1)

        @block.vector
        def _(dve):
            def step(ins):
                ins.then_inc(dve_step, 1)

            def norm(first):
                for t in range(CT):
                    at = bass.ds(first + (PAD + t), 1)
                    last = nc.vector.tensor_scalar(xn[:, t, :], c.x[:, at, :][:, 0, :], c.mv[:, at, 0], c.rstd[:, at],
                                                   ALU.subtract, ALU.mult)
                last.then_inc(xn_ready, 1)

            def lo_of_xt(u, count):
                dve.wait_ge(xt_hi_ready, count)
                nc.vector.tensor_tensor(xt_lo[u][:], p_t[:], xt_hi[u][:].bitcast(F32), ALU.subtract).then_inc(xt_lo_ready, 1)

            def lo_of_hid(v, count):
                dve.wait_ge(hid_hi_ready, count)
                nc.vector.tensor_tensor(hid_lo[v % RING][:], hid[v % RING][:],
                                        hid_hi[v % RING][:].bitcast(F32), ALU.subtract).then_inc(hid_lo_ready, 1)

            def copy_scores(count):
                dve.wait_ge(scores_ready, count)
                nc.vector.tensor_copy(score[:], p_score[:]).then_inc(scores_copied, 1)

            def find_best():
                for t in range(CT):
                    step(nc.vector.max(best[:, t, :], score[:, t, :]))

            def find_where():
                for t in range(CT):
                    step(nc.vector.max_index(best_at[:, t, :], best[:, t, :], score[:, t, :]))

            def mix_of(s):
                dve.wait_ge(dve_step, s + 2 * CT)
                step(nc.vector.tensor_copy(best_atf[:], best_at[:]))
                dve.wait_ge(dve_step, s + (2 * CT + 1))
                step(nc.vector.tensor_tensor(
                    onehot[:], c.iota[:].unsqueeze(1).unsqueeze(1).broadcast_to([P, CT, TOP, E]),
                    best_atf[:, :, 0:TOP].unsqueeze(3).broadcast_to([P, CT, TOP, E]), ALU.is_equal))
                dve.wait_ge(dve_step, s + (2 * CT + 2))
                step(nc.vector.tensor_tensor(
                    onehot[:], onehot[:], best[:, :, 0:TOP].unsqueeze(3).broadcast_to([P, CT, TOP, E]), ALU.mult))
                dve.wait_ge(dve_step, s + (2 * CT + 3))
                step(nc.vector.tensor_tensor(mix[:], onehot[:, :, 0, :], onehot[:, :, 1, :], ALU.add))

            def parts_of_mix(s):
                dve.wait_ge(dve_step, s + (2 * CT + 4))
                step(nc.vector.tensor_scalar(mix_parts[:, :, 0:E].bitcast(F32R), mix[:], 1.0, None, ALU.mult))
                dve.wait_ge(dve_step, s + (2 * CT + 5))
                nc.vector.tensor_tensor(mix_parts[:, :, E:2 * E].bitcast(F32R), mix[:], mix_parts[:, :, 0:E],
                                        ALU.subtract).then_inc(mix_ready, 1)

            PRE = 2 * CT + 5
            OWN = {BEST_AT + 1: CT, STATS_AT + 1: PRE + CT, STATS_AT + 2: PRE + 2 * CT}
            nc.vector.tensor_scalar(c.rstd[:, PAD:PAD + TILES], c.mv[:, PAD:PAD + TILES, 1], EPS, None, ALU.add).then_inc(var_ready, 1)
            dve.wait_ge(sqrt_ready, 1)
            nc.vector.reciprocal(c.rstd[:, PAD:PAD + TILES], c.rstd[:, PAD:PAD + TILES]).then_inc(var_ready, 1)
            dve.wait_ge(var_ready, 2)
            norm(0)
            for v in range(RING - 2, RING):
                nc.vector.memset(hid[v][:], 0.0).then_inc(hid_ready, 1)
            for n in range(2):
                nc.vector.memset(y_t[:, n * P:(n + 1) * P], 0.0).then_inc(hid_lo_ready, 1)
            lo_of_xt(0, 1)
            copy_scores(1)
            dve.wait_ge(scores_copied, 1)
            find_best()
            dve.wait_ge(dve_step, CT)
            find_where()
            mix_of(0)
            parts_of_mix(0)
            with dve.Fori(0, CHUNKS // UNROLL) as i:
                for u in range(UNROLL):
                    s = i * (UNROLL * STEPS) + (u * STEPS + PRE)
                    for kk, k, v in blocks(i, u):
                        if k == STATS_AT:
                            dve.wait_ge(x_added, i * UNROLL + (u + 1))
                        if k in OWN:
                            dve.wait_ge(dve_step, s + OWN[k])
                        if k == BEST_AT:
                            dve.wait_ge(scores_copied, i * UNROLL + (u + 2))
                        if len(BLOCKS[k]) > 1:
                            dve.wait_ge(spread_copied, i * (UNROLL * E) + (u * E + max(e for _, e, _, _ in BLOCKS[k]) + 1))
                            dve.wait_ge(silu_done, kk + 1)
                            mix_part(nc.vector, k, 1).then_inc(own_mixed, 1)
                            dve.wait_ge(own_mixed, i * (UNROLL * PACKED) + (u * PACKED + sum(len(b) > 1 for b in BLOCKS[:k + 1])))
                        dve.wait_ge(mixed, kk + 2)
                        dve.wait_ge(up_ready, kk + 1)
                        nc.vector.tensor_tensor(hid[v % RING][:], gate[k % 2][:], p_up[k % 2][:], ALU.mult).then_inc(hid_ready, 1)
                        lo_of_hid(v - 1, kk + 1)
                        if k == NORM_AT:
                            dve.wait_ge(xt_ready, i * UNROLL + (u + 1))
                            norm(i * (UNROLL * CT) + (u + 1) * CT)
                        if k == XT_AT:
                            lo_of_xt(1 - u, i * UNROLL + (u + 2))
                        if k == BEST_AT - 1:
                            copy_scores(i * UNROLL + (u + 2))
                        if k == BEST_AT:
                            find_best()
                        if k == BEST_AT + 1:
                            find_where()
                        if k == Y_AT:
                            dve.wait_ge(yt_ready, i * UNROLL + (u + 1))
                            at = bass.ds(i * (UNROLL * CT) + u * CT, CT)
                            nc.vector.tensor_tensor(c.x[:, at, :], c.x[:, at, :], p_t[:].rearrange("p (t d) -> p t d", t=CT),
                                                    ALU.add).then_inc(x_added, 1)
                        if k == BEST_AT + 3:
                            mix_of(s)
                        if k == BEST_AT + 5:
                            parts_of_mix(s)
                        if k == STATS_AT:
                            for t in range(CT):
                                step(nc.vector.bn_stats(stats[:, t, :], c.x[:, bass.ds(i * (UNROLL * CT) + (u * CT + t), 1), :][:, 0, :]))
                        if k == STATS_AT + 1:
                            for t in range(CT):
                                step(nc.vector.bn_aggr(moments[:, t, :], stats[:, t, :]))
                        if k == STATS_AT + 2:
                            nc.vector.tensor_copy(c.mv[:, bass.ds(i * (UNROLL * CT) + u * CT, CT), :], moments[:]).then_inc(moved, 1)
            lo_of_hid(UNROLL * KPC - 1, CHUNKS * KPC + 1)
            dve.wait_ge(yt_ready, CHUNKS + 1)
            tail = c.x[:, TILES:TILES + CT, :]
            nc.vector.tensor_tensor(tail, tail, p_t[:].rearrange("p (t d) -> p t d", t=CT), ALU.add).then_inc(x_added, 1)
            if out is None:
                dve.wait_ge(x_added, CHUNKS + 1)
                end = CHUNKS * STEPS + PRE
                for t in range(CT):
                    step(nc.vector.bn_stats(stats[:, t, :], c.x[:, TILES + t, :]))
                for t in range(CT):
                    dve.wait_ge(dve_step, end + t + 1)
                    step(nc.vector.bn_aggr(c.mv[:, TILES + t, :], stats[:, t, :]))

        @block.tensor
        def _(pe):
            def transposes(dst, src, ready):
                for t in range(CT):
                    last = nc.tensor.transpose(dst[:, t * P:(t + 1) * P], src(t), c.ident[:])
                last.then_inc(ready, 1)

            def scores(u, count):
                pe.wait_ge(xt_lo_ready, count)
                for t in range(CT):
                    at = slice(t * P, (t + 1) * P)
                    last = three(p_score[:, t, :], (xt_hi[u][:, at], xt_lo[u][:, at]), (w.wg[0][:], w.wg[1][:]))
                last.then_inc(scores_ready, 1)

            def part(k, n):
                return w.w[0][:, k, n, :], w.w[1][:, k, n, :]

            def spread(e, u):
                nc.tensor.matmul(p_mix[:], w.spread[0][:, e * P:(e + 1) * P], mix_t[u][:],
                                 start=True, stop=True).then_inc(spread_ready, 1)

            def down(k, v, lo_count):
                pe.wait_ge(hid_lo_ready, lo_count)
                three(p_y[:], part(k, 2), (hid_hi[v % RING][:], hid_lo[v % RING][:]),
                      k == 0, k == KPC - 1).then_inc(down_done, 1)

            pe.wait_ge(xn_ready, 1)
            transposes(p_t, lambda t: xn[:, t, :], xt_ready)
            pe.wait_ge(zeroed, 2 * LAG)
            for n in range(2):
                three(p_y[:], part(0, 0), (hid_hi[0][:], hid_lo[0][:]), start=n == 0, stop=False).then_inc(down_done, 1)
            scores(0, 1)
            pe.wait_ge(mix_ready, 1)
            transposes(p_t[0:2 * E], lambda t: mix_parts[:, t, :], mix_t_ready)
            pe.wait_ge(mix_t_copied, 1)
            spread(0, 0)
            with pe.Fori(0, CHUNKS // UNROLL) as i:
                for u in range(UNROLL):
                    for kk, k, v in blocks(i, u):
                        pe.wait_ge(hid_ready, kk + 1)
                        three(p_gate[k % 2][:], part(k, 0), (xt_hi[u][:], xt_lo[u][:])).then_inc(gate_ready, 1)
                        three(p_up[k % 2][:], part(k, 1), (xt_hi[u][:], xt_lo[u][:])).then_inc(up_ready, 1)
                        if k in SPREADS:
                            n = SPREADS[k]
                            if n == E:
                                pe.wait_ge(mix_t_copied, i * UNROLL + (u + 2))
                            pe.wait_ge(spread_copied, i * (UNROLL * E) + (u * E + n))
                            spread(n % E, u if n < E else 1 - u)
                        if k == LAG:
                            pe.wait_ge(y_copied, i * UNROLL + (u + 1))
                        down((k - LAG) % KPC, v - LAG, kk + 1)
                        if k == NORM_T_AT:
                            pe.wait_ge(xn_ready, i * UNROLL + (u + 2))
                            transposes(p_t, lambda t: xn[:, t, :], xt_ready)
                        if k == SCORES_AT:
                            scores(1 - u, i * UNROLL + (u + 2))
                        if k == Y_T_AT:
                            transposes(p_t, lambda t: y_t[:, t * P:(t + 1) * P], yt_ready)
                        if k == MIX_T_AT:
                            pe.wait_ge(x_added, i * UNROLL + (u + 1))
                            pe.wait_ge(mix_ready, i * UNROLL + (u + 2))
                            transposes(p_t[0:2 * E], lambda t: mix_parts[:, t, :], mix_t_ready)
            for n in range(LAG):
                down(KPC - LAG + n, UNROLL * KPC - LAG + n, CHUNKS * KPC + n + 1 if n < 2 else CHUNKS * KPC + 3)
            pe.wait_ge(y_copied, CHUNKS + 1)
            transposes(p_t, lambda t: y_t[:, t * P:(t + 1) * P], yt_ready)


def project_qkv(nc, c, pads, tag):
    AHEAD = 4
    with ExitStack() as ctx:
        def sb(name, shape, dt=F32):
            return ctx.enter_context(nc.sbuf_tensor(f"{tag}_{name}", shape, dt))

        def psum(name, shape):
            return ctx.enter_context(nc.psum_tensor(f"{tag}_{name}", shape, F32))

        def sem(name):
            return c.sem(f"{tag}_{name}")

        xn = [sb(f"xn{u}", [P, TPB, D]) for u in range(2)]
        xnt = [sb(f"xnt{u}", [P, N]) for u in range(2)]
        p_t = psum("p_t", [P, N])
        p_qkv = [psum(f"p_qkv{u}", [P, 512]) for u in range(4)]
        zeroed = sem("zeroed")
        var_ready = sem("var_ready")
        sqrt_done = sem("sqrt_done")
        xn_ready = sem("xn_ready")
        xt_ready = sem("xt_ready")
        xnt_ready = sem("xnt_ready")
        qkv_ready = sem("qkv_ready")
        qkv_stored = sem("qkv_stored")
        block = ctx.enter_context(nc.Block())

        @block.gpsimd
        def _(pool):
            for pad in pads:
                nc.gpsimd.memset(pad[:].bitcast(F32), 0.0).then_inc(zeroed, 1)

        @block.scalar
        def _(act):
            def copy_xt(u, count):
                act.wait_ge(xt_ready, count)
                nc.scalar.activation(xnt[u][:], p_t[:], ACT.Copy).then_inc(xnt_ready, 1)

            act.wait_ge(var_ready, 1)
            nc.scalar.activation(c.rstd[:, PAD:PAD + TILES], c.rstd[:, PAD:PAD + TILES], ACT.Sqrt).then_inc(sqrt_done, 1)
            copy_xt(0, 1)
            with act.Fori(0, B // 2) as i:
                for u in range(2):
                    copy_xt(1 - u, i * 2 + (u + 2))

        @block.vector
        def _(dve):
            def norm(b, u, tiles):
                for t in tiles:
                    at = bass.ds(b * TPB + (PAD + t), 1)
                    last = nc.vector.tensor_scalar(xn[u][:, t, :], c.x[:, at, :][:, 0, :], c.mv[:, at, 0], c.rstd[:, at],
                                                   ALU.subtract, ALU.mult)
                return last

            nc.vector.tensor_scalar(c.rstd[:, PAD:PAD + TILES], c.mv[:, PAD:PAD + TILES, 1], EPS, None, ALU.add).then_inc(var_ready, 1)
            for p_free in p_qkv:
                nc.vector.memset(p_free[:, 0:1], 0.0).then_inc(qkv_stored, 1)
            dve.wait_ge(sqrt_done, 1)
            nc.vector.reciprocal(c.rstd[:, PAD:PAD + TILES], c.rstd[:, PAD:PAD + TILES]).then_inc(var_ready, 1)
            dve.wait_ge(var_ready, 2)
            norm(0, 0, range(TPB)).then_inc(xn_ready, 1)
            with dve.Fori(0, B // 2) as i:
                for u in range(2):
                    b = i * 2 + u
                    for t in range(TPB):
                        dve.wait_ge(qkv_ready, b * TPB + (t + 1))
                        nc.vector.tensor_tensor(c.qkv[:, :, bass.ds(b * GPB + 1, GPB), t, :],
                                                p_qkv[t % 4][:, 0:3 * D].rearrange("p (a g d) -> p a g d", a=3, g=GPB),
                                                c.b_qkv[:].rearrange("p (a g d) -> p a g d", a=3, g=GPB),
                                                ALU.add).then_inc(qkv_stored, 1)
                        if t < AHEAD:
                            each = TPB // AHEAD
                            last = norm(i * 2 + (u + 1), 1 - u, range(t * each, (t + 1) * each))
                            if t == AHEAD - 1:
                                last.then_inc(xn_ready, 1)

        @block.tensor
        def _(pe):
            def transposes(u, count):
                pe.wait_ge(xn_ready, count)
                for t in range(TPB):
                    last = nc.tensor.transpose(p_t[:, t * P:(t + 1) * P], xn[u][:, t, :], c.ident[:])
                last.then_inc(xt_ready, 1)

            transposes(0, 1)
            with pe.Fori(0, B // 2) as i:
                for u in range(2):
                    b = i * 2 + u
                    pe.wait_ge(xnt_ready, b + 1)
                    for t in range(TPB):
                        pe.wait_ge(qkv_stored, b * TPB + (t + 1))
                        nc.tensor.matmul(p_qkv[t % 4][:, 0:3 * D], xnt[u][:, t * P:(t + 1) * P], c.w_qkv[:],
                                         start=True, stop=True).then_inc(qkv_ready, 1)
                        if t == AHEAD + 1:
                            transposes(1 - u, i * 2 + (u + 2))


def softmax_attention(nc, c, q_pad, k_pad, tag):
    SCALE = float(DB) ** -0.5
    HALF = N // 2
    QUADS = 2 * TPB
    NE = 3
    S_TILES = TPB * GH
    LEAD = 4
    TURNS = [("scores_t", 0, 0), ("scores", 0, 0), ("scores", 0, 1), ("scores_t", 1, 0), ("output", 0, 0),
             ("scores_t", 2, 0), ("scores", 1, 0), ("scores", 1, 1), ("scores_t", 3, 0)]
    LAST_TURNS = [("scores_t", h, 0) for h in range(GH)] + [("output", 0, 0)]
    PARTS = sum(kind == "output" for kind, _, _ in TURNS)
    O_AT, Q_AT, K_AT, M_AT = 2, 4, 6, QUADS - 1
    with ExitStack() as ctx:
        def sb(name, shape, dt=F32):
            return ctx.enter_context(nc.sbuf_tensor(f"{tag}_{name}", shape, dt))

        def psum(name, shape):
            return ctx.enter_context(nc.psum_tensor(f"{tag}_{name}", shape, F32))

        def sem(name):
            return c.sem(f"{tag}_{name}")

        q_nat = [sb(f"q_nat{u}", [P, TPB, GH, SR]) for u in range(2)]
        k_nat = sb("k_nat", [P, TPB, GH, SR])
        q_t = sb("q_t", [P, N], F32R)
        k_t = [sb(f"k_t{u}", [P, N], F32R) for u in range(2)]
        qm_t = [sb(f"qm_t{u}", [P, N], F32R) for u in range(2)]
        v_nat = [sb(f"v_nat{u}", [P, TPB, GH, 32]) for u in range(2)]
        row_max = [sb(f"row_max{u}", [P, TPB, GH]) for u in range(2)]
        prob = [sb(f"prob{n}", [P, HALF]) for n in range(2 * GH)]
        o_t = sb("o_t", [P, N])
        o_den = sb("o_den", [P, TPB, GH])
        p_s = [psum(f"p_s{u}", [P, N]) for u in range(2)]
        p_e = [psum(f"p_e{u}", [P, HALF]) for u in range(NE)]
        p_o = psum("p_o", [P, HALF])

        hi_ready = sem("hi_ready")
        stack_ready = sem("stack_ready")
        v_ready = sem("v_ready")
        zeroed = sem("zeroed")
        qt_ready = sem("qt_ready")
        kt_ready = sem("kt_ready")
        qt_copied = sem("qt_copied")
        kt_copied = sem("kt_copied")
        q_pad_in = sem("q_pad_in")
        k_pad_in = sem("k_pad_in")
        s_ready = sem("s_ready")
        max_done = sem("max_done")
        neg_hi = sem("neg_hi")
        m_ready = sem("m_ready")
        qm_ready = sem("qm_ready")
        qm_copied = sem("qm_copied")
        st_ready = sem("st_ready")
        exp_done = sem("exp_done")
        pv_done = sem("pv_done")
        o_copied = sem("o_copied")
        ot_ready = sem("ot_ready")
        den_done = sem("den_done")
        o_done = sem("o_done")
        biased = sem("biased")

        def users(g):
            out = []
            for q in range(QUADS):
                for n in (2 * q, 2 * q + 1):
                    group, tile = (g, n + LEAD) if n + LEAD < S_TILES else (g + 1, n + LEAD - S_TILES)
                    out.append(("s", group, tile) if group < GROUPS else None)
                if q == O_AT:
                    out.append(("o", g - 2, 0) if g >= 1 else None)
                if q == Q_AT:
                    out.append(("q", g + 1, 0) if g + 1 < GROUPS else None)
                if q == K_AT:
                    out.append(("k", g + 1, 0) if g + 1 < GROUPS else None)
                if q == M_AT:
                    out.append(("m", g, 0) if g < GROUPS else None)
            return out

        FIRST = [("q", 0, 0), ("k", 0, 0)] + [("s", 0, n) for n in range(LEAD)]
        ALL = FIRST + [x for g in range(GROUPS + 1) for x in users(g)] + [("o", GROUPS - 1, 0)]
        PLACE = {x: n for n, x in enumerate(ALL) if x is not None}
        FREED = {"s": (max_done, S_TILES, 0), "q": (qt_copied, 1, 0), "k": (kt_copied, 1, 0),
                 "m": (qm_copied, 1, 0), "o": (o_done, 1, 1)}

        def scores_ring(r):
            free = p_s[1 - PLACE[("o", GROUPS - 2, 0)] % 2]
            return [p[:] for p in p_e] + ([free[:, 0:HALF], free[:, HALF:N]] if r == GROUPS else [])

        def count(group, shift, per, k):
            return group * per + (shift * per + k + 1)

        block = ctx.enter_context(nc.Block())

        def steps(eng, body):
            body(0, 0)
            with eng.Fori(0, (GROUPS - 2) // 2) as i:
                for u in range(2):
                    body(i * 2 + (1 + u), 3 + u)
            body(GROUPS - 1, GROUPS - 1)
            body(GROUPS, GROUPS)


        @block.sync
        def _(sp):
            def pads(dst, src, done):
                for h in range(GH):
                    rows = slice(SR * h, SR * (h + 1))
                    sp.dma_start(dst[rows, h, :].bitcast(F32), src[rows, :].bitcast(F32)).then_inc(done, 16)

            def step(g, r):
                if r < GROUPS:
                    sp.wait_ge(v_ready, count(g, 0, 1, 0))
                    sp.wait_ge(kt_copied, count(g, 0, 1, 0))
                    pads(k_pad[r % 2], k_t[r % 2], k_pad_in)
                if r + 1 < GROUPS:
                    sp.wait_ge(qt_copied, count(g, 1, 1, 0))
                    pads(q_pad[(r + 1) % 2], q_t, q_pad_in)

            sp.wait_ge(qt_copied, 1)
            pads(q_pad[0], q_t, q_pad_in)
            steps(sp, step)

        @block.gpsimd
        def _(pool):
            def stack(g, r):
                u = r % 2
                q = c.qkv[:, 0, bass.ds(g + 1, 1), :, :][:, 0].rearrange("p t (h d) -> p t h d", h=GH)
                k = c.qkv[:, 1, bass.ds(g + 1, 1), :, :][:, 0].rearrange("p t (h d) -> p t h d", h=GH)
                pool.wait_ge(hi_ready, count(g, 0, 2, 0))
                nc.gpsimd.tensor_tensor(q_nat[u][:, :, :, DB:2 * DB], q, q_nat[u][:, :, :, 0:DB], ALU.subtract)
                nc.gpsimd.tensor_copy(q_nat[u][:, :, :, 2 * DB:3 * DB], q_nat[u][:, :, :, 0:DB])
                nc.gpsimd.memset(q_nat[u][:, :, :, 3 * DB:3 * DB + 2], 0.0).then_inc(stack_ready, 1)
                pool.wait_ge(hi_ready, count(g, 0, 2, 1))
                nc.gpsimd.tensor_tensor(k_nat[:, :, :, 2 * DB:3 * DB], k, k_nat[:, :, :, 0:DB], ALU.subtract)
                nc.gpsimd.tensor_copy(k_nat[:, :, :, DB:2 * DB], k_nat[:, :, :, 0:DB]).then_inc(stack_ready, 1)

            def values(g, r):
                v = c.qkv[:, 2, bass.ds(g + 1, 1), :, :][:, 0].rearrange("p t (h d) -> p t h d", h=GH)
                nc.gpsimd.tensor_copy(v_nat[r % 2][:, :, :, 0:DB], v).then_inc(v_ready, 1)

            def step(g, r):
                if r + 1 < GROUPS:
                    stack(g + 1, r + 1)
                elif r < GROUPS:
                    pool.wait_ge(pv_done, count(g, -2, QUADS, QUADS - 1))
                if r < GROUPS:
                    values(g, r)

            for u in range(2):
                nc.gpsimd.memset(q_nat[u][:, :, :, 3 * DB:], 0.0)
                nc.gpsimd.memset(v_nat[u][:, :, :, DB:], 0.0).then_inc(zeroed, 1)
            nc.gpsimd.memset(k_nat[:, :, :, 3 * DB:], 0.0).then_inc(zeroed, 1)
            pool.wait_ge(zeroed, 3)
            for u in range(2):
                nc.gpsimd.memset(v_nat[u][:, :, :, DB:DB + 1], 1.0)
            nc.gpsimd.memset(k_nat[:, :, :, 3 * DB:3 * DB + 2], 1.0)
            stack(0, 0)
            steps(pool, step)
            x = c.x[:, PAD:PAD + TILES, :]
            nc.gpsimd.tensor_tensor(x, x, c.b_o[:].unsqueeze(1).broadcast_to([P, TILES, D]), ALU.add).then_inc(biased, 1)

        @block.scalar
        def _(act):
            def his(g, r):
                for n, dst in enumerate((q_nat[r % 2], k_nat)):
                    src = c.qkv[:, n, bass.ds(g + 1, 1), :, :][:, 0].rearrange("p t (h d) -> p t h d", h=GH)
                    nc.scalar.activation(dst[:, :, :, 0:DB].bitcast(F32R), src, ACT.Copy).then_inc(hi_ready, 1)

            def place(x):
                return p_s[PLACE[x] % 2]

            def q_copy(g, r):
                act.wait_ge(qt_ready, count(g, 0, 1, 0))
                if r > 0:
                    act.wait_ge(q_pad_in, count(g, -1, 64, 63))
                nc.scalar.activation(q_t[:], place(("q", r, 0))[:], ACT.Copy).then_inc(qt_copied, 1)

            def k_copy(g, r):
                act.wait_ge(kt_ready, count(g, 0, 1, 0))
                nc.scalar.activation(k_t[r % 2][:], place(("k", r, 0))[:], ACT.Copy).then_inc(kt_copied, 1)

            def copy_o(g, half):
                act.wait_ge(pv_done, count(g, -1, QUADS, (half + 1) * TPB - 1))
                nc.scalar.activation(o_t[:, half * HALF:(half + 1) * HALF], p_o[:], ACT.Copy).then_inc(o_copied, 1)

            def step(g, r):
                for q in range(QUADS):
                    for h in range(GH):
                        if r > 0:
                            e = 4 * q + h
                            act.wait_ge(st_ready, count(g, -1, 4 * QUADS, e))
                            nc.scalar.activation(prob[(q % 2) * GH + h][:], scores_ring(r)[e % len(scores_ring(r))], ACT.Exp,
                                                 scale=SCALE).then_inc(exp_done, 1)
                        if r > 0 and q == TPB and h == 1:
                            copy_o(g, 0)
                        if h == 0 and r + 1 < GROUPS:
                            if q == 1:
                                if r == 0:
                                    act.wait_ge(kt_ready, 1)
                                his(g + 1, r + 1)
                            if q == Q_AT + 1:
                                q_copy(g + 1, r + 1)
                            if q == K_AT + 1:
                                k_copy(g + 1, r + 1)
                if r < GROUPS:
                    act.wait_ge(qm_ready, count(g, 0, 1, 0))
                    nc.scalar.activation(qm_t[r % 2][:], place(("m", r, 0))[:], ACT.Copy).then_inc(qm_copied, 1)
                if r > 0:
                    copy_o(g, 1)

            act.wait_ge(zeroed, 3)
            nc.scalar.activation(prob[0][:, 0:GH], c.ident[:, 0:GH], ACT.Exp)
            his(0, 0)
            q_copy(0, 0)
            k_copy(0, 0)
            steps(act, step)

        @block.vector
        def _(dve):
            def tile_max(group, shift, r, n):
                dve.wait_ge(s_ready, count(group, shift, S_TILES, n))
                nc.vector.reduce_max(row_max[(r + shift) % 2][:, n // GH, n % GH:n % GH + 1],
                                     p_s[PLACE[("s", r + shift, n)] % 2][:], AX_X).then_inc(max_done, 1)

            def normalize(g, r):
                src = p_s[PLACE[("o", r, 0)] % 2][:].rearrange("p (t h s) -> p t h s", t=TPB, h=GH)
                dve.wait_ge(ot_ready, count(g, 1, 1, 0))
                nc.vector.reciprocal(o_den[:], src[:, :, :, DB]).then_inc(den_done, 1)
                dve.wait_ge(den_done, count(g, 1, 1, 0))
                nc.vector.tensor_tensor(c.qkv[:, 0, bass.ds(g + 1, 1), :, :][:, 0].rearrange("p t (h d) -> p t h d", h=GH),
                                        src[:, :, :, 0:DB], o_den[:].unsqueeze(3).broadcast_to([P, TPB, GH, DB]),
                                        ALU.mult).then_inc(o_done, 1)

            def step(g, r):
                u = r % 2
                for q in range(QUADS):
                    for n in (2 * q, 2 * q + 1):
                        if n + LEAD < S_TILES:
                            if r < GROUPS:
                                tile_max(g, 0, r, n + LEAD)
                        elif r + 1 < GROUPS:
                            tile_max(g, 1, r, n + LEAD - S_TILES)
                        if n + LEAD == S_TILES - 1 and r < GROUPS:
                            dve.wait_ge(max_done, count(g, 0, S_TILES, S_TILES - 1))
                            nc.vector.tensor_scalar(q_nat[u][:, :, :, 3 * DB].bitcast(F32R), row_max[u][:], -1.0, None,
                                                    ALU.mult).then_inc(neg_hi, 1)
                            dve.wait_ge(neg_hi, count(g, 0, 1, 0))
                            nc.vector.scalar_tensor_tensor(
                                out=q_nat[u][:, :, :, 3 * DB + 1].bitcast(F32R), in0=row_max[u][:], scalar=-1.0,
                                in1=q_nat[u][:, :, :, 3 * DB], op0=ALU.mult, op1=ALU.subtract).then_inc(m_ready, 1)
                    if q == O_AT and r > 0:
                        normalize(g - 2, r - 2)

            for half in range(2):
                nc.vector.memset(o_t[:, half * HALF:(half + 1) * HALF], 1.0).then_inc(o_copied, 1)
            for n in range(LEAD):
                tile_max(0, 0, 0, n)
            steps(dve, step)
            normalize(GROUPS - 1, GROUPS - 1)

        @block.tensor
        def _(pe):
            def place(group, shift, x):
                n = PLACE[x]
                before = [m for m in range(n % 2, n, 2) if ALL[m] is not None]
                if before:
                    kind, at, k = ALL[before[-1]]
                    freed, per, late = FREED[kind]
                    pe.wait_ge(freed, count(group, at - (x[1] - shift) + late, per, k))
                return p_s[n % 2]

            def transposes(dst, src, ready):
                for t in range(TPB):
                    last = nc.tensor.transpose(dst[:, t * P:(t + 1) * P], src(t), c.ident[:])
                last.then_inc(ready, 1)

            def scores(g, r, shift, n, half):
                u, t, h = (r + shift) % 2, n // GH, n % GH
                x = ("s", r + shift, n)
                if n == 0 and half == 0:
                    pe.wait_ge(q_pad_in, count(g, shift, 64, 63))
                    pe.wait_ge(kt_copied, count(g, shift, 1, 0))
                dst = place(g, shift, x) if half == 0 else p_s[PLACE[x] % 2]
                ins = nc.tensor.matmul(dst[:, half * HALF:(half + 1) * HALF], q_pad[u][:, h, t * P:(t + 1) * P],
                                       k_t[u][:, half * HALF:(half + 1) * HALF], start=True, stop=True)
                if half == 1:
                    ins.then_inc(s_ready, 1)

            def scores_t(g, r, q, h):
                u, e, blk, half = (r - 1) % 2, 4 * q + h, q % TPB, q // TPB
                if e == 0:
                    pe.wait_ge(qm_copied, count(g, -1, 1, 0))
                    pe.wait_ge(k_pad_in, count(g, -1, 64, 63))
                ring = scores_ring(r)
                if e >= len(ring):
                    pe.wait_ge(exp_done, count(g, -1, 4 * QUADS, e - len(ring)))
                nc.tensor.matmul(ring[e % len(ring)], k_pad[u][:, h, blk * P:(blk + 1) * P],
                                 qm_t[u][:, half * HALF:(half + 1) * HALF], start=True, stop=True).then_inc(st_ready, 1)

            def output(g, r, q, part):
                u, blk = (r - 1) % 2, q % TPB
                if part == 0:
                    if q == 0:
                        pe.wait_ge(v_ready, count(g, -1, 1, 0))
                        pe.wait_ge(o_copied, count(g, -1, 2, 1))
                    if q == TPB:
                        pe.wait_ge(o_copied, count(g, 0, 2, 0))
                    pe.wait_ge(exp_done, count(g, -1, 4 * QUADS, 4 * q + 3))
                cols = HALF // PARTS
                for h in range(GH):
                    last = nc.tensor.matmul(p_o[32 * h:32 * (h + 1), part * cols:(part + 1) * cols],
                                            v_nat[u][:, blk, h, :], prob[(q % 2) * GH + h][:, part * cols:(part + 1) * cols],
                                            start=blk == 0 and part == 0, stop=blk == TPB - 1,
                                            skip_group_check=PARTS > 1)
                if part == PARTS - 1:
                    last.then_inc(pv_done, 1)

            def stack_t(g, r, shift, kind, src, stacked, ready):
                pe.wait_ge(stack_ready, count(g, shift, 2, stacked))
                transposes(place(g, shift, (kind, r + shift, 0)), src, ready)

            def step(g, r):
                for q in range(QUADS):
                    for kind, n, half in TURNS if r < GROUPS else LAST_TURNS:
                        if kind == "scores_t" and r > 0:
                            scores_t(g, r, q, n)
                        if kind == "scores":
                            tile = 2 * q + n + LEAD
                            if tile < S_TILES:
                                if r < GROUPS:
                                    scores(g, r, 0, tile, half)
                            elif r + 1 < GROUPS:
                                scores(g, r, 1, tile - S_TILES, half)
                        if kind == "output" and r > 0 and q >= 1:
                            output(g, r, q - 1, half)
                    if q == O_AT and r > 0:
                        pe.wait_ge(o_copied, count(g, -1, 2, 1))
                        transposes(place(g, -2, ("o", r - 2, 0)), lambda t: o_t[:, t * P:(t + 1) * P], ot_ready)
                    if q == Q_AT and r + 1 < GROUPS:
                        stack_t(g, r, 1, "q", lambda t: q_nat[(r + 1) % 2][:, t], 0, qt_ready)
                    if q == K_AT and r + 1 < GROUPS:
                        stack_t(g, r, 1, "k", lambda t: k_nat[:, t], 1, kt_ready)
                    if q == M_AT and r < GROUPS:
                        pe.wait_ge(m_ready, count(g, 0, 1, 0))
                        transposes(place(g, 0, ("m", r, 0)), lambda t: q_nat[r % 2][:, t], qm_ready)
                if r > 0:
                    for part in range(PARTS):
                        output(g, r, QUADS - 1, part)

            stack_t(0, 0, 0, "q", lambda t: q_nat[0][:, t], 0, qt_ready)
            stack_t(0, 0, 0, "k", lambda t: k_nat[:, t], 1, kt_ready)
            for n in range(LEAD):
                scores(0, 0, 0, n, 0)
                scores(0, 0, 0, n, 1)
            steps(pe, step)
            pe.wait_ge(o_copied, 2 * GROUPS + 2)
            transposes(place(GROUPS - 1, 0, ("o", GROUPS - 1, 0)), lambda t: o_t[:, t * P:(t + 1) * P], ot_ready)


def project_out(nc, c, io, tag, weights):
    OWN, SHARED = 5, 6
    with ExitStack() as ctx:
        def sb(name, shape, dt=F32):
            return ctx.enter_context(nc.sbuf_tensor(f"{tag}_{name}", shape, dt))

        def psum(name, shape):
            return ctx.enter_context(nc.psum_tensor(f"{tag}_{name}", shape, F32))

        def sem(name):
            return c.sem(f"{tag}_{name}")

        o = [sb(f"o{u}", [P, TPB, D]) for u in range(2)]
        o_t = [sb(f"o_t{u}", [P, N]) for u in range(2)]
        stats = sb("stats", [P, TPB, 6])
        moments = sb("moments", [P, TPB, 2])
        p_t = [psum(f"p_t{u}", [P, N]) for u in range(2)]
        p_y = [psum(f"p_y{u}", [P, TPB, D]) for u in range(2)]
        gathered = sem("gathered")
        t_ready = sem("t_ready")
        t_copied = sem("t_copied")
        y_ready = sem("y_ready")
        x_added = sem("x_added")
        counted = sem("counted")
        moved = sem("moved")
        weights.begin(ctx)
        block = ctx.enter_context(nc.Block())

        @block.sync
        def _(sp):
            weights.load(sp, io)

        @block.gpsimd
        def _(pool):
            weights.split(pool, slice(0, OWN))
            weights.split_lo(pool, nc.gpsimd, slice(OWN, OWN + SHARED), 0, weights.lo_done)

        @block.scalar
        def _(act):
            with act.Fori(0, B // 2) as i:
                for u in range(2):
                    b = i * 2 + u
                    nc.scalar.activation(o[u][:].rearrange("p t (g d) -> p g t d", g=GPB),
                                         c.qkv[:, 0, bass.ds(b * GPB + 1, GPB), :, :], ACT.Copy).then_inc(gathered, 1)
                for u in range(2):
                    act.wait_ge(t_ready, i * 2 + (u + 1))
                    nc.scalar.activation(o_t[u][:], p_t[u][:], ACT.Copy).then_inc(t_copied, 1)
            weights.split_hi(act, slice(OWN, None))

        @block.vector
        def _(dve):
            with dve.Fori(0, B // 2) as i:
                for u in range(2):
                    b = i * 2 + u
                    dve.wait_ge(y_ready, b + 1)
                    nc.vector.tensor_tensor(residual_tiles(c.x, b * TPB, TPB), residual_tiles(c.x, b * TPB, TPB),
                                            p_y[u][:], ALU.add).then_inc(x_added, 1)
                    nc.vector.drain()
                    for t in range(TPB):
                        nc.vector.bn_stats(stats[:, t, :], residual_tiles(c.x, b * TPB + t, 1)[:, 0, :]).then_inc(counted, 1)
                    nc.vector.drain()
                    for t in range(TPB):
                        nc.vector.bn_aggr(moments[:, t, :], stats[:, t, :]).then_inc(counted, 1)
                    nc.vector.drain()
                    nc.vector.tensor_copy(c.mv[:, bass.ds(b * TPB + PAD, TPB), :], moments[:]).then_inc(moved, 1)
                    dve.wait_ge(moved, b + 1)
            weights.split_lo(dve, nc.vector, slice(OWN + SHARED, None), SHARED, weights.dve_lo_done)

        @block.tensor
        def _(pe):
            with pe.Fori(0, B // 2) as i:
                for u in range(2):
                    pe.wait_ge(gathered, i * 2 + (u + 1))
                    for t in range(TPB):
                        last = nc.tensor.transpose(p_t[u][:, t * P:(t + 1) * P], o[u][:, t, :], c.ident[:])
                    last.then_inc(t_ready, 1)
                for u in range(2):
                    pe.wait_ge(t_copied, i * 2 + (u + 1))
                    for t in range(TPB):
                        last = nc.tensor.matmul(p_y[u][:, t, :], o_t[u][:, t * P:(t + 1) * P], c.w_o[:], start=True, stop=True)
                    last.then_inc(y_ready, 1)
                for u in range(2):
                    pe.wait_ge(x_added, i * 2 + (u + 1))


def program(nc, io, out):
    with ExitStack() as ctx:
        c = Chip(nc, ctx)
        c.x = c.sb("x", [P, PAD + TILES + TAIL, D])
        c.mv = c.sb("mean_var", [P, PAD + TILES + TAIL, 2])
        c.rstd = c.sb("rstd", [P, PAD + TILES + TAIL])
        c.ident = c.sb("ident", [P, P])
        c.iota = c.sb("iota", [P, E])
        c.w_qkv = c.sb("w_qkv", [P, 3 * D])
        c.b_qkv = c.sb("b_qkv", [P, 3 * D])
        c.w_o = c.sb("w_o", [P, D])
        c.b_o = c.sb("b_o", [P, D])

        with ExitStack() as first:
            weights = ExpertWeights(nc, c, first, "w1")
            attention_a(nc, c, io, weights)
            feed_forward(nc, c, weights, "f1")
        c.qkv = c.sb("qkv", [P, 3, GROUPS + 1, TPB, GC])
        with ExitStack() as middle:
            q_pad, k_pad = [[middle.enter_context(nc.sbuf_tensor(f"{n}_pad{u}", [P, GH, N], F32R))
                             for u in range(2)] for n in "qk"]
            project_qkv(nc, c, q_pad + k_pad, "q")
            softmax_attention(nc, c, q_pad, k_pad, "s")
        weights = ExpertWeights(nc, c, ctx, "w2")
        project_out(nc, c, io, "o", weights)
        feed_forward(nc, c, weights, "f2", out)


def layouts(a):
    import numpy as np

    g = {k: np.asarray(v) for k, v in a.items()}
    w_qkv, b_qkv = g["L0_attn_a_w_qkv"], g["L0_attn_a_b_qkv"]
    wo_a = g["L0_attn_a_w_o"].T.reshape(NA, D // NA, D).transpose(1, 0, 2).reshape(D, D)
    w_ffn = np.zeros((P, KPC, 3, P), np.float32)
    spread = np.tile(np.repeat(np.eye(E, dtype=np.float32), P, axis=1), (2, 1))
    for k, parts in enumerate(BLOCKS):
        for row, e, first, count in parts:
            rows, units = slice(row, row + count), slice(first, first + count)
            w_ffn[:, k, 0, rows] = g["L0_ffn_W1"][e, units].T
            w_ffn[:, k, 1, rows] = g["L0_ffn_W2"][e, units].T
            w_ffn[rows, k, 2, :] = g["L0_ffn_W3"][e][:, units].T
    io = {
        "x": g["L0_attn_a_x"],
        "wkv_a": w_qkv[D:].T, "wq_a": w_qkv[:D], "wo_a": wo_a,
        "bkv_a": np.broadcast_to(b_qkv[D:], (P, 2 * D)), "bq_a": np.broadcast_to(b_qkv[:D, None], (D, P)),
        "bo_a": np.broadcast_to(g["L0_attn_a_b_o"], (P, D)),
        "head_mask": (np.arange(P)[:, None] % NA == np.arange(P)[None, :] % NA).astype(np.float32),
        "ident": np.eye(P, dtype=np.float32),
        "w_b": np.concatenate([g[f"L0_attn_b_W{n}"] for n in "qkv"], 1),
        "b_b": np.broadcast_to(np.concatenate([g[f"L0_attn_b_b{n}"] for n in "qkv"]), (P, 3 * D)),
        "wo_b": g["L0_attn_b_Wo"], "bo_b": np.broadcast_to(g["L0_attn_b_bo"], (P, D)),
        "wg": g["L0_ffn_Wg"].T,
        "w_ffn": w_ffn, "spread": spread,
        "iota": np.broadcast_to(np.arange(E, dtype=np.float32), (P, E)),
    }
    return {k: np.ascontiguousarray(v) for k, v in io.items()}


def kernel(**inputs):
    import concourse.bacc as bacc
    from concourse.bass_utils import run_bass_kernel_spmd

    arrays = layouts(inputs)
    nc = bacc.Bacc("TRN2", target_bir_lowering=False, num_devices=1)
    io = {k: nc.dram_tensor(f"in_{k}", v.shape, F32, kind="ExternalInput").ap() for k, v in arrays.items()}
    out = nc.dram_tensor("out", (B, N, D), F32, kind="ExternalOutput").ap()
    program(nc, io, out)
    r = run_bass_kernel_spmd(nc, [{f"in_{k}": v for k, v in arrays.items()}], core_ids=[0])
    return r.results[0]["out"]
```

```python
from contextlib import ExitStack

import concourse.bass as bass
from concourse import mybir

F32 = mybir.dt.float32
F32R = mybir.dt.float32r
U32 = mybir.dt.uint32
ALU = mybir.AluOpType
ACT = mybir.ActivationFunctionType
AX_X = mybir.AxisListType.X

P = 128
B, N, D = 4, 1024, 128
TPB = N // P
TILES = B * TPB
E, HID, TOP = 8, 352, 2
NA = 8
NB, DB = 16, 8
EPS = 1e-5
CT = 4
CHUNK = CT * P
CHUNKS = TILES // CT
PAD, TAIL = CT, TPB
WHOLE = HID // P
REST = HID - WHOLE * P


def packed(n):
    parts, row = [], 0
    for e in range(E):
        lo, hi = max(e * REST, n * P), min((e + 1) * REST, (n + 1) * P)
        if lo < hi:
            parts.append((e, WHOLE * P + lo - e * REST, hi - lo))
    placed = []
    for e, first, count in sorted(parts, key=lambda part: -part[2]):
        placed.append((row, e, first, count))
        row += count
    return placed


BLOCKS = []
for e in range(E):
    BLOCKS += [[(0, e, j * P, P)] for j in range(WHOLE)]
    BLOCKS += [packed(n) for n in range(E * REST // P) if ((n + 1) * P - 1) // REST == e]
assert E * REST % P == 0
KPC = len(BLOCKS)
PACKED = sum(len(block) > 1 for block in BLOCKS)
GH = 4
GPB = NB // GH
GROUPS = B * GPB
SR = P // GH
GC = GH * DB


class Chip:

    def __init__(self, nc, ctx):
        self.nc, self.ctx = nc, ctx

    def sb(self, name, shape, dt=F32):
        return self.ctx.enter_context(self.nc.sbuf_tensor(name, shape, dt))

    def sem(self, name):
        return self.ctx.enter_context(self.nc.semaphore(name))


def residual_tiles(x, first, count):
    return x[:, bass.ds(first + PAD, count), :]


def attention_a(nc, c, io, weights):
    PAIR = 2 * TPB
    with ExitStack() as ctx:
        def sb(name, shape, dt=F32):
            return ctx.enter_context(nc.sbuf_tensor(name, shape, dt))

        def psum(name, shape):
            return ctx.enter_context(nc.psum_tensor(name, shape, F32))

        wkv = sb("a_wkv", [P, 2 * D])
        wq = sb("a_wq", [P, D])
        wo = sb("a_wo", [P, D])
        bkv = sb("a_bkv", [P, 2 * D])
        bq = sb("a_bq", [P, P])
        bo = sb("a_bo", [P, D])
        mask = sb("a_mask", [P, P])
        xn = [sb(f"a_xn{u}", [P, TPB, D]) for u in range(2)]
        xnt = [sb(f"a_xnt{u}", [P, N]) for u in range(2)]
        kv = [sb(f"a_kv{n}", [P, 2 * D]) for n in range(4)]
        vk = [sb(f"a_vk{u}", [P, P]) for u in range(2)]
        vk_wo = [sb(f"a_vk_wo{u}", [P, D]) for u in range(2)]
        fold = [sb(f"a_fold{u}", [P, D]) for u in range(2)]
        bias = [sb(f"a_bias{u}", [P, D]) for u in range(2)]
        stats = sb("a_stats", [P, PAIR, 6])
        moments = sb("a_moments", [P, PAIR, 2])
        rstd = sb("a_rstd", [P, PAIR])
        p_big = [psum(f"a_p_big{u}", [P, TPB, D]) for u in range(2)]
        p_kv = [psum(f"a_p_kv{n}", [P, 512]) for n in range(2)]
        p_fold = [psum(f"a_p_fold{u}", [P, 4, D]) for u in range(2)]

        x_in = [c.sem(f"a_x_in{n}") for n in range(2)]
        w_in = c.sem("a_w_in")
        dve_step = c.sem("a_dve_step")
        var_ready = c.sem("a_var_ready")
        sqrt_done = c.sem("a_sqrt_done")
        xn_ready = c.sem("a_xn_ready")
        xt_ready = c.sem("a_xt_ready")
        xnt_ready = c.sem("a_xnt_ready")
        kv_ready = c.sem("a_kv_ready")
        kv_copied = c.sem("a_kv_copied")
        vk_ready = c.sem("a_vk_ready")
        vk_masked = c.sem("a_vk_masked")
        vkwo_ready = c.sem("a_vkwo_ready")
        vkwo_copied = c.sem("a_vkwo_copied")
        fold_ready = c.sem("a_fold_ready")
        fold_copied = c.sem("a_fold_copied")
        bias_copied = c.sem("a_bias_copied")
        y_ready = c.sem("a_y_ready")

        loads = [(c.ident, io["ident"]), (wkv, io["wkv_a"]), (bkv, io["bkv_a"]), (mask, io["head_mask"]),
                 (wo, io["wo_a"]), (wq, io["wq_a"]), (bq, io["bq_a"]), (bo, io["bo_a"]), (c.iota, io["iota"])]
        later = [(c.w_qkv, io["w_b"]), (c.b_qk, io["bqk_b"]), (c.b_v, io["bv_b"]), (c.w_o, io["wo_b"]), (c.b_o, io["bo_b"])]
        later_in = c.sem("a_later_in")
        raw = RawWeights(nc, c, ctx, "w1")
        weights.take(raw)
        block = ctx.enter_context(nc.Block())

        @block.sync
        def _(sp):
            for b in range(B):
                sp.dma_start(c.x[:, PAD + b * TPB:PAD + (b + 1) * TPB, :],
                             io["x"][b].rearrange("(p j) d -> p j d", p=P)).then_inc(x_in[b // 2], 16)
            raw.load(sp, io)
            for dst, src in later:
                sp.dma_start(dst[:], src).then_inc(later_in, 16)
            sp.wait_ge(later_in, 16 * len(later))

        @block.gpsimd
        def _(pool):
            weights.split(pool, slice(None))

        @block.scalar
        def _(act):
            for dst, src in loads:
                act.dma_start(dst[:], src).then_inc(w_in, 16)
            with act.Fori(0, B // 2) as i:
                act.wait_ge(var_ready, i + 1)
                nc.scalar.activation(rstd[:], rstd[:], ACT.Sqrt).then_inc(sqrt_done, 1)
                for u in range(2):
                    act.wait_ge(xt_ready, i * 2 + (u + 1))
                    nc.scalar.activation(xnt[u][:], p_big[u][:].rearrange("p t d -> p (t d)"), ACT.Copy).then_inc(xnt_ready, 1)
                for u in range(2):
                    act.wait_ge(vkwo_ready, i * 2 + (u + 1))
                    nc.scalar.activation(vk_wo[u][:], p_fold[u][:, 1], ACT.Copy).then_inc(vkwo_copied, 1)
                    act.wait_ge(fold_ready, i * 2 + (u + 1))
                    nc.scalar.activation(fold[u][:], p_fold[u][:, 2], ACT.Copy).then_inc(fold_copied, 1)

        @block.vector
        def _(dve):
            def mask_vk(i, u):
                dve.wait_ge(vk_ready, i * PAIR + (u + 1) * TPB)
                nc.vector.tensor_tensor(vk[u][:], p_fold[u][:, 0], mask[:], ALU.mult).then_inc(vk_masked, 1)

            def bias_of(i, u):
                dve.wait_ge(fold_ready, i * 2 + (u + 1))
                dve.wait_ge(fold_copied, i * 2 + (u + 1))
                nc.vector.tensor_tensor(bias[u][:], p_fold[u][:, 3], bo[:], ALU.add).then_inc(bias_copied, 1)

            nc.vector.memset(c.mv[:], 0.0)
            nc.vector.memset(c.rstd[:], 1.0)
            nc.vector.memset(c.x[:, 0:PAD, :], 0.0)
            nc.vector.memset(c.x[:, PAD + TILES:, :], 0.0)
            dve.wait_ge(x_in[0], 32)
            with dve.Fori(0, B // 2) as i:
                for t in range(PAIR):
                    nc.vector.bn_stats(stats[:, t, :], residual_tiles(c.x, i * PAIR + t, 1)[:, 0, :]).then_inc(dve_step, 1)
                nc.vector.drain()
                for t in range(PAIR):
                    nc.vector.bn_aggr(moments[:, t, :], stats[:, t, :]).then_inc(dve_step, 1)
                nc.vector.drain()
                nc.vector.tensor_scalar(rstd[:], moments[:, :, 1], EPS, None, ALU.add).then_inc(var_ready, 1)
                dve.wait_ge(sqrt_done, i + 1)
                nc.vector.reciprocal(rstd[:], rstd[:]).then_inc(dve_step, 1)
                nc.vector.drain()
                for u in range(2):
                    for t in range(TPB):
                        at = slice(u * TPB + t, u * TPB + t + 1)
                        last = nc.vector.tensor_scalar(xn[u][:, t, :], residual_tiles(c.x, i * PAIR + (u * TPB + t), 1)[:, 0, :],
                                                       moments[:, at, 0], rstd[:, at], ALU.subtract, ALU.mult)
                    last.then_inc(xn_ready, 1)
                dve.wait_ge(w_in, 16 * len(loads))
                for n in range(PAIR):
                    dve.wait_ge(kv_ready, i * PAIR + (n + 1))
                    if n >= 4:
                        dve.wait_ge(vk_ready, i * PAIR + (n - 3))
                    nc.vector.tensor_tensor(kv[n % 4][:], p_kv[n % 2][:, 0:2 * D], bkv[:], ALU.add).then_inc(kv_copied, 1)
                    if n == TPB + 1:
                        mask_vk(i, 0)
                mask_vk(i, 1)
                for u in range(2):
                    bias_of(i, u)
                    nc.vector.drain()
                    tiles = residual_tiles(c.x, i * PAIR + u * TPB, TPB)
                    nc.vector.tensor_tensor(tiles, tiles, bias[u][:].unsqueeze(1).broadcast_to([P, TPB, D]),
                                            ALU.add).then_inc(dve_step, 1)
                nc.vector.drain()
                for u in range(2):
                    tiles = residual_tiles(c.x, i * PAIR + u * TPB, TPB)
                    dve.wait_ge(y_ready, i * 2 + (u + 1))
                    nc.vector.tensor_tensor(tiles, tiles, p_big[u][:], ALU.add).then_inc(dve_step, 1)
                    nc.vector.drain()
                    for t in range(TPB):
                        nc.vector.bn_stats(stats[:, u * TPB + t, :], residual_tiles(c.x, i * PAIR + (u * TPB + t), 1)[:, 0, :]).then_inc(dve_step, 1)
                nc.vector.drain()
                for t in range(PAIR):
                    nc.vector.bn_aggr(moments[:, t, :], stats[:, t, :]).then_inc(dve_step, 1)
                nc.vector.drain()
                nc.vector.tensor_copy(c.mv[:, bass.ds(i * PAIR + PAD, PAIR), :], moments[:]).then_inc(dve_step, 1)
                nc.vector.drain()
                dve.wait_ge(x_in[1], 32)

        @block.tensor
        def _(pe):
            def vk_wo_of(i, u):
                pe.wait_ge(vk_masked, i * 2 + (u + 1))
                nc.tensor.matmul(p_fold[u][:, 1], vk[u][:], wo[:], start=True, stop=True).then_inc(vkwo_ready, 1)

            def fold_of(i, u):
                pe.wait_ge(vkwo_copied, i * 2 + (u + 1))
                nc.tensor.matmul(p_fold[u][:, 2], wq[:], vk_wo[u][:], start=True, stop=True)
                nc.tensor.matmul(p_fold[u][:, 3], bq[:], vk_wo[u][:], start=True, stop=True).then_inc(fold_ready, 1)

            def vk_of(i, n):
                u, t = n // TPB, n % TPB
                pe.wait_ge(kv_copied, i * PAIR + (n + 1))
                nc.tensor.matmul(p_fold[u][:, 0], kv[n % 4][:, D:2 * D], kv[n % 4][:, 0:D],
                                 start=t == 0, stop=t == TPB - 1).then_inc(vk_ready, 1)

            def output(i, u, tiles):
                for t in tiles:
                    last = nc.tensor.matmul(p_big[u][:, t, :], xnt[u][:, t * P:(t + 1) * P], fold[u][:], start=True, stop=True)
                return last

            pe.wait_ge(w_in, 16 * len(loads))
            with pe.Fori(0, B // 2) as i:
                for u in range(2):
                    pe.wait_ge(xn_ready, i * 2 + (u + 1))
                    for t in range(TPB):
                        last = nc.tensor.transpose(p_big[u][:, t, :], xn[u][:, t, :], c.ident[:])
                    last.then_inc(xt_ready, 1)
                for n in range(PAIR):
                    u, t = n // TPB, n % TPB
                    if t == 0:
                        pe.wait_ge(xnt_ready, i * 2 + (u + 1))
                    if n >= 2:
                        pe.wait_ge(kv_copied, i * PAIR + (n - 1))
                    nc.tensor.matmul(p_kv[n % 2][:, 0:2 * D], xnt[u][:, t * P:(t + 1) * P], wkv[:],
                                     start=True, stop=True).then_inc(kv_ready, 1)
                    if n >= 1:
                        vk_of(i, n - 1)
                    if n == TPB + 3:
                        vk_wo_of(i, 0)
                    if n == TPB + 6:
                        fold_of(i, 0)
                vk_of(i, PAIR - 1)
                pe.wait_ge(fold_copied, i * 2 + 1)
                output(i, 0, range(0, 3))
                vk_wo_of(i, 1)
                output(i, 0, range(3, 6))
                fold_of(i, 1)
                output(i, 0, range(6, TPB)).then_inc(y_ready, 1)
                pe.wait_ge(fold_copied, i * 2 + 2)
                output(i, 1, range(TPB)).then_inc(y_ready, 1)


class RawWeights:
    PIECE = 2

    def __init__(self, nc, c, ctx, tag, room=None):
        width = self.PIECE * 3 * P
        count = KPC // self.PIECE
        if room is None:
            room = [ctx.enter_context(nc.sbuf_tensor(f"{tag}_raw{n}", [P, size], F32))[:]
                    for n, size in enumerate((count * width, E + E * P))]
        *large, small = room
        fit = large[0].shape[1] // width
        self.sources = [("wg", slice(None)), ("spread", slice(None))]
        self.pieces = [small[:, 0:E], small[0:2 * E, E:E + E * P]]
        for n in range(count):
            at = n % fit * width
            self.pieces.append(large[n // fit][:, at:at + width].rearrange("p (k a m) -> p k a m", k=self.PIECE, a=3))
            self.sources.append(("w_ffn", slice(n * self.PIECE, (n + 1) * self.PIECE)))
        self.arrived = [c.sem(f"{tag}_in{n}") for n in range(len(self.pieces))]

    def load(self, eng, io):
        for raw, (name, at), arrived in zip(self.pieces, self.sources, self.arrived):
            eng.dma_start(raw, io[name][:, at]).then_inc(arrived, 16)


class ExpertWeights:

    def __init__(self, nc, c, ctx, tag):
        self.nc, self.c, self.tag = nc, c, tag

        def pair(name, shape):
            return [ctx.enter_context(nc.sbuf_tensor(f"{tag}_{name}_{part}", shape, F32R)) for part in ("hi", "lo")]

        self.w = pair("w", [P, KPC, 3, P])
        self.wg = ctx.enter_context(nc.sbuf_tensor(f"{tag}_wg", [P, 2, E], F32R))
        self.spread = ctx.enter_context(nc.sbuf_tensor(f"{tag}_spread", [2 * E, E * P], F32R))
        self.hi_done = c.sem(f"{tag}_hi_done")
        self.own_hi_done = c.sem(f"{tag}_own_hi_done")
        self.lo_done = c.sem(f"{tag}_lo_done")
        self.dve_lo_done = c.sem(f"{tag}_dve_lo_done")

    def take(self, raw):
        parts = [(self.wg[:, 0, :], self.wg[:, 1, :]), (self.spread[:], None)]
        for n in range(0, KPC, raw.PIECE):
            parts.append((self.w[0][:, n:n + raw.PIECE], self.w[1][:, n:n + raw.PIECE]))
        self.pieces = [(r, hi, lo, arrived) for r, (hi, lo), arrived in zip(raw.pieces, parts, raw.arrived)]

    def split_hi(self, act, which):
        for raw, hi, lo, raw_in in self.pieces[which]:
            act.wait_ge(raw_in, 16)
            self.nc.scalar.activation(hi, raw, ACT.Copy).then_inc(self.hi_done, 1)

    def split_lo(self, eng, ops, which, before, done):
        for n, (raw, hi, lo, raw_in) in enumerate(self.pieces[which]):
            eng.wait_ge(self.hi_done, before + n + 1)
            if lo is None:
                continue
            ops.tensor_tensor(lo, raw, hi.bitcast(F32), ALU.subtract).then_inc(done, 1)

    def split(self, pool, which):
        for n, (raw, hi, lo, raw_in) in enumerate(self.pieces[which]):
            pool.wait_ge(raw_in, 16)
            self.nc.gpsimd.tensor_scalar(hi, raw, 1.0, None, ALU.mult).then_inc(self.own_hi_done, 1)
            pool.wait_ge(self.own_hi_done, n + 1)
            if lo is None:
                continue
            self.nc.gpsimd.tensor_tensor(lo, raw, hi.bitcast(F32), ALU.subtract).then_inc(self.lo_done, 1)


def feed_forward(nc, c, w, tag, out=None):
    UNROLL = 2
    LAG = 3
    RING = LAG + 1
    ROWS = 4
    with ExitStack() as ctx:
        def sb(name, shape, dt=F32):
            return ctx.enter_context(nc.sbuf_tensor(f"{tag}_{name}", shape, dt))

        def psum(name, shape):
            return ctx.enter_context(nc.psum_tensor(f"{tag}_{name}", shape, F32))

        def sem(name):
            return c.sem(f"{tag}_{name}")

        xn = sb("xn", [P, CT, D])
        xt_hi = [sb(f"xt_hi{u}", [P, CHUNK], F32R) for u in range(2)]
        xt_lo = [sb(f"xt_lo{u}", [P, CHUNK], F32R) for u in range(2)]
        mix = sb("mix", [P, CT, E])
        mix_parts = sb("mix_parts", [P, CT, 2 * E])
        mix_t = [sb(f"mix_t{u}", [2 * E, CHUNK], F32R) for u in range(2)]
        mix_rows = [sb(f"mix_rows{u}", [P, CHUNK]) for u in range(ROWS)]
        hid = [sb(f"hid{u}", [P, CHUNK]) for u in range(RING)]
        hid_hi = [sb(f"hid_hi{u}", [P, CHUNK], F32R) for u in range(RING)]
        hid_lo = [sb(f"hid_lo{u}", [P, CHUNK], F32R) for u in range(RING)]
        y_t = xn[:].rearrange("p t d -> p (t d)")
        score = sb("score", [P, CT, E])
        best = sb("best", [P, CT, 8])
        best_at = sb("best_at", [P, CT, 8], U32)
        best_atf = sb("best_atf", [P, CT, 8])
        onehot = sb("onehot", [P, CT, TOP, E])
        stats = sb("stats", [P, CT, 6])
        moments = sb("moments", [P, CT, 2])

        p_gate = [psum(f"p_gate{u}", [P, CHUNK]) for u in range(2)]
        p_up = [psum(f"p_up{u}", [P, CHUNK]) for u in range(2)]
        p_y = psum("p_y", [P, CHUNK])
        p_mix = psum("p_mix", [P, CHUNK])
        p_t = psum("p_t", [P, CHUNK])
        p_score = psum("p_score", [P, CT, 2, E])

        zeroed = sem("zeroed")
        sqrt_ready = sem("sqrt_ready")
        var_ready = sem("var_ready")
        xn_ready = sem("xn_ready")
        xt_ready = sem("xt_ready")
        xt_hi_ready = sem("xt_hi_ready")
        xt_lo_ready = sem("xt_lo_ready")
        scores_ready = sem("scores_ready")
        scores_copied = sem("scores_copied")
        mix_ready = sem("mix_ready")
        mix_t_ready = sem("mix_t_ready")
        mix_t_copied = sem("mix_t_copied")
        spread_ready = sem("spread_ready")
        spread_copied = sem("spread_copied")
        gate_ready = sem("gate_ready")
        up_ready = sem("up_ready")
        silu_done = sem("silu_done")
        mixed = sem("mixed")
        own_mixed = sem("own_mixed")
        hid_ready = sem("hid_ready")
        hid_hi_ready = sem("hid_hi_ready")
        hid_lo_ready = sem("hid_lo_ready")
        down_done = sem("down_done")
        y_copied = sem("y_copied")
        yt_ready = sem("yt_ready")
        x_added = sem("x_added")
        dve_step = sem("dve_step")
        moved = sem("moved")
        stored = sem("stored")

        def three(out_ap, lhs, rhs, start=True, stop=True):
            nc.tensor.matmul(out_ap, lhs[0], rhs[0], start=start, stop=False)
            nc.tensor.matmul(out_ap, lhs[1], rhs[0], start=False, stop=False)
            return nc.tensor.matmul(out_ap, lhs[0], rhs[1], start=False, stop=stop)

        SPREADS = {BLOCKS.index([(0, e, P, P)]): e + 1 for e in range(E)}
        def mix_part(eng, k, v, n):
            row, e, _, count = BLOCKS[k][n]
            rows = slice(row, row + count)
            return eng.tensor_tensor(hid[v % RING][rows], hid[v % RING][rows], mix_rows[e % ROWS][rows], ALU.mult)

        def blocks(i, u):
            return [(i * (UNROLL * KPC) + (u * KPC + k), k, u * KPC + k) for k in range(KPC)]

        STEPS = 2 * CT + 5 + 2 * CT
        NORM_AT, NORM_T_AT, XT_AT, SCORES_AT, BEST_AT = 0, 2, 4, 6, 8
        Y_T_AT, Y_AT, STATS_AT, MIX_T_AT, MIX_COPY_AT = 7, 12, 16, 16, 18

        block = ctx.enter_context(nc.Block())

        @block.sync
        def _(sp):
            if out is not None:
                halves = TPB // CT
                rows = out.rearrange("b (p j) d -> p b j d", p=P)
                with sp.Fori(0, B) as b:
                    for h in range(halves):
                        sp.wait_ge(x_added, b * halves + (h + 2))
                        sp.dma_start(rows[:, bass.ds(b, 1), h * CT:(h + 1) * CT, :][:, 0],
                                     residual_tiles(c.x, b * TPB + h * CT, CT)).then_inc(stored, 16)
                sp.wait_ge(stored, 16 * CHUNKS)

        @block.gpsimd
        def _(pool):
            for v in range(LAG):
                nc.gpsimd.memset(hid_hi[v][:].bitcast(F32), 0.0).then_inc(zeroed, 1)
                nc.gpsimd.memset(hid_lo[v][:].bitcast(F32), 0.0).then_inc(zeroed, 1)
            nc.gpsimd.memset(mix_rows[ROWS - 1][:, 0:1], 0.0).then_inc(mixed, 1)
            with pool.Fori(0, CHUNKS // UNROLL) as i:
                for u in range(UNROLL):
                    for kk, k, v in blocks(i, u):
                        pool.wait_ge(spread_copied, i * (UNROLL * E) + (u * E + max(e for _, e, _, _ in BLOCKS[k]) + 1))
                        pool.wait_ge(silu_done, kk + 1)
                        if len(BLOCKS[k]) != len(BLOCKS[k - 1]):
                            pool.wait_ge(mixed, kk + 1)
                        mix_part(nc.gpsimd, k, v, 0).then_inc(mixed, 1)

        @block.scalar
        def _(act):
            def hi_of_xt(u, count):
                act.wait_ge(xt_ready, count)
                nc.scalar.activation(xt_hi[u][:], p_t[:], ACT.Copy).then_inc(xt_hi_ready, 1)

            def copy_mix(u, count):
                act.wait_ge(mix_t_ready, count)
                nc.scalar.activation(mix_t[u][:], p_t[0:2 * E, :], ACT.Copy).then_inc(mix_t_copied, 1)

            def copy_spread(n, count):
                act.wait_ge(spread_ready, count)
                nc.scalar.activation(mix_rows[n % ROWS][:], p_mix[:], ACT.Copy).then_inc(spread_copied, 1)

            def hi_of_hid(v, hid_count, down_count):
                act.wait_ge(hid_ready, hid_count)
                act.wait_ge(down_done, down_count)
                nc.scalar.activation(hid_hi[v % RING][:], hid[v % RING][:], ACT.Copy).then_inc(hid_hi_ready, 1)

            act.wait_ge(var_ready, 1)
            nc.scalar.activation(c.rstd[:, PAD:PAD + TILES], c.rstd[:, PAD:PAD + TILES], ACT.Sqrt).then_inc(sqrt_ready, 1)
            nc.scalar.activation(hid[0][:, 0:1], c.ident[:, 0:1], ACT.Silu)
            hi_of_xt(0, 1)
            copy_mix(0, 1)
            copy_spread(0, 1)
            with act.Fori(0, CHUNKS // UNROLL) as i:
                for u in range(UNROLL):
                    for kk, k, v in blocks(i, u):
                        if k == LAG:
                            act.wait_ge(xt_ready, i * UNROLL + (u + 2))
                            act.wait_ge(down_done, i * (UNROLL * KPC) + (u * KPC + LAG + 2))
                            nc.scalar.activation(y_t, p_y[:], ACT.Copy).then_inc(y_copied, 1)
                        act.wait_ge(gate_ready, kk + 1)
                        nc.scalar.activation(hid[v % RING][:], p_gate[k % 2][:], ACT.Silu).then_inc(silu_done, 1)
                        hi_of_hid(v - 1, kk + 2, kk + 1)
                        if k in SPREADS:
                            copy_spread(SPREADS[k], i * (UNROLL * E) + (u * E + SPREADS[k] + 1))
                        if k == XT_AT:
                            hi_of_xt(1 - u, i * UNROLL + (u + 2))
                        if k == MIX_COPY_AT:
                            copy_mix(1 - u, i * UNROLL + (u + 2))
            hi_of_hid(UNROLL * KPC - 1, CHUNKS * KPC + 2, CHUNKS * KPC + 1)
            act.wait_ge(down_done, CHUNKS * KPC + LAG + 2)
            nc.scalar.activation(y_t, p_y[:], ACT.Copy).then_inc(y_copied, 1)

        @block.vector
        def _(dve):
            def step(ins):
                ins.then_inc(dve_step, 1)

            def norm(first):
                for t in range(CT):
                    at = bass.ds(first + (PAD + t), 1)
                    last = nc.vector.tensor_scalar(xn[:, t, :], c.x[:, at, :][:, 0, :], c.mv[:, at, 0], c.rstd[:, at],
                                                   ALU.subtract, ALU.mult)
                last.then_inc(xn_ready, 1)

            def lo_of_xt(u, count):
                dve.wait_ge(xt_hi_ready, count)
                nc.vector.tensor_tensor(xt_lo[u][:], p_t[:], xt_hi[u][:].bitcast(F32), ALU.subtract).then_inc(xt_lo_ready, 1)

            def lo_of_hid(v, count):
                dve.wait_ge(hid_hi_ready, count)
                nc.vector.tensor_tensor(hid_lo[v % RING][:], hid[v % RING][:],
                                        hid_hi[v % RING][:].bitcast(F32), ALU.subtract).then_inc(hid_lo_ready, 1)

            def copy_scores(count):
                dve.wait_ge(scores_ready, count)
                nc.vector.tensor_reduce(score[:], p_score[:].rearrange("p t a e -> p t e a"), axis=AX_X,
                                        op=ALU.add).then_inc(scores_copied, 1)

            def find_best():
                for t in range(CT):
                    step(nc.vector.max(best[:, t, :], score[:, t, :]))

            def find_where():
                for t in range(CT):
                    step(nc.vector.max_index(best_at[:, t, :], best[:, t, :], score[:, t, :]))

            def mix_of(s):
                dve.wait_ge(dve_step, s + 2 * CT)
                step(nc.vector.tensor_copy(best_atf[:], best_at[:]))
                dve.wait_ge(dve_step, s + (2 * CT + 1))
                step(nc.vector.tensor_tensor(
                    onehot[:], c.iota[:].unsqueeze(1).unsqueeze(1).broadcast_to([P, CT, TOP, E]),
                    best_atf[:, :, 0:TOP].unsqueeze(3).broadcast_to([P, CT, TOP, E]), ALU.is_equal))
                dve.wait_ge(dve_step, s + (2 * CT + 2))
                step(nc.vector.tensor_tensor(
                    onehot[:], onehot[:], best[:, :, 0:TOP].unsqueeze(3).broadcast_to([P, CT, TOP, E]), ALU.mult))
                dve.wait_ge(dve_step, s + (2 * CT + 3))
                step(nc.vector.tensor_tensor(mix[:], onehot[:, :, 0, :], onehot[:, :, 1, :], ALU.add))

            def parts_of_mix(s):
                dve.wait_ge(dve_step, s + (2 * CT + 4))
                step(nc.vector.tensor_scalar(mix_parts[:, :, 0:E].bitcast(F32R), mix[:], 1.0, None, ALU.mult))
                dve.wait_ge(dve_step, s + (2 * CT + 5))
                nc.vector.tensor_tensor(mix_parts[:, :, E:2 * E].bitcast(F32R), mix[:], mix_parts[:, :, 0:E],
                                        ALU.subtract).then_inc(mix_ready, 1)

            PRE = 2 * CT + 5
            OWN = {BEST_AT + 1: CT, STATS_AT + 1: PRE + CT, STATS_AT + 2: PRE + 2 * CT}
            nc.vector.tensor_scalar(c.rstd[:, PAD:PAD + TILES], c.mv[:, PAD:PAD + TILES, 1], EPS, None, ALU.add).then_inc(var_ready, 1)
            dve.wait_ge(sqrt_ready, 1)
            nc.vector.reciprocal(c.rstd[:, PAD:PAD + TILES], c.rstd[:, PAD:PAD + TILES]).then_inc(var_ready, 1)
            dve.wait_ge(var_ready, 2)
            norm(0)
            for v in range(RING - 2, RING):
                nc.vector.memset(hid[v][:], 0.0).then_inc(hid_ready, 1)
            for n in range(2):
                nc.vector.memset(hid[1][:, n:n + 1], 0.0).then_inc(hid_lo_ready, 1)
            lo_of_xt(0, 1)
            copy_scores(1)
            dve.wait_ge(scores_copied, 1)
            find_best()
            dve.wait_ge(dve_step, CT)
            find_where()
            mix_of(0)
            parts_of_mix(0)
            with dve.Fori(0, CHUNKS // UNROLL) as i:
                for u in range(UNROLL):
                    s = i * (UNROLL * STEPS) + (u * STEPS + PRE)
                    for kk, k, v in blocks(i, u):
                        if k == STATS_AT:
                            dve.wait_ge(x_added, i * UNROLL + (u + 1))
                        if k in OWN:
                            dve.wait_ge(dve_step, s + OWN[k])
                        if k == BEST_AT:
                            dve.wait_ge(scores_copied, i * UNROLL + (u + 2))
                        if len(BLOCKS[k]) > 1:
                            dve.wait_ge(spread_copied, i * (UNROLL * E) + (u * E + max(e for _, e, _, _ in BLOCKS[k]) + 1))
                            dve.wait_ge(silu_done, kk + 1)
                            mix_part(nc.vector, k, v, 1).then_inc(own_mixed, 1)
                            dve.wait_ge(own_mixed, i * (UNROLL * PACKED) + (u * PACKED + sum(len(b) > 1 for b in BLOCKS[:k + 1])))
                        dve.wait_ge(mixed, kk + 2)
                        dve.wait_ge(up_ready, kk + 1)
                        nc.vector.tensor_tensor(hid[v % RING][:], hid[v % RING][:], p_up[k % 2][:], ALU.mult).then_inc(hid_ready, 1)
                        lo_of_hid(v - 1, kk + 1)
                        if k == NORM_AT:
                            dve.wait_ge(xt_ready, i * UNROLL + (u + 1))
                            norm(i * (UNROLL * CT) + (u + 1) * CT)
                        if k == XT_AT:
                            lo_of_xt(1 - u, i * UNROLL + (u + 2))
                        if k == BEST_AT - 1:
                            copy_scores(i * UNROLL + (u + 2))
                        if k == BEST_AT:
                            find_best()
                        if k == BEST_AT + 1:
                            find_where()
                        if k == Y_AT:
                            dve.wait_ge(yt_ready, i * UNROLL + (u + 1))
                            at = bass.ds(i * (UNROLL * CT) + u * CT, CT)
                            nc.vector.tensor_tensor(c.x[:, at, :], c.x[:, at, :], p_t[:].rearrange("p (t d) -> p t d", t=CT),
                                                    ALU.add).then_inc(x_added, 1)
                        if k == BEST_AT + 3:
                            mix_of(s)
                        if k == BEST_AT + 5:
                            parts_of_mix(s)
                        if k == STATS_AT:
                            for t in range(CT):
                                step(nc.vector.bn_stats(stats[:, t, :], c.x[:, bass.ds(i * (UNROLL * CT) + (u * CT + t), 1), :][:, 0, :]))
                        if k == STATS_AT + 1:
                            for t in range(CT):
                                step(nc.vector.bn_aggr(moments[:, t, :], stats[:, t, :]))
                        if k == STATS_AT + 2:
                            nc.vector.tensor_copy(c.mv[:, bass.ds(i * (UNROLL * CT) + u * CT, CT), :], moments[:]).then_inc(moved, 1)
            lo_of_hid(UNROLL * KPC - 1, CHUNKS * KPC + 1)
            dve.wait_ge(yt_ready, CHUNKS + 1)
            tail = c.x[:, TILES:TILES + CT, :]
            nc.vector.tensor_tensor(tail, tail, p_t[:].rearrange("p (t d) -> p t d", t=CT), ALU.add).then_inc(x_added, 1)
            if out is None:
                dve.wait_ge(x_added, CHUNKS + 1)
                end = CHUNKS * STEPS + PRE
                for t in range(CT):
                    step(nc.vector.bn_stats(stats[:, t, :], c.x[:, TILES + t, :]))
                for t in range(CT):
                    dve.wait_ge(dve_step, end + t + 1)
                    step(nc.vector.bn_aggr(c.mv[:, TILES + t, :], stats[:, t, :]))

        @block.tensor
        def _(pe):
            def transposes(dst, src, ready):
                for t in range(CT):
                    last = nc.tensor.transpose(dst[:, t * P:(t + 1) * P], src(t), c.ident[:])
                last.then_inc(ready, 1)

            def scores(u, count):
                pe.wait_ge(xt_lo_ready, count)
                for t in range(CT):
                    at = slice(t * P, (t + 1) * P)
                    nc.tensor.matmul(p_score[:, t], xt_hi[u][:, at], w.wg[:], start=True, stop=False,
                                     skip_group_check=True)
                    last = nc.tensor.matmul(p_score[:, t, 0], xt_lo[u][:, at], w.wg[:, 0], start=False, stop=True,
                                            skip_group_check=True)
                last.then_inc(scores_ready, 1)

            def part(k, n):
                return w.w[0][:, k, n, :], w.w[1][:, k, n, :]

            def spread(e, u):
                nc.tensor.matmul(p_mix[:], w.spread[:, e * P:(e + 1) * P], mix_t[u][:],
                                 start=True, stop=True).then_inc(spread_ready, 1)

            def down(k, v, lo_count):
                pe.wait_ge(hid_lo_ready, lo_count)
                three(p_y[:], part(k, 2), (hid_hi[v % RING][:], hid_lo[v % RING][:]),
                      k == 0, k == KPC - 1).then_inc(down_done, 1)

            pe.wait_ge(xn_ready, 1)
            transposes(p_t, lambda t: xn[:, t, :], xt_ready)
            pe.wait_ge(zeroed, 2 * LAG)
            for n in range(2):
                three(p_y[:], part(0, 0), (hid_hi[0][:], hid_lo[0][:]), start=n == 0, stop=False).then_inc(down_done, 1)
            scores(0, 1)
            pe.wait_ge(mix_ready, 1)
            transposes(p_t[0:2 * E], lambda t: mix_parts[:, t, :], mix_t_ready)
            pe.wait_ge(mix_t_copied, 1)
            spread(0, 0)
            with pe.Fori(0, CHUNKS // UNROLL) as i:
                for u in range(UNROLL):
                    for kk, k, v in blocks(i, u):
                        pe.wait_ge(hid_ready, kk + 1)
                        three(p_gate[k % 2][:], part(k, 0), (xt_hi[u][:], xt_lo[u][:])).then_inc(gate_ready, 1)
                        three(p_up[k % 2][:], part(k, 1), (xt_hi[u][:], xt_lo[u][:])).then_inc(up_ready, 1)
                        if k in SPREADS:
                            n = SPREADS[k]
                            if n == E:
                                pe.wait_ge(mix_t_copied, i * UNROLL + (u + 2))
                            pe.wait_ge(spread_copied, i * (UNROLL * E) + (u * E + n))
                            spread(n % E, u if n < E else 1 - u)
                        if k == LAG:
                            pe.wait_ge(y_copied, i * UNROLL + (u + 1))
                        down((k - LAG) % KPC, v - LAG, kk + 1)
                        if k == NORM_T_AT:
                            pe.wait_ge(xn_ready, i * UNROLL + (u + 2))
                            transposes(p_t, lambda t: xn[:, t, :], xt_ready)
                        if k == SCORES_AT:
                            scores(1 - u, i * UNROLL + (u + 2))
                        if k == Y_T_AT:
                            transposes(p_t, lambda t: y_t[:, t * P:(t + 1) * P], yt_ready)
                        if k == MIX_T_AT:
                            pe.wait_ge(x_added, i * UNROLL + (u + 1))
                            pe.wait_ge(mix_ready, i * UNROLL + (u + 2))
                            transposes(p_t[0:2 * E], lambda t: mix_parts[:, t, :], mix_t_ready)
            for n in range(LAG):
                down(KPC - LAG + n, UNROLL * KPC - LAG + n, CHUNKS * KPC + n + 1 if n < 2 else CHUNKS * KPC + 3)
            pe.wait_ge(y_copied, CHUNKS + 1)
            transposes(p_t, lambda t: y_t[:, t * P:(t + 1) * P], yt_ready)


class Stacks:
    ADDS_1, ADDS_2, ADDS_MAX = 16 * 3 * (GH + 2), 16 * 3 * (GH + 1), 16 * 2 * GH

    def __init__(self, nc, c, outer, ctx):
        def two(name, shape):
            return [ctx.enter_context(nc.sbuf_tensor(f"{name}{u}", shape, F32R)) for u in range(2)]

        def split(ctx, name):
            return ctx.enter_context(nc.sbuf_tensor(name, [P, B, N], F32R))

        self.lo = [split(outer, "q_lo"), split(outer, "k_lo")]
        self.hi = [split(outer, "q_hi"), split(ctx, "k_hi")]
        self.q_pad = two("q_pad", [P, 2, N])
        self.k_t = two("k_t", [P, N])
        self.k_pad = two("k_pad", [P, GH, N])
        self.qm_t = two("qm_t", [P, N])
        self.pass1_in = c.sem("pass1_in")
        self.pass2_in = c.sem("pass2_in")
        self.max_in = c.sem("max_in")

    def room(self):
        flat = [t[:].rearrange("p b n -> p (b n)").bitcast(F32) for t in self.lo + self.hi[0:1]]
        return flat[0:2] + [flat[2][:, 0:N], flat[2][:, N:]]

    def zeroed(self):
        return self.q_pad + self.k_t + self.k_pad + self.qm_t

    @staticmethod
    def rows_of(part, batch, first, count):
        return part[first:first + count, bass.ds(batch, 1), :][:, 0].bitcast(F32)

    def load_pass1(self, sp, u, batch, place):
        for block, (q, k) in enumerate(((self.hi, self.hi), (self.lo, self.hi), (self.hi, self.lo))):
            for pair in range(2):
                row, src = P // 2 * pair + SR // 2 * block, GC * place + GC // 2 * pair
                sp.dma_start(self.k_t[u][row:row + SR // 2, :].bitcast(F32),
                             self.rows_of(k[1], batch, src, GC // 2)).then_inc(self.pass1_in, 16)
                for h in range(2):
                    at = slice(row + DB * h, row + DB * (h + 1))
                    sp.dma_start(self.q_pad[u][at, h, :].bitcast(F32),
                                 self.rows_of(q[0], batch, src + DB * h, DB)).then_inc(self.pass1_in, 16)

    def load_pass2(self, sp, u, batch, place):
        for block, (q, k) in enumerate(((self.hi, self.hi), (self.lo, self.hi), (self.hi, self.lo))):
            sp.dma_start(self.qm_t[u][SR * block:SR * (block + 1), :].bitcast(F32),
                         self.rows_of(q[0], batch, GC * place, GC)).then_inc(self.pass2_in, 16)
            for h in range(GH):
                row = SR * block + DB * h
                sp.dma_start(self.k_pad[u][row:row + DB, h, :].bitcast(F32),
                             self.rows_of(k[1], batch, GC * place + DB * h, DB)).then_inc(self.pass2_in, 16)

    def load_max(self, sp, u, max_rows):
        for h in range(GH):
            for part in range(2):
                row, src = 3 * SR + DB * h + part, (2 * h + part) * TPB
                sp.dma_start(self.qm_t[u][row:row + 1, :].rearrange("o (t n) -> o t n", t=TPB).bitcast(F32),
                             max_rows[src:src + TPB, :].bitcast(F32)).then_inc(self.max_in, 16)


def project_qkv(nc, c, stacks, tag):
    VT = TPB // 2
    with ExitStack() as ctx:
        def sb(name, shape, dt=F32):
            return ctx.enter_context(nc.sbuf_tensor(f"{tag}_{name}", shape, dt))

        def psum(name, shape):
            return ctx.enter_context(nc.psum_tensor(f"{tag}_{name}", shape, F32))

        def sem(name):
            return c.sem(f"{tag}_{name}")

        xn = [sb(f"xn{u}", [P, TPB, D]) for u in range(2)]
        xnt = [sb(f"xnt{u}", [P, N]) for u in range(2)]
        p_t = psum("p_t", [P, N])
        p_qk = [psum(f"p_{name}", [P, N]) for name in "qk"]
        p_v = [psum(f"p_v{n}", [P, VT, D]) for n in range(2)]
        ones = sb("ones", [DB, N])
        zeroed = sem("zeroed")
        ones_ready = sem("ones_ready")
        ones_in = sem("ones_in")
        var_ready = sem("var_ready")
        sqrt_done = sem("sqrt_done")
        xn_ready = sem("xn_ready")
        xt_ready = sem("xt_ready")
        xnt_ready = sem("xnt_ready")
        qk_ready = sem("qk_ready")
        hi_ready = sem("hi_ready")
        qk_done = sem("qk_done")
        v_ready = sem("v_ready")
        v_stored = sem("v_stored")
        block = ctx.enter_context(nc.Block())

        @block.gpsimd
        def _(pool):
            for tensor in stacks.zeroed():
                nc.gpsimd.memset(tensor[:].bitcast(F32), 0.0).then_inc(zeroed, 1)

        @block.sync
        def _(sp):
            sp.wait_ge(zeroed, len(stacks.zeroed()))
            sp.wait_ge(qk_done, 4)
            stacks.load_pass1(sp, 0, 0, 0)
            sp.wait_ge(ones_ready, 1)
            for k_pad in stacks.k_pad:
                for h in range(GH):
                    rows = slice(3 * SR + DB * h, 3 * SR + DB * (h + 1))
                    sp.dma_start(k_pad[rows, h, :].bitcast(F32), ones[:]).then_inc(ones_in, 16)
            sp.wait_ge(ones_in, 16 * 2 * GH)

        @block.scalar
        def _(act):
            def copy_xt(u, count):
                act.wait_ge(xt_ready, count)
                nc.scalar.activation(xnt[u][:], p_t[:], ACT.Copy).then_inc(xnt_ready, 1)

            act.wait_ge(var_ready, 1)
            nc.scalar.activation(c.rstd[:, PAD:PAD + TILES], c.rstd[:, PAD:PAD + TILES], ACT.Sqrt).then_inc(sqrt_done, 1)
            copy_xt(0, 1)
            with act.Fori(0, B // 2) as i:
                for u in range(2):
                    b = i * 2 + u
                    for n in range(2):
                        act.wait_ge(qk_ready, b * 2 + (n + 1))
                        nc.scalar.activation(stacks.hi[n][:, bass.ds(b, 1), :][:, 0], p_qk[n][:], ACT.Identity,
                                             bias=c.b_qk[:, n:n + 1]).then_inc(hi_ready, 1)
                    copy_xt(1 - u, i * 2 + (u + 2))

        @block.vector
        def _(dve):
            def norm(b, u, tiles):
                for t in tiles:
                    at = bass.ds(b * TPB + (PAD + t), 1)
                    last = nc.vector.tensor_scalar(xn[u][:, t, :], c.x[:, at, :][:, 0, :], c.mv[:, at, 0], c.rstd[:, at],
                                                   ALU.subtract, ALU.mult)
                return last

            def lo_of(b, n):
                at = bass.ds(b, 1)
                nc.vector.scalar_tensor_tensor(
                    out=stacks.lo[n][:, at, :][:, 0], in0=p_qk[n][:], scalar=c.b_qk[:, n:n + 1],
                    in1=stacks.hi[n][:, at, :][:, 0].bitcast(F32), op0=ALU.add, op1=ALU.subtract).then_inc(qk_done, 1)

            def store_v(b, n):
                for g in range(GPB):
                    last = nc.vector.tensor_tensor(
                        c.v[:, bass.ds(b * GPB + g, 1), n * VT:(n + 1) * VT, :][:, 0],
                        p_v[n][:, :, g * GC:(g + 1) * GC],
                        c.b_v[:, g * GC:(g + 1) * GC].unsqueeze(1).broadcast_to([P, VT, GC]), ALU.add)
                last.then_inc(v_stored, 1)

            nc.vector.tensor_scalar(c.rstd[:, PAD:PAD + TILES], c.mv[:, PAD:PAD + TILES, 1], EPS, None, ALU.add).then_inc(var_ready, 1)
            nc.vector.memset(ones[:], 1.0).then_inc(ones_ready, 1)
            for p_free in p_qk:
                nc.vector.memset(p_free[:, 0:1], 0.0).then_inc(qk_done, 1)
            for p_free in p_v:
                nc.vector.memset(p_free[:, 0, 0:1], 0.0).then_inc(v_stored, 1)
            dve.wait_ge(sqrt_done, 1)
            nc.vector.reciprocal(c.rstd[:, PAD:PAD + TILES], c.rstd[:, PAD:PAD + TILES]).then_inc(var_ready, 1)
            dve.wait_ge(var_ready, 2)
            norm(0, 0, range(TPB)).then_inc(xn_ready, 1)
            with dve.Fori(0, B // 2) as i:
                for u in range(2):
                    b = i * 2 + u
                    norm(i * 2 + (u + 1), 1 - u, range(TPB - 1))
                    dve.wait_ge(hi_ready, b * 2 + 1)
                    norm(i * 2 + (u + 1), 1 - u, [TPB - 1]).then_inc(xn_ready, 1)
                    lo_of(b, 0)
                    dve.wait_ge(hi_ready, b * 2 + 2)
                    dve.wait_ge(v_ready, b * 2 + 1)
                    store_v(b, 0)
                    lo_of(b, 1)
                    dve.wait_ge(v_ready, b * 2 + 2)
                    store_v(b, 1)

        @block.tensor
        def _(pe):
            def transposes(u, count):
                pe.wait_ge(xn_ready, count)
                for t in range(TPB):
                    last = nc.tensor.transpose(p_t[:, t * P:(t + 1) * P], xn[u][:, t, :], c.ident[:])
                last.then_inc(xt_ready, 1)

            transposes(0, 1)
            with pe.Fori(0, B // 2) as i:
                for u in range(2):
                    b = i * 2 + u
                    pe.wait_ge(xnt_ready, b + 1)
                    for n in range(2):
                        pe.wait_ge(qk_done, b * 2 + (n + 1))
                        for half in range(2):
                            cols = slice(half * (N // 2), (half + 1) * (N // 2))
                            last = nc.tensor.matmul(p_qk[n][:, cols], c.w_qkv[:, n * D:(n + 1) * D], xnt[u][:, cols],
                                                    start=True, stop=True)
                        last.then_inc(qk_ready, 1)
                    transposes(1 - u, i * 2 + (u + 2))
                    for n in range(2):
                        pe.wait_ge(v_stored, b * 2 + (n + 1))
                        for t in range(VT):
                            at = (n * VT + t) * P
                            last = nc.tensor.matmul(p_v[n][:, t, :], xnt[u][:, at:at + P], c.w_qkv[:, 2 * D:3 * D],
                                                    start=True, stop=True)
                        last.then_inc(v_ready, 1)


def softmax_attention(nc, c, io, stacks, raw, tag):
    SCALE = float(DB) ** -0.5
    HALF = N // 2
    QUADS = 2 * TPB
    NE = 3
    S_TILES = TPB * GH
    LEAD = 8
    TURNS = [("scores_t", 0, 0), ("scores", 0, 0), ("scores", 0, 1), ("scores_t", 1, 0), ("output", 0, 0),
             ("scores_t", 2, 0), ("scores", 1, 0), ("scores", 1, 1), ("scores_t", 3, 0)]
    LAST_TURNS = [("scores_t", h, 0) for h in range(GH)] + [("output", 0, 0)]
    O_AT, M_AT = 2, QUADS - 4
    with ExitStack() as ctx:
        def sb(name, shape, dt=F32):
            return ctx.enter_context(nc.sbuf_tensor(f"{tag}_{name}", shape, dt))

        def psum(name, shape):
            return ctx.enter_context(nc.psum_tensor(f"{tag}_{name}", shape, F32))

        def sem(name):
            return c.sem(f"{tag}_{name}")

        q_pad, k_t, k_pad, qm_t = stacks.q_pad, stacks.k_t, stacks.k_pad, stacks.qm_t
        neg_max = sb("neg_max", [P, 2, GH, 2, TPB])
        max_rows = sb("max_rows", [GH * 2 * TPB, P], F32R)
        v_nat = [sb(f"v_nat{u}", [P, TPB, GH, 32]) for u in range(2)]
        row_max = [sb(f"row_max{u}", [P, TPB, GH]) for u in range(2)]
        prob = [sb(f"prob{n}", [P, HALF]) for n in range(2 * GH)]
        o_t = sb("o_t", [P, N])
        o_den = sb("o_den", [P, TPB, GH])
        p_s = [psum(f"p_s{u}", [P, N]) for u in range(2)]
        p_e = [psum(f"p_e{u}", [P, HALF]) for u in range(NE)]
        p_o = psum("p_o", [P, HALF])

        v_ready = sem("v_ready")
        zeroed = sem("zeroed")
        m_copied = sem("m_copied")
        s_ready = sem("s_ready")
        max_done = sem("max_done")
        neg_zeroed = sem("neg_zeroed")
        neg_hi = sem("neg_hi")
        m_ready = sem("m_ready")
        qm_ready = sem("qm_ready")
        st_ready = sem("st_ready")
        exp_done = sem("exp_done")
        pv_done = sem("pv_done")
        o_copied = sem("o_copied")
        ot_ready = sem("ot_ready")
        den_done = sem("den_done")
        o_done = sem("o_done")
        biased = sem("biased")

        def users(g):
            out = []
            for q in range(QUADS):
                for n in (2 * q, 2 * q + 1):
                    group, tile = (g, n + LEAD) if n + LEAD < S_TILES else (g + 1, n + LEAD - S_TILES)
                    out.append(("s", group, tile) if group < GROUPS else None)
                    if q == M_AT and n == 2 * q:
                        out.append(("m", g, 0) if g < GROUPS else None)
                if q == O_AT:
                    out.append(("o", g - 2, 0) if g >= 2 else None)
            return out

        FIRST = [("s", 0, n) for n in range(LEAD)]
        ALL = FIRST + [x for g in range(GROUPS + 1) for x in users(g)] + [("o", GROUPS - 1, 0)]
        PLACE = {x: n for n, x in enumerate(ALL) if x is not None}
        FREED = {"s": (max_done, S_TILES, 0), "m": (m_copied, 1, 0), "o": (o_done, 1, 0)}

        def scores_ring(r):
            first = ring_start(r)
            free = p_s[1 - PLACE[("o", GROUPS - 2, 0)] % 2]
            return [p_e[(first + n) % NE][:] for n in range(NE)] + ([free[:, 0:HALF], free[:, HALF:N]] if r == GROUPS else [])

        def ring_start(r):
            return r % 2

        def user_before(r, e):
            buffer = (ring_start(r) + e) % NE
            return max(n for n in range(4 * QUADS) if (ring_start(r - 1) + n) % NE == buffer)


        def count(group, shift, per, k):
            return group * per + (shift * per + k + 1)

        block = ctx.enter_context(nc.Block())

        LOOPED = (GROUPS - 3) // GPB * GPB

        def steps(eng, body):
            body(0, 0, None)
            body(1, 1, None)
            with eng.Fori(0, LOOPED // GPB) as i:
                for u in range(GPB):
                    body(i * GPB + (2 + u), GPB + 2 + u, i)
            for g in range(LOOPED + 2, GROUPS + 1):
                body(g, g, None)


        @block.sync
        def _(sp):
            def at(i, r, shift):
                batch = (r + shift) // GPB
                return (batch if i is None else i + (batch - 1)), (r + shift) % GPB

            def step(g, r, i):
                if r < GROUPS:
                    sp.wait_ge(s_ready, count(g, 0, S_TILES, LEAD))
                    if r + 1 < GROUPS:
                        stacks.load_pass1(sp, (r + 1) % 2, *at(i, r, 1))
                    stacks.load_pass2(sp, r % 2, *at(i, r, 0))
                    sp.wait_ge(m_copied, count(g, 0, 1, 0))
                    stacks.load_max(sp, r % 2, max_rows)

            steps(sp, step)
            sp.wait_ge(stacks.pass1_in, GROUPS * stacks.ADDS_1)
            sp.wait_ge(stacks.pass2_in, GROUPS * stacks.ADDS_2)
            raw.load(sp, io)

        @block.gpsimd
        def _(pool):
            def step(g, r, i):
                if r < GROUPS:
                    v = c.v[:, bass.ds(g, 1), :, :][:, 0].rearrange("p t (h d) -> p t h d", h=GH)
                    pool.wait_ge(s_ready, count(g, 0, S_TILES, LEAD + 2))
                    nc.gpsimd.tensor_copy(v_nat[r % 2][:, :, :, 0:DB], v).then_inc(v_ready, 1)

            for u in range(2):
                nc.gpsimd.memset(v_nat[u][:, :, :, DB:], 0.0).then_inc(zeroed, 1)
            pool.wait_ge(zeroed, 2)
            for u in range(2):
                last = nc.gpsimd.memset(v_nat[u][:, :, :, DB:DB + 1], 1.0)
            last.then_inc(zeroed, 1)
            steps(pool, step)
            x = c.x[:, PAD:PAD + TILES, :]
            nc.gpsimd.tensor_tensor(x, x, c.b_o[:].unsqueeze(1).broadcast_to([P, TILES, D]), ALU.add).then_inc(biased, 1)

        @block.scalar
        def _(act):
            def place(x):
                return p_s[PLACE[x] % 2]

            def copy_o(g, shift, half):
                act.wait_ge(pv_done, count(g, shift, QUADS, (half + 1) * TPB - 1))
                nc.scalar.activation(o_t[:, half * HALF:(half + 1) * HALF], p_o[:], ACT.Copy).then_inc(o_copied, 1)

            def step(g, r, i):
                for q in range(QUADS):
                    for h in range(GH):
                        if h == 2 and q == M_AT and r < GROUPS:
                            act.wait_ge(qm_ready, count(g, 0, 1, 0))
                            nc.scalar.activation(max_rows[:], place(("m", r, 0))[0:GH * 2 * TPB, 0:P], ACT.Copy).then_inc(m_copied, 1)
                        if r > 0:
                            e = 4 * q + h
                            act.wait_ge(st_ready, count(g, -1, 4 * QUADS, e))
                            nc.scalar.activation(prob[(q % 2) * GH + h][:], scores_ring(r)[e % len(scores_ring(r))], ACT.Exp,
                                                 scale=SCALE).then_inc(exp_done, 1)
                        if r > 1 and q == 0 and h == 1:
                            copy_o(g, -2, 1)
                        if r > 0 and q == TPB and h == 1:
                            copy_o(g, -1, 0)
                if r == GROUPS:
                    copy_o(g, -1, 1)

            nc.scalar.activation(prob[0][:, 0:GH], c.ident[:, 0:GH], ACT.Exp)
            steps(act, step)

        @block.vector
        def _(dve):
            def tile_max(group, shift, r, n):
                dve.wait_ge(s_ready, count(group, shift, S_TILES, n))
                nc.vector.reduce_max(row_max[(r + shift) % 2][:, n // GH, n % GH:n % GH + 1],
                                     p_s[PLACE[("s", r + shift, n)] % 2][:], AX_X).then_inc(max_done, 1)

            def normalize(g, r):
                src = p_s[PLACE[("o", r, 0)] % 2][:].rearrange("p (t h s) -> p t h s", t=TPB, h=GH)
                dve.wait_ge(ot_ready, count(g, 0, 1, 0))
                nc.vector.reciprocal(o_den[:], src[:, :, :, DB]).then_inc(den_done, 1)
                dve.wait_ge(den_done, count(g, 0, 1, 0))
                nc.vector.tensor_tensor(c.v[:, bass.ds(g, 1), :, :][:, 0].rearrange("p t (h d) -> p t h d", h=GH),
                                        src[:, :, :, 0:DB], o_den[:].unsqueeze(3).broadcast_to([P, TPB, GH, DB]),
                                        ALU.mult).then_inc(o_done, 1)

            def step(g, r, i):
                u = r % 2
                for q in range(QUADS):
                    for n in (2 * q, 2 * q + 1):
                        if n + LEAD < S_TILES:
                            if r < GROUPS:
                                tile_max(g, 0, r, n + LEAD)
                        elif r + 1 < GROUPS:
                            tile_max(g, 1, r, n + LEAD - S_TILES)
                        if n + LEAD == S_TILES - 1 and r < GROUPS:
                            dve.wait_ge(max_done, count(g, 0, S_TILES, S_TILES - 1))
                            row_max_h = row_max[u][:].rearrange("p t h -> p h t")
                            nc.vector.tensor_scalar(neg_max[:, 0, :, 0, :].bitcast(F32R), row_max_h, -1.0, None,
                                                    ALU.mult).then_inc(neg_hi, 1)
                            dve.wait_ge(neg_hi, count(g, 0, 1, 0))
                            nc.vector.scalar_tensor_tensor(
                                out=neg_max[:, 0, :, 1, :].bitcast(F32R), in0=row_max_h, scalar=-1.0,
                                in1=neg_max[:, 0, :, 0, :], op0=ALU.mult, op1=ALU.subtract).then_inc(m_ready, 1)
                    if q == O_AT and r > 1:
                        normalize(g - 2, r - 2)

            nc.vector.memset(neg_max[:], 0.0).then_inc(neg_zeroed, 1)
            dve.wait_ge(neg_zeroed, 1)
            for n in range(LEAD):
                tile_max(0, 0, 0, n)
            steps(dve, step)
            normalize(GROUPS - 1, GROUPS - 1)

        @block.tensor
        def _(pe):
            def place(group, shift, x):
                n = PLACE[x]
                before = [m for m in range(n % 2, n, 2) if ALL[m] is not None]
                if before:
                    kind, at, k = ALL[before[-1]]
                    freed, per, late = FREED[kind]
                    pe.wait_ge(freed, count(group, at - (x[1] - shift) + late, per, k))
                return p_s[n % 2]

            def transposes(dst, src, ready):
                for t in range(TPB):
                    last = nc.tensor.transpose(dst[:, t * P:(t + 1) * P], src(t), c.ident[:])
                last.then_inc(ready, 1)

            def scores(g, r, shift, n, half):
                u, t, h = (r + shift) % 2, n // GH, n % GH
                x = ("s", r + shift, n)
                if n == 0 and half == 0:
                    pe.wait_ge(stacks.pass1_in, count(g, shift, stacks.ADDS_1, stacks.ADDS_1 - 1))
                dst = place(g, shift, x) if half == 0 else p_s[PLACE[x] % 2]
                rows = slice(P // 2 * (h // 2), P // 2 * (h // 2 + 1))
                ins = nc.tensor.matmul(dst[:, half * HALF:(half + 1) * HALF], q_pad[u][rows, h % 2, t * P:(t + 1) * P],
                                       k_t[u][rows, half * HALF:(half + 1) * HALF], start=True, stop=True)
                if half == 1:
                    ins.then_inc(s_ready, 1)

            def scores_t(g, r, q, h):
                u, e, blk, half = (r - 1) % 2, 4 * q + h, q % TPB, q // TPB
                if e == 0:
                    pe.wait_ge(stacks.pass2_in, count(g, -1, stacks.ADDS_2, stacks.ADDS_2 - 1))
                    pe.wait_ge(stacks.max_in, count(g, -1, stacks.ADDS_MAX, stacks.ADDS_MAX - 1))
                ring = scores_ring(r)
                if e >= len(ring):
                    pe.wait_ge(exp_done, count(g, -1, 4 * QUADS, e - len(ring)))
                elif e < NE and r > 1:
                    pe.wait_ge(exp_done, count(g, -2, 4 * QUADS, user_before(r, e)))
                nc.tensor.matmul(ring[e % len(ring)], k_pad[u][:, h, blk * P:(blk + 1) * P],
                                 qm_t[u][:, half * HALF:(half + 1) * HALF], start=True, stop=True).then_inc(st_ready, 1)

            def output(g, r, shift, q):
                u, blk = (r + shift) % 2, q % TPB
                if q == 0:
                    pe.wait_ge(v_ready, count(g, shift, 1, 0))
                    if r + shift > 0:
                        pe.wait_ge(o_copied, count(g, shift - 1, 2, 1))
                if q == TPB:
                    pe.wait_ge(o_copied, count(g, shift, 2, 0))
                pe.wait_ge(exp_done, count(g, shift, 4 * QUADS, 4 * q + 3))
                for h in range(GH):
                    last = nc.tensor.matmul(p_o[32 * h:32 * (h + 1), :], v_nat[u][:, blk, h, :], prob[(q % 2) * GH + h][:],
                                            start=blk == 0, stop=blk == TPB - 1)
                last.then_inc(pv_done, 1)

            def step(g, r, i):
                for q in range(QUADS):
                    for kind, n, half in TURNS if r < GROUPS else LAST_TURNS:
                        if kind == "scores_t" and r > 0:
                            scores_t(g, r, q, n)
                        if kind == "scores":
                            tile = 2 * q + n + LEAD
                            if tile < S_TILES:
                                if r < GROUPS:
                                    scores(g, r, 0, tile, half)
                            elif r + 1 < GROUPS:
                                scores(g, r, 1, tile - S_TILES, half)
                        if kind == "output" and q == 0 and r > 1:
                            output(g, r, -2, QUADS - 1)
                        if kind == "output" and q > 0 and r > 0:
                            output(g, r, -1, q - 1)
                        if kind == "output" and q == M_AT and r < GROUPS:
                            pe.wait_ge(m_ready, count(g, 0, 1, 0))
                            nc.tensor.transpose(place(g, 0, ("m", r, 0))[:, 0:P],
                                                neg_max[:].rearrange("p z h a t -> p (z h a t)"), c.ident[:]).then_inc(qm_ready, 1)
                    if q == O_AT and r > 1:
                        pe.wait_ge(o_copied, count(g, -2, 2, 1))
                        transposes(place(g, -2, ("o", r - 2, 0)), lambda t: o_t[:, t * P:(t + 1) * P], ot_ready)
                if r == GROUPS:
                    output(g, r, -1, QUADS - 1)

            for n in range(LEAD):
                scores(0, 0, 0, n, 0)
                scores(0, 0, 0, n, 1)
            steps(pe, step)
            pe.wait_ge(o_copied, 2 * GROUPS)
            transposes(place(GROUPS - 1, 0, ("o", GROUPS - 1, 0)), lambda t: o_t[:, t * P:(t + 1) * P], ot_ready)


def project_out(nc, c, tag, weights):
    OWN, SHARED = 3, 6
    with ExitStack() as ctx:
        def sb(name, shape, dt=F32):
            return ctx.enter_context(nc.sbuf_tensor(f"{tag}_{name}", shape, dt))

        def psum(name, shape):
            return ctx.enter_context(nc.psum_tensor(f"{tag}_{name}", shape, F32))

        def sem(name):
            return c.sem(f"{tag}_{name}")

        o = [sb(f"o{u}", [P, TPB, D]) for u in range(2)]
        o_t = [sb(f"o_t{u}", [P, N]) for u in range(2)]
        stats = sb("stats", [P, TPB, 6])
        moments = sb("moments", [P, TPB, 2])
        p_t = [psum(f"p_t{u}", [P, N]) for u in range(2)]
        p_y = [psum(f"p_y{u}", [P, TPB, D]) for u in range(2)]
        gathered = sem("gathered")
        t_ready = sem("t_ready")
        t_copied = sem("t_copied")
        y_ready = sem("y_ready")
        x_added = sem("x_added")
        counted = sem("counted")
        moved = sem("moved")
        block = ctx.enter_context(nc.Block())

        @block.gpsimd
        def _(pool):
            weights.split(pool, slice(0, OWN))
            weights.split_lo(pool, nc.gpsimd, slice(OWN, OWN + SHARED), 0, weights.lo_done)

        @block.scalar
        def _(act):
            with act.Fori(0, B // 2) as i:
                for u in range(2):
                    b = i * 2 + u
                    nc.scalar.activation(o[u][:].rearrange("p t (g d) -> p g t d", g=GPB),
                                         c.v[:, bass.ds(b * GPB, GPB), :, :], ACT.Copy).then_inc(gathered, 1)
                for u in range(2):
                    act.wait_ge(t_ready, i * 2 + (u + 1))
                    nc.scalar.activation(o_t[u][:], p_t[u][:], ACT.Copy).then_inc(t_copied, 1)
            weights.split_hi(act, slice(OWN, None))

        @block.vector
        def _(dve):
            with dve.Fori(0, B // 2) as i:
                for u in range(2):
                    b = i * 2 + u
                    dve.wait_ge(y_ready, b + 1)
                    nc.vector.tensor_tensor(residual_tiles(c.x, b * TPB, TPB), residual_tiles(c.x, b * TPB, TPB),
                                            p_y[u][:], ALU.add).then_inc(x_added, 1)
                    nc.vector.drain()
                    for t in range(TPB):
                        nc.vector.bn_stats(stats[:, t, :], residual_tiles(c.x, b * TPB + t, 1)[:, 0, :]).then_inc(counted, 1)
                    nc.vector.drain()
                    for t in range(TPB):
                        nc.vector.bn_aggr(moments[:, t, :], stats[:, t, :]).then_inc(counted, 1)
                    nc.vector.drain()
                    nc.vector.tensor_copy(c.mv[:, bass.ds(b * TPB + PAD, TPB), :], moments[:]).then_inc(moved, 1)
                    dve.wait_ge(moved, b + 1)
            weights.split_lo(dve, nc.vector, slice(OWN + SHARED, None), SHARED, weights.dve_lo_done)

        @block.tensor
        def _(pe):
            with pe.Fori(0, B // 2) as i:
                for u in range(2):
                    pe.wait_ge(gathered, i * 2 + (u + 1))
                    for t in range(TPB):
                        last = nc.tensor.transpose(p_t[u][:, t * P:(t + 1) * P], o[u][:, t, :], c.ident[:])
                    last.then_inc(t_ready, 1)
                for u in range(2):
                    pe.wait_ge(t_copied, i * 2 + (u + 1))
                    for t in range(TPB):
                        last = nc.tensor.matmul(p_y[u][:, t, :], o_t[u][:, t * P:(t + 1) * P], c.w_o[:], start=True, stop=True)
                    last.then_inc(y_ready, 1)
                for u in range(2):
                    pe.wait_ge(x_added, i * 2 + (u + 1))


def program(nc, io, out):
    with ExitStack() as ctx:
        c = Chip(nc, ctx)
        c.x = c.sb("x", [P, PAD + TILES + TAIL, D])
        c.mv = c.sb("mean_var", [P, PAD + TILES + TAIL, 2])
        c.rstd = c.sb("rstd", [P, PAD + TILES + TAIL])
        c.ident = c.sb("ident", [P, P])
        c.iota = c.sb("iota", [P, E])
        c.w_qkv = c.sb("w_qkv", [P, 3 * D])
        c.b_qk = c.sb("b_qk", [P, 2])
        c.b_v = c.sb("b_v", [P, D])
        c.w_o = c.sb("w_o", [P, D])
        c.b_o = c.sb("b_o", [P, D])

        with ExitStack() as first:
            weights = ExpertWeights(nc, c, first, "w1")
            attention_a(nc, c, io, weights)
            feed_forward(nc, c, weights, "f1")
        c.v = c.sb("v", [P, GROUPS, TPB, GC])
        with ExitStack() as middle:
            stacks = Stacks(nc, c, ctx, middle)
            raw = RawWeights(nc, c, None, "w2", stacks.room())
            project_qkv(nc, c, stacks, "q")
            softmax_attention(nc, c, io, stacks, raw, "s")
        weights = ExpertWeights(nc, c, ctx, "w2")
        weights.take(raw)
        project_out(nc, c, "o", weights)
        feed_forward(nc, c, weights, "f2", out)


def layouts(a):
    import numpy as np

    g = {k: np.asarray(v) for k, v in a.items()}
    w_qkv, b_qkv = g["L0_attn_a_w_qkv"], g["L0_attn_a_b_qkv"]
    wo_a = g["L0_attn_a_w_o"].T.reshape(NA, D // NA, D).transpose(1, 0, 2).reshape(D, D)
    w_ffn = np.zeros((P, KPC, 3, P), np.float32)
    spread = np.tile(np.repeat(np.eye(E, dtype=np.float32), P, axis=1), (2, 1))
    for k, parts in enumerate(BLOCKS):
        for row, e, first, count in parts:
            rows, units = slice(row, row + count), slice(first, first + count)
            w_ffn[:, k, 0, rows] = g["L0_ffn_W1"][e, units].T
            w_ffn[:, k, 1, rows] = g["L0_ffn_W2"][e, units].T
            w_ffn[rows, k, 2, :] = g["L0_ffn_W3"][e][:, units].T
    io = {
        "x": g["L0_attn_a_x"],
        "wkv_a": w_qkv[D:].T, "wq_a": w_qkv[:D], "wo_a": wo_a,
        "bkv_a": np.broadcast_to(b_qkv[D:], (P, 2 * D)), "bq_a": np.broadcast_to(b_qkv[:D, None], (D, P)),
        "bo_a": np.broadcast_to(g["L0_attn_a_b_o"], (P, D)),
        "head_mask": (np.arange(P)[:, None] % NA == np.arange(P)[None, :] % NA).astype(np.float32),
        "ident": np.eye(P, dtype=np.float32),
        "w_b": np.concatenate([g[f"L0_attn_b_W{n}"] for n in "qkv"], 1),
        "bqk_b": np.stack([g["L0_attn_b_bq"], g["L0_attn_b_bk"]], 1),
        "bv_b": np.broadcast_to(g["L0_attn_b_bv"], (P, D)),
        "wo_b": g["L0_attn_b_Wo"], "bo_b": np.broadcast_to(g["L0_attn_b_bo"], (P, D)),
        "wg": g["L0_ffn_Wg"].T,
        "w_ffn": w_ffn, "spread": spread,
        "iota": np.broadcast_to(np.arange(E, dtype=np.float32), (P, E)),
    }
    return {k: np.ascontiguousarray(v) for k, v in io.items()}


def kernel(**inputs):
    import concourse.bacc as bacc
    from concourse.bass_utils import run_bass_kernel_spmd

    arrays = layouts(inputs)
    nc = bacc.Bacc("TRN2", target_bir_lowering=False, num_devices=1)
    io = {k: nc.dram_tensor(f"in_{k}", v.shape, F32, kind="ExternalInput").ap() for k, v in arrays.items()}
    out = nc.dram_tensor("out", (B, N, D), F32, kind="ExternalOutput").ap()
    program(nc, io, out)
    r = run_bass_kernel_spmd(nc, [{f"in_{k}": v for k, v in arrays.items()}], core_ids=[0])
    return r.results[0]["out"]
```
